# Optimizing a Trainium2 kernel written in Bass

```python
import numpy as np
import jax
import jax.numpy as jnp

def _softmax(x, axis=-1):
    return jax.nn.softmax(x, axis=axis)

def _gelu(x):
    return jax.nn.gelu(x, approximate=True)

def _silu(x):
    return jax.nn.silu(x)

def _sigmoid(x):
    return jax.nn.sigmoid(x)

def _layernorm(x, axis=-1, eps=1e-05):
    m = jnp.mean(x, axis=axis, keepdims=True)
    v = jnp.var(x, axis=axis, keepdims=True)
    return (x - m) / jnp.sqrt(v + eps)

def _scatter_add(tgt, idx, src, axis=0):
    return tgt.at[idx].add(src)

def _segment_sum(src, seg, n):
    return jax.ops.segment_sum(src, seg, n)
kernel_name = 'mk_macaron_d1_jaxref_r8_966d9e'

def setup_inputs(seed: int=0):
    np.random.seed(seed)
    _w = jnp.asarray

    def _L0_attn_setup():
        import jax, jax.numpy as jnp
        import numpy as np
        CHUNK = 32
        H = 4

        def silu(x):
            return x * jax.nn.sigmoid(x)

        def l2norm(x):
            return x * jax.lax.rsqrt(jnp.sum(x * x, -1, keepdims=True) + 1e-06)

        def dwconv_causal(x_cl, w):
            k = w.shape[1]
            xp = jnp.pad(x_cl, ((0, 0), (0, 0), (k - 1, 0)))
            return jax.lax.conv_general_dilated(xp, w[:, None, :], (1,), 'VALID', dimension_numbers=('NCH', 'OIH', 'NCH'), feature_group_count=x_cl.shape[1])

        def short_conv_silu(x_bld, w):
            y = dwconv_causal(jnp.swapaxes(x_bld, 1, 2), w)
            return silu(jnp.swapaxes(y, 1, 2))

        def delta_rule_chunkwise(q, k, v, beta, chunk=CHUNK):
            b, h, L, dk = q.shape
            dv = v.shape[-1]
            pad = -L % chunk
            if pad:
                q, k, v = (jnp.pad(t, ((0, 0), (0, 0), (0, pad), (0, 0))) for t in (q, k, v))
                beta = jnp.pad(beta, ((0, 0), (0, 0), (0, pad)))
            n = (L + pad) // chunk
            q = l2norm(q)
            k = l2norm(k)
            v = v * beta[..., None]
            kb = k * beta[..., None]
            ch = lambda x: x.reshape(b, h, n, chunk, x.shape[-1])
            qc, kc, vc, kbc = map(ch, (q, k, v, kb))
            idx = jnp.arange(chunk)
            strict_lower = (idx[:, None] > idx[None, :]).astype(q.dtype)
            incl_lower = (idx[:, None] >= idx[None, :]).astype(q.dtype)
            attn = -jnp.einsum('bhncd,bhned->bhnce', kbc, kc) * strict_lower
            for i in range(1, chunk):
                upd = jnp.einsum('...j,...ji->...i', attn[..., i, :], attn[..., :, :i])
                attn = attn.at[..., i, :i].add(upd)
            attn = attn + jnp.eye(chunk, dtype=q.dtype)
            u = attn @ vc
            w = attn @ kbc
            xs = tuple((jnp.moveaxis(t, 2, 0) for t in (qc, kc, u, w)))
            S0 = jnp.zeros((b, h, dk, dv), q.dtype)

            def step(S, x):
                qi, ki, ui, wi = x
                a_loc = jnp.einsum('bhcd,bhed->bhce', qi, ki) * incl_lower
                ui = ui - wi @ S
                oi = qi @ S + a_loc @ ui
                S = S + jnp.einsum('bhcd,bhcv->bhdv', ki, ui)
                return (S, oi)
            S, o = jax.lax.scan(step, S0, xs)
            o = jnp.moveaxis(o, 0, 2).reshape(b, h, n * chunk, dv)[:, :, :L]
            return (o, S)

        def multiscale_conv(v, ms_w3, ms_w15, ms_w31, kernel_mix_w, channel_mixer_w):
            b, l, h, d = v.shape
            x = jnp.swapaxes(v.reshape(b, l, h * d), 1, 2)
            outs = [dwconv_causal(x, w) for w in (ms_w3, ms_w15, ms_w31)]
            y = jnp.concatenate(outs, axis=1)
            y = y.reshape(b, h, 3 * d, l).transpose(0, 3, 1, 2)
            y = y @ kernel_mix_w
            y = (y.reshape(b, l, h * d) @ channel_mixer_w).reshape(b, l, h, d)
            return y

        def _forward(hidden_states, Wq, Wk, Wv, Wb, conv_q_w, conv_k_w, conv_v_w, ms_w3, ms_w15, ms_w31, kernel_mix_w, channel_mixer_w, fusion_w1, fusion_b1, fusion_w2, fusion_b2, o_norm_w, Wo):
            b, L, D = hidden_states.shape
            h = H
            dk = Wq.shape[1] // h
            dv = Wv.shape[1] // h
            q = short_conv_silu(hidden_states @ Wq, conv_q_w).reshape(b, L, h, dk)
            k = short_conv_silu(hidden_states @ Wk, conv_k_w).reshape(b, L, h, dk)
            v = short_conv_silu(hidden_states @ Wv, conv_v_w).reshape(b, L, h, dv)
            v_direct = v
            beta = jax.nn.sigmoid(hidden_states @ Wb)
            tr = lambda x: jnp.swapaxes(x, 1, 2)
            delta_out, _S = delta_rule_chunkwise(tr(q), tr(k), tr(v), tr(beta))
            delta_out = jnp.swapaxes(delta_out, 1, 2)
            ms_out = multiscale_conv(v_direct, ms_w3, ms_w15, ms_w31, kernel_mix_w, channel_mixer_w)
            bn = lambda x: jnp.mean(jnp.abs(x), -1)
            gate_features = jnp.concatenate([hidden_states, bn(ms_out), bn(delta_out), bn(v_direct)], -1)
            hdn = jax.nn.gelu(gate_features @ fusion_w1 + fusion_b1, approximate=False)
            logits = (hdn @ fusion_w2 + fusion_b2).reshape(b, L, h, 3)
            wts = jax.nn.softmax(logits, -1)
            o = wts[..., 0:1] * ms_out + wts[..., 1:2] * delta_out + wts[..., 2:3] * v_direct
            o = o * jax.lax.rsqrt(jnp.mean(o * o, -1, keepdims=True) + 1e-05) * o_norm_w
            return o.reshape(b, L, h * dv) @ Wo
        B, L, D = (4, 256, 128)
        h, d = (H, D // H)
        key = jax.random.key(seed)
        ks = jax.random.split(key, 20)
        nrm = lambda k, shp, s: jax.random.normal(k, shp, dtype=jnp.float32) * s
        inp = {'hidden_states': nrm(ks[0], (B, L, D), 1.0), 'Wq': nrm(ks[1], (D, D), D ** (-0.5)), 'Wk': nrm(ks[2], (D, D), D ** (-0.5)), 'Wv': nrm(ks[3], (D, D), D ** (-0.5)), 'Wb': nrm(ks[4], (D, h), D ** (-0.5)), 'conv_q_w': nrm(ks[5], (D, 4), 0.3), 'conv_k_w': nrm(ks[6], (D, 4), 0.3), 'conv_v_w': nrm(ks[7], (D, 4), 0.3), 'ms_w3': nrm(ks[8], (D, 3), 0.02), 'ms_w15': nrm(ks[9], (D, 15), 0.02), 'ms_w31': nrm(ks[10], (D, 31), 0.02), 'kernel_mix_w': nrm(ks[11], (3 * d, d), (3 * d) ** (-0.5)), 'channel_mixer_w': nrm(ks[12], (D, D), D ** (-0.5)), 'fusion_w1': nrm(ks[13], (D + 3 * h, 2 * D), (D + 3 * h) ** (-0.5)), 'fusion_b1': jnp.zeros((2 * D,), jnp.float32), 'fusion_w2': nrm(ks[14], (2 * D, 3 * h), (2 * D) ** (-0.5)), 'fusion_b2': jnp.concatenate([jnp.zeros((2 * h,), jnp.float32), jnp.ones((h,), jnp.float32)]), 'o_norm_w': jnp.ones((d,), jnp.float32), 'Wo': nrm(ks[15], (D, D), D ** (-0.5))}
        return inp
    _L0_attn_in = _L0_attn_setup()

    def _L0_ffn_setup():
        import jax, jax.numpy as jnp
        import numpy as np
        TOP_K = 2
        CAPACITY_FACTOR = 1.25

        def _moe_forward(x, gate_w, wi_gate, wi_up, wo):
            B, S, D = x.shape
            E = wi_gate.shape[0]
            N = B * S
            capacity = max(int(N / E * CAPACITY_FACTOR), 1)
            x_flat = x.reshape(N, D)
            router_logits = x_flat @ gate_w.T
            router_probs = jax.nn.softmax(router_logits, axis=-1)
            top_k_probs, top_k_idx = jax.lax.top_k(router_probs, TOP_K)
            top_k_probs = top_k_probs / jnp.sum(top_k_probs, axis=-1, keepdims=True)
            out = jnp.zeros_like(x_flat)
            experts = jnp.arange(E, dtype=jnp.int32)
            for k in range(TOP_K):
                eid = top_k_idx[:, k]
                ew = top_k_probs[:, k]
                onehot = (eid[:, None] == experts[None, :]).astype(jnp.int32)
                pos_all = jnp.cumsum(onehot, axis=0) - 1
                pos = jnp.take_along_axis(pos_all, eid[:, None].astype(jnp.int32), axis=1)[:, 0]
                valid = pos < capacity
                pos_c = jnp.where(valid, pos, 0)
                disp = jnp.zeros((E, capacity, D), x_flat.dtype).at[eid, pos_c].add(jnp.where(valid[:, None], x_flat, 0.0))
                gate = jax.nn.silu(jnp.einsum('ecd,efd->ecf', disp, wi_gate))
                up = jnp.einsum('ecd,efd->ecf', disp, wi_up)
                expert_out = jnp.einsum('ecf,edf->ecd', gate * up, wo)
                tok_out = expert_out[eid, pos_c]
                out = out + jnp.where(valid[:, None], ew[:, None] * tok_out, 0.0)
            return out.reshape(B, S, D)
        key = jax.random.key(seed)
        k1, k2, k3, k4, k5 = jax.random.split(key, 5)
        B, S, D, F, E = (4, 256, 128, 512, 8)
        return {'x': jax.random.normal(k1, (B, S, D), dtype=jnp.float32), 'gate_w': jax.random.normal(k2, (E, D), dtype=jnp.float32) * 0.02, 'wi_gate': jax.random.normal(k3, (E, F, D), dtype=jnp.float32) * 0.02, 'wi_up': jax.random.normal(k4, (E, F, D), dtype=jnp.float32) * 0.02, 'wo': jax.random.normal(k5, (E, D, F), dtype=jnp.float32) * 0.02}
    _L0_ffn_in = _L0_ffn_setup()
    _d = {'L0_attn_hidden_states': _L0_attn_in['hidden_states'], 'L0_attn_Wq': _L0_attn_in['Wq'], 'L0_attn_Wk': _L0_attn_in['Wk'], 'L0_attn_Wv': _L0_attn_in['Wv'], 'L0_attn_Wb': _L0_attn_in['Wb'], 'L0_attn_conv_q_w': _L0_attn_in['conv_q_w'], 'L0_attn_conv_k_w': _L0_attn_in['conv_k_w'], 'L0_attn_conv_v_w': _L0_attn_in['conv_v_w'], 'L0_attn_ms_w3': _L0_attn_in['ms_w3'], 'L0_attn_ms_w15': _L0_attn_in['ms_w15'], 'L0_attn_ms_w31': _L0_attn_in['ms_w31'], 'L0_attn_kernel_mix_w': _L0_attn_in['kernel_mix_w'], 'L0_attn_channel_mixer_w': _L0_attn_in['channel_mixer_w'], 'L0_attn_fusion_w1': _L0_attn_in['fusion_w1'], 'L0_attn_fusion_b1': _L0_attn_in['fusion_b1'], 'L0_attn_fusion_w2': _L0_attn_in['fusion_w2'], 'L0_attn_fusion_b2': _L0_attn_in['fusion_b2'], 'L0_attn_o_norm_w': _L0_attn_in['o_norm_w'], 'L0_attn_Wo': _L0_attn_in['Wo'], 'L0_ffn_gate_w': _L0_ffn_in['gate_w'], 'L0_ffn_wi_gate': _L0_ffn_in['wi_gate'], 'L0_ffn_wi_up': _L0_ffn_in['wi_up'], 'L0_ffn_wo': _L0_ffn_in['wo']}
    _x0 = _d['L0_attn_hidden_states']
    _d['L0_attn_hidden_states'] = jax.random.normal(jax.random.fold_in(jax.random.key(seed), 1), (16, 256, 128), dtype=_x0.dtype)
    del _x0
    return _d

def reference(L0_attn_hidden_states, L0_attn_Wq, L0_attn_Wk, L0_attn_Wv, L0_attn_Wb, L0_attn_conv_q_w, L0_attn_conv_k_w, L0_attn_conv_v_w, L0_attn_ms_w3, L0_attn_ms_w15, L0_attn_ms_w31, L0_attn_kernel_mix_w, L0_attn_channel_mixer_w, L0_attn_fusion_w1, L0_attn_fusion_b1, L0_attn_fusion_w2, L0_attn_fusion_b2, L0_attn_o_norm_w, L0_attn_Wo, L0_ffn_gate_w, L0_ffn_wi_gate, L0_ffn_wi_up, L0_ffn_wo):

    def _L0_attn_ref(hidden_states, Wq, Wk, Wv, Wb, conv_q_w, conv_k_w, conv_v_w, ms_w3, ms_w15, ms_w31, kernel_mix_w, channel_mixer_w, fusion_w1, fusion_b1, fusion_w2, fusion_b2, o_norm_w, Wo):
        import jax, jax.numpy as jnp
        import numpy as np
        CHUNK = 32
        H = 4

        def silu(x):
            return x * jax.nn.sigmoid(x)

        def l2norm(x):
            return x * jax.lax.rsqrt(jnp.sum(x * x, -1, keepdims=True) + 1e-06)

        def dwconv_causal(x_cl, w):
            k = w.shape[1]
            xp = jnp.pad(x_cl, ((0, 0), (0, 0), (k - 1, 0)))
            return jax.lax.conv_general_dilated(xp, w[:, None, :], (1,), 'VALID', dimension_numbers=('NCH', 'OIH', 'NCH'), feature_group_count=x_cl.shape[1])

        def short_conv_silu(x_bld, w):
            y = dwconv_causal(jnp.swapaxes(x_bld, 1, 2), w)
            return silu(jnp.swapaxes(y, 1, 2))

        def delta_rule_chunkwise(q, k, v, beta, chunk=CHUNK):
            b, h, L, dk = q.shape
            dv = v.shape[-1]
            pad = -L % chunk
            if pad:
                q, k, v = (jnp.pad(t, ((0, 0), (0, 0), (0, pad), (0, 0))) for t in (q, k, v))
                beta = jnp.pad(beta, ((0, 0), (0, 0), (0, pad)))
            n = (L + pad) // chunk
            q = l2norm(q)
            k = l2norm(k)
            v = v * beta[..., None]
            kb = k * beta[..., None]
            ch = lambda x: x.reshape(b, h, n, chunk, x.shape[-1])
            qc, kc, vc, kbc = map(ch, (q, k, v, kb))
            idx = jnp.arange(chunk)
            strict_lower = (idx[:, None] > idx[None, :]).astype(q.dtype)
            incl_lower = (idx[:, None] >= idx[None, :]).astype(q.dtype)
            attn = -jnp.einsum('bhncd,bhned->bhnce', kbc, kc) * strict_lower
            for i in range(1, chunk):
                upd = jnp.einsum('...j,...ji->...i', attn[..., i, :], attn[..., :, :i])
                attn = attn.at[..., i, :i].add(upd)
            attn = attn + jnp.eye(chunk, dtype=q.dtype)
            u = attn @ vc
            w = attn @ kbc
            xs = tuple((jnp.moveaxis(t, 2, 0) for t in (qc, kc, u, w)))
            S0 = jnp.zeros((b, h, dk, dv), q.dtype)

            def step(S, x):
                qi, ki, ui, wi = x
                a_loc = jnp.einsum('bhcd,bhed->bhce', qi, ki) * incl_lower
                ui = ui - wi @ S
                oi = qi @ S + a_loc @ ui
                S = S + jnp.einsum('bhcd,bhcv->bhdv', ki, ui)
                return (S, oi)
            S, o = jax.lax.scan(step, S0, xs)
            o = jnp.moveaxis(o, 0, 2).reshape(b, h, n * chunk, dv)[:, :, :L]
            return (o, S)

        def multiscale_conv(v, ms_w3, ms_w15, ms_w31, kernel_mix_w, channel_mixer_w):
            b, l, h, d = v.shape
            x = jnp.swapaxes(v.reshape(b, l, h * d), 1, 2)
            outs = [dwconv_causal(x, w) for w in (ms_w3, ms_w15, ms_w31)]
            y = jnp.concatenate(outs, axis=1)
            y = y.reshape(b, h, 3 * d, l).transpose(0, 3, 1, 2)
            y = y @ kernel_mix_w
            y = (y.reshape(b, l, h * d) @ channel_mixer_w).reshape(b, l, h, d)
            return y

        def _forward(hidden_states, Wq, Wk, Wv, Wb, conv_q_w, conv_k_w, conv_v_w, ms_w3, ms_w15, ms_w31, kernel_mix_w, channel_mixer_w, fusion_w1, fusion_b1, fusion_w2, fusion_b2, o_norm_w, Wo):
            b, L, D = hidden_states.shape
            h = H
            dk = Wq.shape[1] // h
            dv = Wv.shape[1] // h
            q = short_conv_silu(hidden_states @ Wq, conv_q_w).reshape(b, L, h, dk)
            k = short_conv_silu(hidden_states @ Wk, conv_k_w).reshape(b, L, h, dk)
            v = short_conv_silu(hidden_states @ Wv, conv_v_w).reshape(b, L, h, dv)
            v_direct = v
            beta = jax.nn.sigmoid(hidden_states @ Wb)
            tr = lambda x: jnp.swapaxes(x, 1, 2)
            delta_out, _S = delta_rule_chunkwise(tr(q), tr(k), tr(v), tr(beta))
            delta_out = jnp.swapaxes(delta_out, 1, 2)
            ms_out = multiscale_conv(v_direct, ms_w3, ms_w15, ms_w31, kernel_mix_w, channel_mixer_w)
            bn = lambda x: jnp.mean(jnp.abs(x), -1)
            gate_features = jnp.concatenate([hidden_states, bn(ms_out), bn(delta_out), bn(v_direct)], -1)
            hdn = jax.nn.gelu(gate_features @ fusion_w1 + fusion_b1, approximate=False)
            logits = (hdn @ fusion_w2 + fusion_b2).reshape(b, L, h, 3)
            wts = jax.nn.softmax(logits, -1)
            o = wts[..., 0:1] * ms_out + wts[..., 1:2] * delta_out + wts[..., 2:3] * v_direct
            o = o * jax.lax.rsqrt(jnp.mean(o * o, -1, keepdims=True) + 1e-05) * o_norm_w
            return o.reshape(b, L, h * dv) @ Wo
        return _forward(hidden_states, Wq, Wk, Wv, Wb, conv_q_w, conv_k_w, conv_v_w, ms_w3, ms_w15, ms_w31, kernel_mix_w, channel_mixer_w, fusion_w1, fusion_b1, fusion_w2, fusion_b2, o_norm_w, Wo)

    def _L0_ffn_ref(x, gate_w, wi_gate, wi_up, wo):
        import jax, jax.numpy as jnp
        import numpy as np
        TOP_K = 2
        CAPACITY_FACTOR = 1.25

        def _moe_forward(x, gate_w, wi_gate, wi_up, wo):
            B, S, D = x.shape
            E = wi_gate.shape[0]
            N = B * S
            capacity = max(int(N / E * CAPACITY_FACTOR), 1)
            x_flat = x.reshape(N, D)
            router_logits = x_flat @ gate_w.T
            router_probs = jax.nn.softmax(router_logits, axis=-1)
            top_k_probs, top_k_idx = jax.lax.top_k(router_probs, TOP_K)
            top_k_probs = top_k_probs / jnp.sum(top_k_probs, axis=-1, keepdims=True)
            out = jnp.zeros_like(x_flat)
            experts = jnp.arange(E, dtype=jnp.int32)
            for k in range(TOP_K):
                eid = top_k_idx[:, k]
                ew = top_k_probs[:, k]
                onehot = (eid[:, None] == experts[None, :]).astype(jnp.int32)
                pos_all = jnp.cumsum(onehot, axis=0) - 1
                pos = jnp.take_along_axis(pos_all, eid[:, None].astype(jnp.int32), axis=1)[:, 0]
                valid = pos < capacity
                pos_c = jnp.where(valid, pos, 0)
                disp = jnp.zeros((E, capacity, D), x_flat.dtype).at[eid, pos_c].add(jnp.where(valid[:, None], x_flat, 0.0))
                gate = jax.nn.silu(jnp.einsum('ecd,efd->ecf', disp, wi_gate))
                up = jnp.einsum('ecd,efd->ecf', disp, wi_up)
                expert_out = jnp.einsum('ecf,edf->ecd', gate * up, wo)
                tok_out = expert_out[eid, pos_c]
                out = out + jnp.where(valid[:, None], ew[:, None] * tok_out, 0.0)
            return out.reshape(B, S, D)
        return _moe_forward(x, gate_w, wi_gate, wi_up, wo)
    x = L0_attn_hidden_states
    x = x + 0.5 * _L0_ffn_ref(_layernorm(x, axis=-1), L0_ffn_gate_w, L0_ffn_wi_gate, L0_ffn_wi_up, L0_ffn_wo)
    x = x + _L0_attn_ref(_layernorm(x, axis=-1), L0_attn_Wq, L0_attn_Wk, L0_attn_Wv, L0_attn_Wb, L0_attn_conv_q_w, L0_attn_conv_k_w, L0_attn_conv_v_w, L0_attn_ms_w3, L0_attn_ms_w15, L0_attn_ms_w31, L0_attn_kernel_mix_w, L0_attn_channel_mixer_w, L0_attn_fusion_w1, L0_attn_fusion_b1, L0_attn_fusion_w2, L0_attn_fusion_b2, L0_attn_o_norm_w, L0_attn_Wo)
    x = x + 0.5 * _L0_ffn_ref(_layernorm(x, axis=-1), L0_ffn_gate_w, L0_ffn_wi_gate, L0_ffn_wi_up, L0_ffn_wo)
    return x

_drawn_inputs = setup_inputs


def setup_inputs(seed=0):
    import zlib

    import numpy as np

    out = dict(_drawn_inputs(seed))
    spreads = {'L0_attn_fusion_b1': (0.0, 0.356), 'L0_attn_o_norm_w': (1.0, 0.2)}
    factors = {'L0_attn_ms_w3': 3.692,
     'L0_ffn_gate_w': 8.0,
     'L0_ffn_wi_gate': 8.0,
     'L0_ffn_wi_up': 8.0,
     'L0_ffn_wo': 8.0}
    for name, (base, spread) in spreads.items():
        noise = np.random.default_rng([zlib.crc32(name.encode()), seed]).standard_normal(out[name].shape)
        drawn = base * np.exp(spread * noise) if base else spread * noise
        out[name] = jnp.asarray(drawn.astype(out[name].dtype))
    for name, factor in factors.items():
        out[name] = (out[name] * factor).astype(out[name].dtype)
    return out
```

```python
from contextlib import ExitStack

import numpy as np

import concourse.bass as bass
from concourse import mybir

F32 = mybir.dt.float32
BF16 = mybir.dt.bfloat16
U32 = mybir.dt.uint32
ALU = mybir.AluOpType
ACT = mybir.ActivationFunctionType
AX = mybir.AxisListType

P = 128
BATCH, SEQ, D = 16, 256, 128
H, DH = 4, 32
CHUNK = 32
NT = BATCH * SEQ // P
TPP = 4
NPAIR = NT // TPP
PT = TPP * P
NCH = SEQ // CHUNK
QC = P // CHUNK
E, TOPK, F = 8, 2, 512
CAP = int(BATCH * SEQ / E * 1.25)
SLOTS = TOPK * E * CAP
CT = CAP // P
HALF = CAP // 2
FT = F // P
TAPS = 4
PAD = TAPS - 1
LAGS = 31
GRP = 8
YB = NT + 2 * TPP
NGRP = NT // GRP
NOUT = 3 * H
LN_EPS, L2_EPS, RMS_EPS = 1e-5, 1e-6, 1e-5

C_ID, C_HEAD, C_UP, C_ONE = 0, 128, 256, 384
C_NEG, C_INC, C_IOTA, C_BASE, C_EYE = 512, 544, 576, 584, 586
C_END = C_EYE + CHUNK * CHUNK


def shape_constants():
    c = np.zeros((P, C_END), np.float32)
    p = np.arange(P)
    c[:, C_ID:C_ID + P] = np.eye(P)
    c[:, C_HEAD:C_HEAD + P] = p[:, None] // DH == p[None, :] // DH
    c[:, C_UP:C_UP + P] = p[:, None] < p[None, :]
    c[:, C_ONE:C_ONE + P] = 1.0
    e = np.arange(CHUNK)
    c[:, C_NEG:C_NEG + CHUNK] = -1.0 * (e[None, :] < p[:, None] % CHUNK)
    c[:, C_INC:C_INC + CHUNK] = p[:, None] % CHUNK <= e[None, :]
    c[:, C_IOTA:C_IOTA + E] = np.arange(E)
    c[:, C_BASE:C_BASE + TOPK] = np.arange(TOPK) * E * CAP - SLOTS
    c[:, C_EYE:C_END] = np.eye(CHUNK).reshape(1, -1)
    return c


def bc(ap, shape):
    return ap.to_broadcast(list(shape))


class Memory:

    def __init__(self, nc, ctx):
        self.nc, self.ctx = nc, ctx

    def sb(self, name, shape, dt=F32):
        return self.ctx.enter_context(self.nc.sbuf_tensor(name, list(shape), dt))

    def ps(self, name, shape, dt=F32):
        return self.ctx.enter_context(self.nc.psum_tensor(name, list(shape), dt))

    def sem(self, name):
        return self.ctx.enter_context(self.nc.semaphore(name))


def prepare(nc, io, keep):
    with ExitStack() as ctx:
        m = Memory(nc, ctx)
        k = keep
        wqkv = m.sb("wqkv", [P, 3, D])
        taps = m.sb("taps", [P, TAPS, 3 * D])
        ms3, ms15, ms31 = m.sb("ms3", [P, 3]), m.sb("ms15", [P, 15]), m.sb("ms31", [P, 31])
        mixT = m.sb("mixT", [P, 3 * D])
        chan = m.sb("chan", [P, D])
        base = m.sb("base", [P, 3, D])
        wo_raw = m.sb("wo_raw", [P, D])
        onorm = m.sb("onorm", [P, 1])
        zero = m.sb("zero", [P, 20 * D])
        pbase = m.ps("pbase", [P, 512])
        loaded, mixed, cleared, mixzero = m.sem("loaded"), m.sem("mixed"), m.sem("cleared"), m.sem("mixzero")
        based, wiped, folded, lagged = m.sem("based"), m.sem("wiped"), m.sem("folded"), m.sem("lagged")
        block = ctx.enter_context(nc.Block())
        loads = [
            (k.x[:], io.x.rearrange("(n p) d -> p n d", p=P)),
            (k.const[:], io.const), (k.gate[:], io.gate), (wqkv[:], io.wqkv),
            (taps[:].rearrange("p a b -> p (a b)"), io.taps.partition_broadcast(P)),
            (k.wb[:], io.wb), (ms3[:], io.ms3), (ms15[:], io.ms15), (ms31[:], io.ms31),
            (chan[:], io.chan), (k.w1[:], io.w1[0:D, :]), (k.w1s[:], io.w1[D:D + NOUT, :]),
            (k.b1[:], io.b1), (k.w2[:], io.w2.rearrange("(f p) n -> p f n", p=P)),
            (k.b2[:], io.b2.partition_broadcast(P)), (wo_raw[:], io.wo),
        ] + [(onorm[DH * h:DH * h + DH, :], io.onorm.rearrange("(d a) -> d a", a=1)) for h in range(H)]

        @block.sync
        def _(sp):
            for dst, src in loads:
                sp.dma_start(dst, src).then_inc(loaded, 16)
            sp.wait_ge(mixzero, 1)
            for h in range(H):
                sp.dma_start(mixT[DH * h:DH * h + DH, 3 * DH * h:3 * DH * h + 3 * DH], io.mixT).then_inc(mixed, 16)
            sp.wait_ge(wiped, 1)
            queue = io.queue.rearrange("(p r) d -> p (r d)", p=P)
            for n in range(SLOTS // P // 20):
                sp.dma_start(queue[:, n * 20 * D:(n + 1) * 20 * D], zero[:]).then_inc(cleared, 16)
            sp.dma_start(io.rows[SLOTS:SLOTS + 1, :], zero[0:1, 0:D]).then_inc(cleared, 16)
            sp.wait_ge(cleared, 16 * (SLOTS // P // 20 + 1))

        @block.tensor
        def _(pe):
            pe.wait_ge(loaded, 16 * len(loads))
            pe.wait_ge(mixed, 16 * H)
            for s in range(3):
                mm = pe.matmul(pbase[:, s * D:s * D + D], mixT[:, s * D:s * D + D], chan[:], start=True, stop=True)
            mm.then_inc(based, 1)

        @block.vector
        def _(dve):
            dve.memset(mixT[:], 0.0).then_inc(mixzero, 1)
            dve.memset(zero[:], 0.0).then_inc(wiped, 1)
            dve.memset(k.eps[:, 0:1], LN_EPS)
            dve.memset(k.eps[:, 1:2], L2_EPS)
            dve.memset(k.eps[:, 2:3], RMS_EPS)
            dve.memset(k.slot[:], 0)
            dve.wait_ge(loaded, 16 * len(loads))
            dve.tensor_copy(k.upper[:], k.const[:, C_UP:C_UP + P])
            dve.tensor_copy(k.ones[:], k.const[:, C_ONE:C_ONE + P])
            for j in range(TAPS):
                dve.tensor_tensor(k.wtap[:, j, :], taps[:, j, :], wqkv[:].rearrange("p a b -> p (a b)"), ALU.mult)
            dve.tensor_scalar(k.wout[:], wo_raw[:], onorm[:, 0:1], None, ALU.mult)
            dve.wait_ge(based, 1)
            dve.tensor_copy(base[:].rearrange("p a b -> p (a b)"), pbase[:, 0:3 * D]).then_inc(folded, 1)
            dve.wait_ge(folded, 1)
            for lag in range(LAGS):
                dve.tensor_scalar(k.lag[:, lag, :], base[:, 2, :], ms31[:, 30 - lag:31 - lag], None,
                                  ALU.mult).then_inc(lagged, 1)
            dve.wait_ge(lagged, LAGS)
            for lag in range(15):
                dve.scalar_tensor_tensor(k.lag[:, lag, :], base[:, 1, :], ms15[:, 14 - lag:15 - lag],
                                         k.lag[:, lag, :], ALU.mult, ALU.add).then_inc(lagged, 1)
            dve.wait_ge(lagged, LAGS + 15)
            for lag in range(3):
                dve.scalar_tensor_tensor(k.lag[:, lag, :], base[:, 0, :], ms3[:, 2 - lag:3 - lag],
                                         k.lag[:, lag, :], ALU.mult, ALU.add).then_inc(lagged, 1)
            dve.wait_ge(lagged, LAGS + 18)



class Steps:

    def __init__(self, eng, sem, base=0):
        self.eng, self.sem, self.base, self.n = eng, sem, base, 0

    def done(self, ins):
        self.n += 1
        ins.then_inc(self.sem, 1)
        self.eng.wait_ge(self.sem, self.base + self.n)


def wait_apart(eng, sem, value, beat):
    eng.wait_ge(sem, value)
    eng.sem_inc(beat, 1)


def layernorm_stats(dve, link, stat, mv, tiles, varied, beat):
    for j, tile in enumerate(tiles):
        last = dve.bn_stats(stat[:, j, :], tile)
    link(last)
    dve.sem_inc(beat, 1)
    for j in range(len(tiles)):
        last = dve.bn_aggr(mv[:, j, :], stat[:, j, :])
    last.then_inc(varied, 1)


def route(nc, io, keep, name):
    k = keep
    with ExitStack() as ctx:
        m = Memory(nc, ctx)
        sem = lambda s: m.sem(f"{name}_{s}")
        sb = lambda s, shape, dt=F32: m.sb(f"{name}_{s}", shape, dt)
        stat, mv = sb("stat", [P, GRP, 6]), sb("mv", [P, GRP, 2])
        std, rstd = sb("std", [P, GRP]), sb("rstd", [P, GRP])
        xn = sb("xn", [P, NT, D])
        xnT = sb("xnT", [P, GRP * P])
        logit = sb("logit", [P, GRP, E])
        top, index = sb("top", [P, GRP, 8]), sb("index", [P, GRP, 8], U32)
        idx = sb("idx", [P, GRP, TOPK])
        hot = sb("hot", [P, GRP, TOPK, E], BF16)
        before = sb("before", [P, GRP, TOPK * E], BF16)
        prod, pos = sb("prod", [P, GRP * TOPK, E]), sb("pos", [P, GRP, TOPK])
        place, valid = sb("place", [P, GRP, TOPK]), sb("valid", [P, GRP, TOPK])
        gap, ratio, share = sb("gap", [P, GRP]), sb("ratio", [P, GRP]), sb("share", [P, GRP, TOPK])
        ptr = m.ps(f"{name}_ptr", [P, 2, 512])
        plog, ppos = m.ps(f"{name}_plog", [P, 512]), m.ps(f"{name}_ppos", [P, 512])
        chain, beat = sem("chain"), sem("beat")
        varied, rooted, normed, turned = sem("varied"), sem("rooted"), sem("normed"), sem("turned")
        evac, scored, gapped, powered = sem("evac"), sem("scored"), sem("gapped"), sem("powered")
        counted, placed, slotted, sent = sem("counted"), sem("placed"), sem("slotted"), sem("sent")
        block = ctx.enter_context(nc.Block())

        @block.vector
        def _(dve):
            steps = Steps(dve, chain)
            link = steps.done
            link(dve.memset(k.count[:], 0.0))
            for g in range(NGRP):
                layernorm_stats(dve, link, stat, mv, [k.x[:, g * GRP + j, :] for j in range(GRP)], varied, beat)
                dve.wait_ge(rooted, g + 1)
                link(dve.reciprocal(rstd[:], std[:]))
                for j in range(GRP):
                    last = dve.tensor_scalar(xn[:, g * GRP + j, :], k.x[:, g * GRP + j, :],
                                             mv[:, j, 0:1], rstd[:, j:j + 1], ALU.subtract, ALU.mult)
                last.then_inc(normed, 1)
                dve.wait_ge(scored, g + 1)
                link(dve.tensor_copy(logit[:].rearrange("p a b -> p (a b)"), plog[:, 0:GRP * E]))
                for j in range(GRP):
                    last = dve.max(top[:, j, :], logit[:, j, :])
                link(last)
                dve.tensor_tensor(gap[:], top[:, :, 1], top[:, :, 0], ALU.subtract).then_inc(gapped, 1)
                for j in range(GRP):
                    last = dve.max_index(index[:, j, :], top[:, j, :], logit[:, j, :])
                link(last)
                link(dve.tensor_copy(idx[:], index[:, :, 0:TOPK]))
                link(dve.tensor_tensor(
                    hot[:], bc(k.const[:, C_IOTA:C_IOTA + E].unsqueeze(1).unsqueeze(1), [P, GRP, TOPK, E]),
                    bc(idx[:].unsqueeze(3), [P, GRP, TOPK, E]), ALU.is_equal))
                flat = hot[:].rearrange("p a b c -> p a (b c)")
                link(dve.tensor_copy(before[:, 0, :], k.count[:]))
                for j in range(1, GRP):
                    link(dve.tensor_tensor(before[:, j, :], before[:, j - 1, :], flat[:, j - 1, :], ALU.add))
                dve.tensor_tensor(k.count[:], before[:, GRP - 1, :], flat[:, GRP - 1, :],
                                  ALU.add).then_inc(counted, 1)
                dve.wait_ge(placed, g + 1)
                link(dve.tensor_tensor(prod[:], ppos[:, 0:GRP * TOPK * E].rearrange("p (a b) -> p a b", b=E),
                                       hot[:].rearrange("p a b c -> p (a b) c"), ALU.mult))
                link(dve.tensor_reduce(pos[:].rearrange("p a b -> p (a b)"), prod[:], AX.X, ALU.add))
                dve.tensor_scalar(valid[:], pos[:], float(CAP), None, ALU.is_lt)
                link(dve.scalar_tensor_tensor(place[:], idx[:], float(CAP), pos[:], ALU.mult, ALU.add))
                link(dve.tensor_tensor(place[:], place[:],
                                       bc(k.const[:, C_BASE:C_BASE + TOPK].unsqueeze(1), [P, GRP, TOPK]), ALU.add))
                link(dve.tensor_tensor(place[:], place[:], valid[:], ALU.mult))
                dve.tensor_scalar(k.slot[:, g * GRP:(g + 1) * GRP, :], place[:], float(SLOTS), None,
                                  ALU.add).then_inc(slotted, 1)
                dve.wait_ge(powered, g + 1)
                link(dve.tensor_scalar(gap[:], ratio[:], 1.0, None, ALU.add))
                link(dve.reciprocal(share[:, :, 0], gap[:]))
                link(dve.tensor_tensor(share[:, :, 1], share[:, :, 0], ratio[:], ALU.mult))
                link(dve.scalar_tensor_tensor(k.share[:, g * GRP:(g + 1) * GRP, :], share[:], 0.5, valid[:],
                                              ALU.mult, ALU.mult))

        @block.scalar
        def _(act):
            for g in range(NGRP):
                act.wait_ge(varied, g + 1)
                act.activation(std[:], mv[:, :, 1], ACT.Sqrt, bias=k.eps[:, 0:1]).then_inc(rooted, 1)
                for n in range(2):
                    act.wait_ge(turned, g * 2 + n + 1)
                    act.activation(xnT[:, n * 512:n * 512 + 512], ptr[:, n, :], ACT.Copy).then_inc(evac, 1)
                act.wait_ge(gapped, g + 1)
                act.activation(ratio[:], gap[:], ACT.Exp).then_inc(powered, 1)

        @block.tensor
        def _(pe):
            for g in range(NGRP):
                pe.wait_ge(normed, g + 1)
                for n in range(2):
                    for j in range(4):
                        mm = pe.transpose(ptr[:, n, j * P:j * P + P], xn[:, g * GRP + n * 4 + j, :],
                                          k.const[:, C_ID:C_ID + P])
                    mm.then_inc(turned, 1)
                pe.wait_ge(evac, 2 * g + 2)
                for j in range(GRP):
                    mm = pe.matmul(plog[:, j * E:j * E + E], xnT[:, j * P:j * P + P], k.gate[:], start=True, stop=True)
                mm.then_inc(scored, 1)
                pe.wait_ge(counted, g + 1)
                pe.matmul(ppos[:, 0:GRP * TOPK * E], k.upper[:], hot[:].rearrange("p a b c -> p (a b c)"),
                          start=True, stop=False)
                pe.matmul(ppos[:, 0:GRP * TOPK * E], k.ones[:], before[:].rearrange("p a b -> p (a b)"),
                          start=False, stop=True).then_inc(placed, 1)

        @block.gpsimd
        def _(pool):
            for g in range(NGRP):
                pool.wait_ge(slotted, g + 1)
                for j in range(g * GRP, (g + 1) * GRP):
                    for c in range(TOPK):
                        pool.indirect_dma_start(
                            io.queue, bass.IndirectOffsetOnAxis(ap=k.slot[:, j, c:c + 1], axis=0),
                            xn[:, j, :], None, bounds_check=SLOTS - 1, oob_is_err=False).then_inc(sent, 16)
            pool.wait_ge(sent, 16 * NT * TOPK)


def experts(nc, io, keep, name):
    k = keep
    with ExitStack() as ctx:
        m = Memory(nc, ctx)
        sem = lambda s: m.sem(f"{name}_{s}")
        sb = lambda s, shape, dt=F32: m.sb(f"{name}_{s}", shape, dt)
        w = [sb(f"w{i}", [P, 3, F]) for i in range(2)]
        xs = [sb(f"xs{i}", [P, CT, D]) for i in range(2)]
        xT = [sb(f"xT{i}", [P, CAP]) for i in range(2)]
        sg = [sb(f"sg{i}", [P, HALF]) for i in range(2)]
        hid = [sb(f"hid{i}", [P, FT, CAP]) for i in range(2)]
        rows = [sb(f"rows{i}", [P, CT, D]) for i in range(2)]
        pt, po = m.ps(f"{name}_pt", [P, 2, 512]), m.ps(f"{name}_po", [P, 2, 512])
        pg = [m.ps(f"{name}_pg{i}", [P, 512]) for i in range(2)]
        pu = [m.ps(f"{name}_pu{i}", [P, 512]) for i in range(2)]
        wgot = [sem(f"wgot{i}") for i in range(2)]
        xgot = [sem(f"xgot{i}") for i in range(2)]
        beat = sem("beat")
        wfree, xfree, rfree, hfree = sem("wfree"), sem("xfree"), sem("rfree"), sem("hfree")
        turned, evac, gued, silued = sem("turned"), sem("evac"), sem("gued"), sem("silued")
        downed, ofree, rready, stored = sem("downed"), sem("ofree"), sem("rready"), sem("stored")
        block = ctx.enter_context(nc.Block())
        NQ = TOPK * E
        NB = 2 * FT

        @block.sync
        def _(sp):
            with sp.Fori(0, TOPK) as c:
                with sp.Fori(0, E // 2) as ee:
                    for par in range(2):
                        q = c * E + ee * 2 + par
                        wait_apart(sp, xfree, q + 1, beat)
                        sp.dma_start(xs[par][:], io.queue[bass.ds(q * CAP, CAP), :].rearrange(
                            "(s p) d -> p s d", p=P)).then_inc(xgot[par], 16)
                        wait_apart(sp, wfree, q + 1, beat)
                        sp.dma_start(w[par][:].rearrange("p a b -> p (a b)"),
                                     io.wexp[bass.ds((ee * 2 + par) * P, P), :]).then_inc(wgot[par], 16)

        @block.tensor
        def _(pe):
            pe.sem_inc(xfree, 2)
            pe.sem_inc(wfree, 2)

            def turn(q, par, half):
                pe.wait_ge(xgot[par], 16 * half)
                for s in range(CT):
                    mm = pe.transpose(pt[:, s // 4, (s % 4) * P:(s % 4) * P + P], xs[par][:, s, :],
                                      k.const[:, C_ID:C_ID + P])
                mm.then_inc(turned, 1)

            def down(par, s):
                for f in range(FT):
                    mm = pe.matmul(po[:, s // 4, (s % 4) * P:(s % 4) * P + P], hid[par][:, f, s * P:s * P + P],
                                   w[par][:, 2, f * P:f * P + P], start=(f == 0), stop=(f == FT - 1))
                return mm

            def queue(q, par, half, follow):
                pe.wait_ge(evac, q + 1)
                pe.sem_inc(xfree, 1)
                pe.wait_ge(wgot[par], 16 * half)
                for c in range(2):
                    for f in range(FT):
                        n = c * FT + f
                        pe.wait_ge(hfree, q * NB + n + 1)
                        cols = slice(c * HALF, c * HALF + HALF)
                        pe.matmul(pg[n % 2][:, 0:HALF], w[par][:, 0, f * P:f * P + P], xT[par][:, cols],
                                  start=True, stop=True)
                        pe.matmul(pu[n % 2][:, 0:HALF], w[par][:, 1, f * P:f * P + P], xT[par][:, cols],
                                  start=True, stop=True).then_inc(gued, 1)
                if follow is not None:
                    turn(q + 1, 1 - par, follow)
                pe.wait_ge(ofree, q + 1)
                pe.wait_ge(hfree, q * NB + FT + 2)
                for s in range(HALF // P):
                    down(par, s)
                pe.wait_ge(hfree, q * NB + NB + 2)
                for s in range(HALF // P, CT):
                    mm = down(par, s)
                mm.then_inc(downed, 1)

            turn(0, 0, 1)
            with pe.Fori(0, NQ // 2 - 1) as r:
                queue(r * 2, 0, r + 1, r + 1)
                queue(r * 2 + 1, 1, r + 1, r + 2)
            queue(NQ - 2, 0, NQ // 2, NQ // 2)
            queue(NQ - 1, 1, NQ // 2, None)

        @block.scalar
        def _(act):
            def evacuate(q, par):
                act.wait_ge(turned, q + 1)
                act.activation(xT[par][:, 0:512], pt[:, 0, :], ACT.Copy)
                act.activation(xT[par][:, 512:CAP], pt[:, 1, 0:CAP - 512], ACT.Copy).then_inc(evac, 1)

            def queue(q, par, follow):
                for n in range(NB):
                    act.wait_ge(gued, q * NB + n + 1)
                    act.activation(sg[n % 2][:], pg[n % 2][:, 0:HALF], ACT.Silu).then_inc(silued, 1)
                if follow:
                    evacuate(q + 1, 1 - par)

            evacuate(0, 0)
            with act.Fori(0, NQ // 2 - 1) as r:
                queue(r * 2, 0, True)
                queue(r * 2 + 1, 1, True)
            queue(NQ - 2, 0, True)
            queue(NQ - 1, 1, False)

        @block.vector
        def _(dve):
            dve.sem_inc(hfree, 2)
            dve.sem_inc(ofree, 1)
            with dve.Fori(0, NQ // 2) as r:
                for par in range(2):
                    q = r * 2 + par
                    for n in range(NB):
                        c, f = n // FT, n % FT
                        dve.wait_ge(silued, q * NB + n + 1)
                        dve.tensor_tensor(hid[par][:, f, c * HALF:c * HALF + HALF], sg[n % 2][:],
                                          pu[n % 2][:, 0:HALF], ALU.mult).then_inc(hfree, 1)
                    dve.wait_ge(downed, q + 1)
                    dve.sem_inc(wfree, 1)
                    dve.wait_ge(rfree, q + 1)
                    flat = rows[par][:].rearrange("p a b -> p (a b)")
                    dve.tensor_copy(flat[:, 0:512], po[:, 0, :]).then_inc(rready, 1)
                    dve.tensor_copy(flat[:, 512:CAP], po[:, 1, 0:CAP - 512]).then_inc(rready, 1)
                    dve.wait_ge(rready, q * 2 + 2)
                    dve.sem_inc(ofree, 1)

        @block.gpsimd
        def _(pool):
            pool.sem_inc(rfree, 2)
            with pool.Fori(0, NQ // 2) as r:
                for par in range(2):
                    q = r * 2 + par
                    pool.wait_ge(rready, q * 2 + 2)
                    pool.dma_start(io.rows[bass.ds(q * CAP, CAP), :].rearrange("(s p) d -> p s d", p=P),
                                   rows[par][:]).then_inc(stored, 16)
                    pool.wait_ge(stored, 16 * (q + 1))
                    pool.sem_inc(rfree, 1)


def project(nc, io, keep):
    k = keep
    G = TPP * H
    with ExitStack() as ctx:
        m = Memory(nc, ctx)
        sem, sb = m.sem, m.sb
        slots = [sb(f"slots{i}", [P, TPP * TOPK], U32) for i in range(2)]
        got = [sb(f"got{i}", [P, TPP, TOPK, D]) for i in range(2)]
        stat, mv = sb("stat", [P, TPP, 6]), sb("mv", [P, TPP, 2])
        std, rstd = sb("std", [P, TPP]), sb("rstd", [P, TPP])
        xn = sb("xn", [P, PT])
        xnT = sb("xnT", [P, 2, PAD + SEQ])
        qkv = sb("qkv", [P, TPP, 3 * D])
        tanhb, beta = sb("tanhb", [P, G]), sb("beta", [P, G])
        sq, ss = sb("sq", [P, TPP, 2 * D]), sb("ss", [P, 2 * G])
        rn = sb("rn", [P, 2 * G])
        qk = sb("qk", [P, TPP, 2 * D])
        kq = sb("kq", [P, 2, PT])
        vT = sb("vT", [P, PT])
        kb, vb = sb("kb", [P, PT]), sb("vb", [P, PT])
        low, loc = sb("low", [P, G, CHUNK]), sb("loc", [P, G, CHUNK])
        px, pk, pq, pv = (m.ps(f"pp{i}", [P, 512]) for i in range(4))
        pa = m.ps("pa", [P, 4, 512])
        chain, beat = sem("chain"), sem("beat")
        gathered = [sem(f"gathered{i}") for i in range(2)]
        indexed, varied = sem("indexed"), sem("varied")
        rooted, normed, turned, evac = sem("rooted"), sem("normed"), sem("turned"), sem("evac")
        projected, silued, squared, summed = sem("projected"), sem("silued"), sem("squared"), sem("summed")
        lengths, scaled, turned3, moved = sem("lengths"), sem("scaled"), sem("turned3"), sem("moved")
        grammed, masked, weighted, saved = sem("grammed"), sem("masked"), sem("weighted"), sem("saved")
        padded, room, unmasked = sem("padded"), sem("room"), sem("unmasked")
        block = ctx.enter_context(nc.Block())

        NSAVE = 7 + 1 + QC
        LINKS = 7

        @block.gpsimd
        def _(pool):
            def gather(t, par):
                wait_apart(pool, indexed, t + 1, beat)
                for j in range(TPP):
                    for c in range(TOPK):
                        i = j * TOPK + c
                        pool.indirect_dma_start(
                            got[par][:, j, c, :], None, io.rows,
                            bass.IndirectOffsetOnAxis(ap=slots[par][:, i:i + 1], axis=0)).then_inc(gathered[par], 16)

            def weigh(t):
                pool.wait_ge(masked, t + 1)
                pool.tensor_tensor(low[:], low[:], bc(beta[:].unsqueeze(2), [P, G, CHUNK]),
                                   ALU.mult).then_inc(weighted, 1)

            gather(0, 0)
            with pool.Fori(0, NPAIR // 2 - 1) as r:
                for par in range(2):
                    gather(r * 2 + par + 1, 1 - par)
                    weigh(r * 2 + par)
            gather(NPAIR - 1, 1)
            weigh(NPAIR - 2)
            weigh(NPAIR - 1)

        @block.vector
        def _(dve):
            SLOTROW = TPP * TOPK
            table = k.slot[:].rearrange("p a b -> p (a b)")
            for par in range(2):
                dve.tensor_copy(slots[par][:], table[:, par * SLOTROW:(par + 1) * SLOTROW]).then_inc(indexed, 1)
            dve.memset(xnT[:, :, 0:PAD], 0.0).then_inc(padded, 1)
            with dve.Fori(0, NPAIR // 2) as r:
                for par in range(2):
                    t = r * 2 + par
                    steps = Steps(dve, chain, t * LINKS)
                    link = steps.done
                    dve.wait_ge(gathered[par], (r + 1) * 16 * TPP * TOPK)
                    tile = lambda j: k.x[:, bass.ds(t * TPP + j, 1), :].rearrange("p a d -> p (a d)")
                    share = lambda j, c: k.share[:, bass.ds(t * TPP + j, 1), c]
                    dve.tensor_copy(slots[par][:], table[:, bass.ds((t + 2) * SLOTROW, SLOTROW)])
                    for c in range(TOPK):
                        for j in range(TPP):
                            last = dve.scalar_tensor_tensor(tile(j), got[par][:, j, c, :], share(j, c), tile(j),
                                                            ALU.mult, ALU.add)
                        link(last)
                    dve.sem_inc(indexed, 1)
                    layernorm_stats(dve, link, stat, mv, [tile(j) for j in range(TPP)], varied, beat)
                    dve.wait_ge(rooted, t + 1)
                    link(dve.reciprocal(rstd[:], std[:]))
                    for j in range(TPP):
                        last = dve.tensor_scalar(xn[:, j * D:j * D + D], tile(j), mv[:, j, 0:1], rstd[:, j:j + 1],
                                                 ALU.subtract, ALU.mult)
                    last.then_inc(normed, 1)
                    dve.wait_ge(squared, t + 1)
                    dve.tensor_reduce(ss[:], sq[:].rearrange("p a (b c) -> p (a b) c", c=DH), AX.X,
                                      ALU.add).then_inc(summed, 1)
                    dve.wait_ge(room, t + 1)
                    link(dve.tensor_scalar(beta[:], tanhb[:], 0.5, 0.5, ALU.mult, ALU.add))
                    dve.wait_ge(lengths, t + 1)
                    link(dve.reciprocal(rn[:], rn[:]))
                    dve.tensor_tensor(qk[:].rearrange("p a (b c) -> p a b c", c=DH),
                                      qkv[:, :, 0:2 * D].rearrange("p a (b c) -> p a b c", c=DH),
                                      bc(rn[:].rearrange("p (a b) -> p a b", a=TPP).unsqueeze(3), [P, TPP, 2 * H, DH]),
                                      ALU.mult).then_inc(scaled, 1)
                    dve.wait_ge(turned3, 3 * t + 1)
                    dve.tensor_copy(kq[:, 0, :], pk[:]).then_inc(moved, 1)
                    dve.wait_ge(turned3, 3 * t + 3)
                    dve.tensor_copy(vT[:], pv[:]).then_inc(moved, 1)
                    dve.wait_ge(scaled, t + 1)
                    b3 = bc(beta[:].rearrange("p (a b) -> p a b", a=TPP).unsqueeze(3), [P, TPP, H, DH])
                    heads = lambda ap: ap.rearrange("p a (b c) -> p a b c", c=DH)
                    dve.tensor_tensor(kb[:].rearrange("p (a b c) -> p a b c", a=TPP, c=DH),
                                      heads(qk[:, :, D:2 * D]), b3, ALU.mult)
                    dve.tensor_tensor(vb[:].rearrange("p (a b c) -> p a b c", a=TPP, c=DH),
                                      heads(qkv[:, :, 2 * D:3 * D]), b3, ALU.mult)
                    dve.wait_ge(grammed, t + 1)
                    gram = lambda i: pa[:, :, 0:TPP * 2 * CHUNK].rearrange(
                        "p h (a g c) -> p h a g c", a=TPP, g=2)[:, :, :, i, :]
                    mask = lambda c: bc(k.const[:, c:c + CHUNK].unsqueeze(1).unsqueeze(1), [P, H, TPP, CHUNK])
                    to = lambda ap: ap.rearrange("p (a h) c -> p h a c", h=H)
                    dve.tensor_tensor(to(low[:]), gram(0), mask(C_NEG), ALU.mult).then_inc(masked, 1)
                    link(dve.tensor_tensor(to(loc[:]), gram(1), mask(C_INC), ALU.mult))
                    dve.sem_inc(unmasked, 1)
                    assert steps.n == LINKS, steps.n

        @block.scalar
        def _(act):
            act.wait_ge(padded, 1)
            with act.Fori(0, NPAIR) as t:
                act.wait_ge(varied, t + 1)
                act.activation(std[:], mv[:, :, 1], ACT.Sqrt, bias=k.eps[:, 0:1]).then_inc(rooted, 1)
                act.wait_ge(turned, t + 1)
                act.wait_ge(room, t + 1)
                act.activation(xnT[:, :, PAD:], px[:].rearrange("p (b c) -> p b c", b=2), ACT.Copy).then_inc(evac, 1)
                for j in range(TPP):
                    act.wait_ge(projected, t * TPP + j + 1)
                    act.activation(qkv[:, j, :], pa[:, j, 0:3 * D], ACT.Silu)
                    act.activation(tanhb[:, j * H:j * H + H], pa[:, j, 3 * D:3 * D + H], ACT.Tanh,
                                   scale=0.5).then_inc(silued, 1)
                act.wait_ge(silued, (t + 1) * TPP)
                act.activation(sq[:], qkv[:, :, 0:2 * D], ACT.Square).then_inc(squared, 1)
                act.wait_ge(summed, t + 1)
                act.activation(rn[:], ss[:], ACT.Sqrt, bias=k.eps[:, 1:2]).then_inc(lengths, 1)
                act.wait_ge(turned3, 3 * t + 2)
                act.activation(kq[:, 1, :], pq[:], ACT.Copy).then_inc(moved, 1)

        @block.tensor
        def _(pe):
            ident = k.const[:, C_ID:C_ID + P]
            pe.sem_inc(unmasked, 1)
            with pe.Fori(0, NPAIR) as t:
                pe.wait_ge(normed, t + 1)
                for j in range(TPP):
                    mm = pe.transpose(px[:, j * P:j * P + P], xn[:, j * D:j * D + D], ident)
                mm.then_inc(turned, 1)
                pe.wait_ge(evac, t + 1)
                for j in range(TPP):
                    if j == 0:
                        pe.wait_ge(unmasked, t + 1)
                    at = (j % 2) * P
                    for tap in range(TAPS):
                        pe.matmul(pa[:, j, 0:3 * D], xnT[:, j // 2, at + tap:at + tap + P], k.wtap[:, tap, :],
                                  start=(tap == 0), stop=(tap == TAPS - 1))
                    pe.matmul(pa[:, j, 3 * D:3 * D + H], xnT[:, j // 2, at + PAD:at + PAD + P], k.wb[:],
                              start=True, stop=True).then_inc(projected, 1)
                pe.wait_ge(silued, (t + 1) * TPP)
                for j in range(TPP):
                    mm = pe.transpose(pv[:, j * P:j * P + P], qkv[:, j, 2 * D:3 * D], ident)
                pe.wait_ge(scaled, t + 1)
                for j in range(TPP):
                    mm = pe.transpose(pk[:, j * P:j * P + P], qk[:, j, D:2 * D], ident)
                mm.then_inc(turned3, 1)
                for j in range(TPP):
                    mm = pe.transpose(pq[:, j * P:j * P + P], qk[:, j, 0:D], ident)
                mm.then_inc(turned3, 2)
                wait_apart(pe, moved, 3 * (t + 1), beat)
                for j in range(TPP):
                    for n in range(QC):
                        at = j * P + n * CHUNK
                        for h in range(H):
                            rows = slice(h * DH, h * DH + DH)
                            mm = pe.matmul(pa[n * CHUNK:n * CHUNK + CHUNK, h, j * 64:j * 64 + 64],
                                           kq[rows, 0, at:at + CHUNK], kq[rows, :, at:at + CHUNK],
                                           start=True, stop=True)
                mm.then_inc(grammed, 1)

        @block.sync
        def _(sp):
            sp.sem_inc(room, 1)
            with sp.Fori(0, NPAIR) as t:
                def save(field, src):
                    shape = io.pair[bass.ds(t * P, P), field * PT:field * PT + PT]
                    if len(src.shape) == 3:
                        shape = shape.rearrange("p (a b) -> p a b", a=src.shape[1])
                    sp.dma_start(shape, src).then_inc(saved, 16)

                wait_apart(sp, evac, t + 1, beat)
                save(6, xnT[:, :, PAD:])
                wait_apart(sp, silued, (t + 1) * TPP, beat)
                save(2, qkv[:, :, 2 * D:3 * D])
                wait_apart(sp, scaled, t + 1, beat)
                save(1, qk[:, :, D:2 * D])
                wait_apart(sp, moved, 3 * (t + 1), beat)
                save(0, kq[:, 1, :])
                sp.dma_start(io.vT[bass.ds(t * P, P), :], vT[:]).then_inc(saved, 16)
                wait_apart(sp, chain, (t + 1) * LINKS, beat)
                save(3, kb[:])
                save(4, vb[:])
                save(5, loc[:].rearrange("p a b -> p (a b)"))
                wait_apart(sp, weighted, t + 1, beat)
                for n in range(QC):
                    dst = io.low[bass.ds((t * QC + n) * G, G), :].rearrange("g (c e) -> c g e", e=CHUNK)
                    sp.dma_start(dst, low[n * CHUNK:n * CHUNK + CHUNK, :, :]).then_inc(saved, 16)
                sp.wait_ge(saved, (t + 1) * 16 * NSAVE)
                sp.sem_inc(room, 1)


def invert(nc, io, keep):
    k = keep
    with ExitStack() as ctx:
        m = Memory(nc, ctx)
        sem, sb = m.sem, m.sb
        low = [sb(f"ilow{i}", [P, CHUNK, CHUNK]) for i in range(2)]
        inv = [sb(f"inv{i}", [P, CHUNK, CHUNK]) for i in range(2)]
        prod = sb("prod", [P, CHUNK * CHUNK])
        vpad = [sb(f"vpad{i}", [P, LAGS - 1 + SEQ]) for i in range(2)]
        pm = [m.ps(f"pm{i}", [P, 512]) for i in range(2)]
        lgot, vgot = [sem(f"lgot{i}") for i in range(2)], [sem(f"vgot{i}") for i in range(2)]
        beat, chain, inverted, stored = sem("ibeat"), sem("ichain"), sem("inverted"), sem("stored_inv")
        padded, convolved, kept, vfree = sem("vpadded"), sem("convolved"), sem("kept"), sem("vfree")
        block = ctx.enter_context(nc.Block())
        ifree = sem("ifree")
        NINV = BATCH * H * NCH // P
        ROWS = CHUNK - 1

        @block.sync
        def _(sp):
            sp.wait_ge(padded, 2)
            with sp.Fori(0, BATCH // 2) as r:
                for par in range(2):
                    wait_apart(sp, vfree, r * 2 + par + 1, beat)
                    sp.dma_start(vpad[par][:, LAGS - 1:], io.vT[bass.ds(r * P, P), par * SEQ:par * SEQ + SEQ])\
                      .then_inc(vgot[par], 16)

        @block.gpsimd
        def _(pool):
            for par in range(2):
                pool.memset(vpad[par][:, 0:LAGS - 1], 0.0).then_inc(padded, 1)
            for n in range(2):
                pool.dma_start(low[n][:].rearrange("p a b -> p (a b)"), io.low[n * P:n * P + P, :])\
                    .then_inc(lgot[n], 16)
            pool.sem_inc(ifree, 2)
            for n in range(NINV):
                pool.wait_ge(inverted, n + 1)
                pool.dma_start(io.inv[n * P:n * P + P, :], inv[n % 2][:].rearrange("p a b -> p (a b)"))\
                    .then_inc(stored, 16)
                if n + 2 < NINV:
                    pool.dma_start(low[n % 2][:].rearrange("p a b -> p (a b)"), io.low[(n + 2) * P:(n + 3) * P, :])\
                        .then_inc(lgot[n % 2], 16)
                pool.wait_ge(stored, 16 * (n + 1))
                pool.sem_inc(ifree, 1)

        @block.vector
        def _(dve):
            with dve.Fori(0, NINV // 2) as r:
                for par in range(2):
                    n = r * 2 + par
                    A, T = low[par], inv[par]
                    steps = Steps(dve, chain, n * (2 * ROWS + 1))
                    dve.wait_ge(ifree, n + 1)
                    dve.wait_ge(lgot[par], (r + 1) * 16)
                    steps.done(dve.tensor_copy(T[:].rearrange("p a b -> p (a b)"), k.const[:, C_EYE:C_END]))
                    for i in range(1, CHUNK):
                        part = prod[:, 0:i * i].rearrange("p (c j) -> p c j", j=i)
                        steps.done(dve.tensor_tensor(part, bc(A[:, i:i + 1, 0:i], [P, i, i]), T[:, 0:i, 0:i],
                                                     ALU.mult))
                        last = dve.tensor_reduce(T[:, 0:i, i], part, AX.X, ALU.add)
                        if i < CHUNK - 1:
                            steps.done(last)
                    steps.done(last)
                    dve.sem_inc(inverted, 1)

        @block.tensor
        def _(pe):
            pe.sem_inc(vfree, 2)
            with pe.Fori(0, BATCH // 2) as r:
                for par in range(2):
                    b = r * 2 + par
                    pe.wait_ge(vgot[par], (r + 1) * 16)
                    pe.wait_ge(kept, b + 1)
                    for half in range(2):
                        for lag in range(LAGS):
                            at = LAGS - 1 - lag + half * P
                            mm = pe.matmul(pm[par][:, half * P:half * P + P], vpad[par][:, at:at + P],
                                           k.lag[:, lag, :], start=(lag == 0), stop=(lag == LAGS - 1))
                    mm.then_inc(convolved, 1)

        @block.scalar
        def _(act):
            act.sem_inc(kept, 2)
            with act.Fori(0, BATCH // 2) as r:
                for par in range(2):
                    b = r * 2 + par
                    act.wait_ge(convolved, b + 1)
                    act.sem_inc(vfree, 1)
                    act.activation(k.ms[:, bass.ds(b * 2, 2), :].rearrange("p a b -> p (a b)"),
                                   pm[par][:, 0:SEQ], ACT.Copy).then_inc(kept, 1)


def attend(nc, io, keep):
    k = keep
    G = TPP * H
    with ExitStack() as ctx:
        m = Memory(nc, ctx)
        sem, sb = m.sem, m.sb
        qT, kn, kb, vb = (sb(f"a_{n}", [P, PT]) for n in ("qT", "kn", "kb", "vb"))
        loc, inv = sb("a_loc", [P, G, CHUNK]), sb("a_inv", [P, G, CHUNK])
        v, xnT = sb("a_v", [P, TPP, D]), sb("a_xnT", [P, PT])
        u, wT = sb("u", [P, TPP, D]), sb("wT", [P, PT])
        state = [sb(f"state{i}", [P, D]) for i in range(2)]
        delta = sb("delta", [P, TPP, D])
        mean = sb("mean", [P, TPP, NOUT])
        meanT = sb("meanT", [NOUT, PT])
        hdn = sb("hdn", [P, 2, PT])
        lg, top = sb("lg", [P, G, 3]), sb("ltop", [P, G])
        mix, part = sb("mix", [P, TPP, D]), sb("part", [P, TPP, D])
        sq, ss, rs = sb("osq", [P, TPP, D]), sb("oss", [P, G]), sb("ors", [P, G])
        oT = sb("oT", [P, PT])
        pu = m.ps("a_pu", [P, 512])
        pw = m.ps("a_pw", [P, 4, 512])
        po = [m.ps(f"a_po{i}", [P, 512]) for i in range(2)]
        pf = m.ps("a_pf", [P, 512])
        pread, pstate = [pw[:, i, :] for i in range(2)], [pw[:, 2 + i, :] for i in range(2)]
        chain, beat = sem("achain"), sem("abeat")
        scangot, gategot, scandone, gatedone = sem("scangot"), sem("gategot"), sem("scandone"), sem("gatedone")
        solved, taken = sem("solved"), sem("taken")
        reads, subbed, updated, stated = ([sem(f"{n}{i}") for i in range(2)]
                                          for n in ("reads", "subbed", "updated", "stated"))
        out, outed = sem("out"), sem("outed")
        meaned, meanturned, meankept = sem("meaned"), sem("meanturned"), sem("meankept")
        hidden, gelued, gated, lowered, powered = (sem("hidden"), sem("gelued"), sem("gated"), sem("lowered"),
                                                   sem("lpowered"))
        mixed, squared, summed, rooted = sem("omixed"), sem("osquared"), sem("osummed"), sem("orooted")
        scaled, oturned, okept, done, added = sem("oscaled"), sem("oturned"), sem("okept"), sem("done"), sem("added")
        block = ctx.enter_context(nc.Block())
        SCANLOADS, GATELOADS = 5 + QC, 2
        LINKS = 11

        @block.sync
        def _(sp):
            sp.sem_inc(scandone, 1)
            sp.sem_inc(gatedone, 1)
            with sp.Fori(0, NPAIR) as t:
                def load(dst, field, sem_):
                    sp.dma_start(dst, io.pair[bass.ds(t * P, P), field * PT:field * PT + PT]).then_inc(sem_, 16)

                wait_apart(sp, scandone, t + 1, beat)
                load(qT[:], 0, scangot)
                load(kn[:], 1, scangot)
                load(kb[:], 3, scangot)
                load(vb[:], 4, scangot)
                load(loc[:].rearrange("p a b -> p (a b)"), 5, scangot)
                for n in range(QC):
                    src = io.inv[bass.ds((t * QC + n) * G, G), :].rearrange("g (e c) -> e g c", c=CHUNK)
                    sp.dma_start(inv[n * CHUNK:n * CHUNK + CHUNK, :, :], src).then_inc(scangot, 16)
                wait_apart(sp, gatedone, t + 1, beat)
                load(v[:].rearrange("p a b -> p (a b)"), 2, gategot)
                load(xnT[:], 6, gategot)

        @block.tensor
        def _(pe):
            ident = k.const[:, C_ID:C_ID + P]
            pe.sem_inc(added, 1)
            with pe.Fori(0, NPAIR) as t:
                pe.wait_ge(scangot, (t + 1) * 16 * SCANLOADS)
                wait_apart(pe, added, t + 1, beat)
                for j in range(TPP):
                    for n in range(QC):
                        rows = slice(n * CHUNK, n * CHUNK + CHUNK)
                        for h in range(H):
                            g, at = j * H + h, j * D + h * DH
                            pe.matmul(pu[rows, at:at + DH], inv[rows, g, :], vb[rows, at:at + DH],
                                      start=True, stop=True)
                            mm = pe.matmul(pw[h * DH:h * DH + DH, n, j * CHUNK:j * CHUNK + CHUNK],
                                           kb[rows, at:at + DH], inv[rows, g, :], start=True, stop=True)
                mm.then_inc(solved, 1)
                pe.wait_ge(taken, 2 * (t + 1))
                for n in range(NCH):
                    j0, rows = n // QC, slice(n % QC * CHUNK, n % QC * CHUNK + CHUNK)
                    for b in range(2):
                        j = 2 * b + j0
                        at = j * P + n % QC * CHUNK
                        if n:
                            pe.wait_ge(stated[b], t * (NCH - 1) + n)
                            pe.matmul(pread[b][rows, 0:D], wT[:, at:at + CHUNK], state[b][:],
                                      start=True, stop=True).then_inc(reads[b], 1)
                            pe.matmul(po[b][rows, j0 * D:j0 * D + D], qT[:, at:at + CHUNK], state[b][:],
                                      start=True, stop=False, skip_group_check=True)
                    for b in range(2):
                        j = 2 * b + j0
                        if n:
                            wait_apart(pe, subbed[b], t * (NCH - 1) + n, beat)
                        if n < NCH - 1:
                            pe.matmul(pstate[b][:, 0:D], kn[rows, j * D:j * D + D], u[rows, j, :],
                                      start=(n == 0), stop=True, skip_group_check=True).then_inc(updated[b], 1)
                        for h in range(H):
                            col = j0 * D + h * DH
                            mm = pe.matmul(po[b][rows, col:col + DH], loc[rows, j * H + h, :],
                                           u[rows, j, h * DH:h * DH + DH], start=(n == 0), stop=True,
                                           skip_group_check=True)
                        if n == NCH - 1:
                            mm.then_inc(out, 1)
                pe.wait_ge(meaned, t + 1)
                for j in range(TPP):
                    mm = pe.transpose(pf[0:NOUT, j * P:j * P + P], mean[:, j, :], ident)
                mm.then_inc(meanturned, 1)
                pe.wait_ge(meankept, t + 1)
                pe.wait_ge(gategot, (t + 1) * 16 * GATELOADS)
                for f in range(2):
                    pe.matmul(pw[:, f, :], k.w1[:, f * P:f * P + P], xnT[:], start=True, stop=False)
                    pe.matmul(pw[:, f, :], k.w1s[:, f * P:f * P + P], meanT[:], start=False,
                              stop=True).then_inc(hidden, 1)
                pe.wait_ge(gelued, 2 * (t + 1))
                for j in range(TPP):
                    for f in range(2):
                        mm = pe.matmul(pu[:, j * NOUT:j * NOUT + NOUT], hdn[:, f, j * P:j * P + P], k.w2[:, f, :],
                                       start=(f == 0), stop=(f == 1))
                mm.then_inc(gated, 1)
                pe.wait_ge(scaled, t + 1)
                for j in range(TPP):
                    mm = pe.transpose(pf[:, j * P:j * P + P], mix[:, j, :], ident)
                mm.then_inc(oturned, 1)
                pe.wait_ge(okept, t + 1)
                for j in range(TPP):
                    mm = pe.matmul(pu[:, j * P:j * P + P], oT[:, j * P:j * P + P], k.wout[:], start=True, stop=True)
                mm.then_inc(done, 1)

        @block.vector
        def _(dve):
            heads = lambda ap: ap.rearrange("p a (b c) -> p (a b) c", c=DH)
            flat = lambda ap: ap.rearrange("p a b -> p (a b)")
            with dve.Fori(0, NPAIR) as t:
                steps = Steps(dve, chain, t * LINKS)
                link = steps.done
                dve.wait_ge(solved, t + 1)
                dve.tensor_copy(flat(u[:]), pu[:]).then_inc(taken, 1)
                dve.tensor_copy(wT[:].rearrange("p (a n c) -> p n a c", a=TPP, n=QC),
                                pw[:, :, 0:TPP * CHUNK].rearrange("p n (a c) -> p n a c", a=TPP)).then_inc(taken, 1)
                dve.wait_ge(taken, 2 * (t + 1))
                for n in range(NCH):
                    j0, rows = n // QC, slice(n % QC * CHUNK, n % QC * CHUNK + CHUNK)
                    for b in range(2):
                        if n:
                            dve.wait_ge(reads[b], t * (NCH - 1) + n)
                            dve.tensor_tensor(u[rows, 2 * b + j0, :], u[rows, 2 * b + j0, :], pread[b][rows, 0:D],
                                              ALU.subtract).then_inc(subbed[b], 1)
                    for b in range(2):
                        if n < NCH - 1:
                            dve.wait_ge(updated[b], t * (NCH - 1) + n + 1)
                            dve.tensor_tensor(state[b][:], pstate[b][:, 0:D], k.const[:, C_HEAD:C_HEAD + P],
                                              ALU.mult).then_inc(stated[b], 1)
                dve.wait_ge(outed, 2 * (t + 1))
                dve.sem_inc(scandone, 1)
                dve.wait_ge(gategot, (t + 1) * 16 * GATELOADS)
                ms = k.ms[:, bass.ds(t * TPP, TPP), :]
                for i, src in enumerate((ms, delta[:], v[:])):
                    last = dve.tensor_reduce(mean[:, :, i * H:i * H + H],
                                             src.rearrange("p a (b c) -> p a b c", c=DH), AX.X, ALU.add,
                                             apply_absolute_value=True)
                last.then_inc(meaned, 1)
                dve.wait_ge(gated, t + 1)
                link(dve.tensor_tensor(lg[:].rearrange("p (a h) b -> p a (h b)", a=TPP),
                                       pu[:, 0:TPP * NOUT].rearrange("p (a b) -> p a b", a=TPP),
                                       bc(k.b2[:].unsqueeze(1), [P, TPP, NOUT]), ALU.add))
                link(dve.tensor_reduce(top[:], lg[:], AX.X, ALU.max))
                dve.tensor_tensor(lg[:], lg[:], bc(top[:].unsqueeze(2), [P, G, 3]), ALU.subtract).then_inc(lowered, 1)
                dve.wait_ge(powered, t + 1)
                link(dve.tensor_reduce(top[:], lg[:], AX.X, ALU.add))
                link(dve.reciprocal(top[:], top[:]))
                link(dve.tensor_tensor(lg[:], lg[:], bc(top[:].unsqueeze(2), [P, G, 3]), ALU.mult))
                weight = lambda i: bc(lg[:, :, i:i + 1], [P, G, DH])
                dve.tensor_tensor(heads(mix[:]), heads(ms), weight(0), ALU.mult)
                link(dve.tensor_tensor(heads(part[:]), heads(delta[:]), weight(1), ALU.mult))
                link(dve.tensor_tensor(mix[:], mix[:], part[:], ALU.add))
                link(dve.tensor_tensor(heads(part[:]), heads(v[:]), weight(2), ALU.mult))
                link(dve.tensor_tensor(mix[:], mix[:], part[:], ALU.add))
                dve.sem_inc(mixed, 1)
                dve.sem_inc(gatedone, 1)
                dve.wait_ge(squared, t + 1)
                dve.tensor_reduce(ss[:], heads(sq[:]), AX.X, ALU.add).then_inc(summed, 1)
                dve.wait_ge(rooted, t + 1)
                link(dve.reciprocal(rs[:], rs[:]))
                dve.tensor_tensor(heads(mix[:]), heads(mix[:]), bc(rs[:].unsqueeze(2), [P, G, DH]),
                                  ALU.mult).then_inc(scaled, 1)
                dve.wait_ge(done, t + 1)
                x = k.x[:, bass.ds(t * TPP, TPP), :].rearrange("p a b -> p (a b)")
                link(dve.tensor_tensor(x, x, pu[:], ALU.add))
                dve.sem_inc(added, 1)
                assert steps.n == LINKS, steps.n

        @block.scalar
        def _(act):
            flat = lambda ap: ap.rearrange("p a b -> p (a b)")
            with act.Fori(0, NPAIR) as t:
                act.wait_ge(out, 2 * (t + 1))
                for b in range(2):
                    act.activation(flat(delta[:, 2 * b:2 * b + 2, :]), po[b][:, 0:SEQ], ACT.Copy).then_inc(outed, 1)
                act.wait_ge(meanturned, t + 1)
                act.activation(meanT[:], pf[0:NOUT, :], ACT.Copy, scale=1.0 / DH).then_inc(meankept, 1)
                for f in range(2):
                    act.wait_ge(hidden, t * 2 + f + 1)
                    act.activation(hdn[:, f, :], pw[:, f, :], ACT.Gelu, bias=k.b1[:, f:f + 1]).then_inc(gelued, 1)
                act.wait_ge(lowered, t + 1)
                act.activation(lg[:], lg[:], ACT.Exp).then_inc(powered, 1)
                act.wait_ge(mixed, t + 1)
                act.activation(sq[:], mix[:], ACT.Square).then_inc(squared, 1)
                act.wait_ge(summed, t + 1)
                act.activation(rs[:], ss[:], ACT.Sqrt, bias=k.eps[:, 2:3], scale=1.0 / DH).then_inc(rooted, 1)
                act.wait_ge(oturned, t + 1)
                act.activation(oT[:], pf[:], ACT.Copy).then_inc(okept, 1)


def collect(nc, io, keep):
    k = keep
    with ExitStack() as ctx:
        m = Memory(nc, ctx)
        got = m.sb("cgot", [P, NT, TOPK, D])
        gathered = [m.sem(f"cgathered{i}") for i in range(NPAIR)]
        added, stored = m.sem("cadded"), m.sem("cstored")
        block = ctx.enter_context(nc.Block())

        @block.gpsimd
        def _(pool):
            for j in range(NT):
                for c in range(TOPK):
                    pool.indirect_dma_start(
                        got[:, j, c, :], None, io.rows,
                        bass.IndirectOffsetOnAxis(ap=k.slot[:, j, c:c + 1], axis=0)).then_inc(gathered[j // TPP], 16)

        @block.vector
        def _(dve):
            for t in range(NPAIR):
                dve.wait_ge(gathered[t], TPP * TOPK * 16)
                for c in range(TOPK):
                    for j in range(t * TPP, (t + 1) * TPP):
                        dve.scalar_tensor_tensor(k.x[:, j, :], got[:, j, c, :], k.share[:, j, c:c + 1], k.x[:, j, :],
                                                 ALU.mult, ALU.add).then_inc(added, 1)
                    dve.wait_ge(added, t * TPP * TOPK + (c + 1) * TPP)

        @block.sync
        def _(sp):
            dst = io.out.rearrange("(n p) d -> p n d", p=P)
            for t in range(NPAIR):
                sp.wait_ge(added, (t + 1) * TPP * TOPK)
                sp.dma_start(dst[:, t * TPP:(t + 1) * TPP, :], k.x[:, t * TPP:(t + 1) * TPP, :]).then_inc(stored, 16)
            sp.wait_ge(stored, 16 * NPAIR)


class Kept:

    def __init__(self, m):
        self.x = m.sb("x", [P, NT, D])
        self.const = m.sb("const", [P, C_END])
        self.gate = m.sb("gate", [P, E])
        self.wb = m.sb("wb", [P, H])
        self.wtap = m.sb("wtap", [P, TAPS, 3 * D])
        self.w1, self.w1s = m.sb("w1", [P, 2 * D]), m.sb("w1s", [NOUT, 2 * D])
        self.b1 = m.sb("b1", [P, 2])
        self.w2, self.b2 = m.sb("w2", [P, 2, NOUT]), m.sb("b2", [P, NOUT])
        self.wout = m.sb("wout", [P, D])
        self.lag = m.sb("lag", [P, LAGS, D])
        self.eps = m.sb("eps", [P, 3])
        self.count = m.sb("count", [P, TOPK * E])
        self.slot = m.sb("slot", [P, YB, TOPK], U32)
        self.share = m.sb("share", [P, NT, TOPK])
        self.upper, self.ones = m.sb("upper", [P, P], BF16), m.sb("ones", [P, P], BF16)
        self.ms = m.sb("ms", [P, NT, D])


class Dram:

    def __init__(self, nc, arrays):
        def given(n):
            v = arrays[n]
            return nc.dram_tensor(n + "_in", v.shape, mybir.dt.from_np(v.dtype), kind="ExternalInput").ap()

        def scratch(n, *shape):
            return nc.dram_tensor(n, shape, F32, kind="Internal").ap()

        self.x, self.const, self.gate, self.wexp = given("x"), given("const"), given("gate"), given("wexp")
        self.wqkv, self.taps, self.wb = given("wqkv"), given("taps"), given("wb")
        self.ms3, self.ms15, self.ms31 = given("ms3"), given("ms15"), given("ms31")
        self.mixT, self.chan = given("mixT"), given("chan")
        self.w1, self.b1, self.w2, self.b2 = given("w1"), given("b1"), given("w2"), given("b2")
        self.onorm, self.wo = given("onorm"), given("wo")
        self.out = nc.dram_tensor("out", (BATCH * SEQ, D), F32, kind="ExternalOutput").ap()
        self.queue = scratch("queue", SLOTS, D)
        self.rows = scratch("rows", SLOTS + 1, D)
        self.pair = scratch("pair", NPAIR * P, 7 * PT)
        self.vT = scratch("vT_dram", NPAIR * P, PT)
        self.low = scratch("low_dram", BATCH * H * NCH, CHUNK * CHUNK)
        self.inv = scratch("inv_dram", BATCH * H * NCH, CHUNK * CHUNK)


def program(nc, io):
    with ExitStack() as ctx:
        keep = Kept(Memory(nc, ctx))
        prepare(nc, io, keep)
        route(nc, io, keep, "r1")
        experts(nc, io, keep, "e1")
        project(nc, io, keep)
        invert(nc, io, keep)
        attend(nc, io, keep)
        route(nc, io, keep, "r2")
        experts(nc, io, keep, "e2")
        collect(nc, io, keep)


def layouts(inputs):
    a = {n: np.asarray(v) for n, v in inputs.items()}
    at = lambda n: a["L0_attn_" + n]
    ff = lambda n: a["L0_ffn_" + n]
    wo = ff("wo").transpose(0, 2, 1).reshape(E, FT, P, D).transpose(0, 2, 1, 3).reshape(E, P, F)
    out = {
        "x": at("hidden_states").reshape(BATCH * SEQ, D),
        "const": shape_constants(),
        "gate": ff("gate_w").T,
        "wexp": np.concatenate([ff("wi_gate").transpose(0, 2, 1), ff("wi_up").transpose(0, 2, 1), wo],
                               axis=2).reshape(E * P, 3 * F),
        "wqkv": np.stack([at("Wq"), at("Wk"), at("Wv")], axis=1),
        "taps": np.stack([at("conv_q_w").T, at("conv_k_w").T, at("conv_v_w").T], axis=1).reshape(-1),
        "wb": at("Wb"), "ms3": at("ms_w3"), "ms15": at("ms_w15"), "ms31": at("ms_w31"),
        "mixT": at("kernel_mix_w").T, "chan": at("channel_mixer_w"),
        "w1": at("fusion_w1"), "b1": at("fusion_b1").reshape(2, P).T, "w2": at("fusion_w2"), "b2": at("fusion_b2"),
        "onorm": at("o_norm_w"), "wo": at("Wo"),
    }
    return {n: np.ascontiguousarray(v) for n, v in out.items()}


def build(nc, arrays):
    program(nc, Dram(nc, arrays))


def kernel(**inputs):
    import concourse.bacc as bacc
    from concourse.bass_utils import run_bass_kernel_spmd

    arrays = layouts(inputs)
    nc = bacc.Bacc("TRN2", target_bir_lowering=False, num_devices=1)
    build(nc, arrays)
    r = run_bass_kernel_spmd(nc, [{n + "_in": v for n, v in arrays.items()}], core_ids=[0])
    return r.results[0]["out"].reshape(BATCH, SEQ, D)
```

```python
from contextlib import ExitStack

import numpy as np

import concourse.bass as bass
from concourse import mybir

F32 = mybir.dt.float32
F32R = mybir.dt.float32r
BF16 = mybir.dt.bfloat16
U32 = mybir.dt.uint32
ALU = mybir.AluOpType
ACT = mybir.ActivationFunctionType
AX = mybir.AxisListType

P = 128
BATCH, SEQ, D = 16, 256, 128
H, DH = 4, 32
CHUNK = 32
NT = BATCH * SEQ // P
TPP = 4
NPAIR = NT // TPP
PT = TPP * P
NCH = SEQ // CHUNK
QC = P // CHUNK
E, TOPK, F = 8, 2, 512
CAP = int(BATCH * SEQ / E * 1.25)
SLOTS = E * CAP
CT = CAP // P
HALF = CAP // 2
FT = F // P
TAPS = 4
PAD = TAPS - 1
LAGS = 31
MS = SEQ // P * LAGS
GRP = 8
YB = NT + 2 * TPP
NGRP = NT // GRP
NOUT = 3 * H
LN_EPS, L2_EPS, RMS_EPS = 1e-5, 1e-6, 1e-5

C_ID, C_HEAD, C_UP, C_ONE = 0, 128, 256, 384
C_NEG, C_INC, C_IOTA, C_EYE = 512, 544, 576, 584
C_END = C_EYE + CHUNK * CHUNK


def shape_constants():
    c = np.zeros((P, C_END), np.float32)
    p = np.arange(P)
    c[:, C_ID:C_ID + P] = np.eye(P)
    c[:, C_HEAD:C_HEAD + P] = p[:, None] // DH == p[None, :] // DH
    c[:, C_UP:C_UP + P] = p[:, None] < p[None, :]
    c[:, C_ONE:C_ONE + P] = 1.0
    e = np.arange(CHUNK)
    c[:, C_NEG:C_NEG + CHUNK] = -1.0 * (e[None, :] < p[:, None] % CHUNK)
    c[:, C_INC:C_INC + CHUNK] = p[:, None] % CHUNK <= e[None, :]
    c[:, C_IOTA:C_IOTA + E] = np.arange(E)
    c[:, C_EYE:C_END] = np.eye(CHUNK).reshape(1, -1)
    return c


def bc(ap, shape):
    return ap.to_broadcast(list(shape))


class Memory:

    def __init__(self, nc, ctx):
        self.nc, self.ctx = nc, ctx

    def sb(self, name, shape, dt=F32):
        return self.ctx.enter_context(self.nc.sbuf_tensor(name, list(shape), dt))

    def ps(self, name, shape, dt=F32):
        return self.ctx.enter_context(self.nc.psum_tensor(name, list(shape), dt))

    def sem(self, name):
        return self.ctx.enter_context(self.nc.semaphore(name))


def prepare(nc, io, keep):
    with ExitStack() as ctx:
        m = Memory(nc, ctx)
        k = keep
        wqkv = m.sb("wqkv", [P, 3, D])
        taps = m.sb("taps", [P, TAPS, 3 * D])
        ms3, ms15, ms31 = m.sb("ms3", [P, 3]), m.sb("ms15", [P, 15]), m.sb("ms31", [P, 31])
        mixT = m.sb("mixT", [P, 3 * D])
        chan = m.sb("chan", [P, D])
        base = m.sb("base", [P, 3, D])
        wo_raw = m.sb("wo_raw", [P, D])
        onorm = m.sb("onorm", [P, 1])
        zero = m.sb("zero", [P, 20 * D])
        pbase = m.ps("pbase", [P, 512])
        loaded, mixed, cleared = m.sem("loaded"), m.sem("mixed"), m.sem("cleared")
        based, wiped, folded = m.sem("based"), m.sem("wiped"), m.sem("folded")
        block = ctx.enter_context(nc.Block())
        loads = [
            (k.x[:], io.x.rearrange("(n p) d -> p n d", p=P)),
            (k.const[:], io.const), (k.gate[:], io.gate), (wqkv[:], io.wqkv),
            (taps[:].rearrange("p a b -> p (a b)"), io.taps.partition_broadcast(P)),
            (k.wb[:], io.wb), (ms3[:], io.ms3), (ms15[:], io.ms15), (ms31[:], io.ms31),
            (chan[:], io.chan), (k.w1[:], io.w1[0:D, :]), (k.w1s[:], io.w1[D:D + NOUT, :]),
            (k.b1[:], io.b1), (k.w2[:], io.w2.rearrange("(f p) n -> p f n", p=P)),
            (k.b2[:], io.b2.partition_broadcast(P)), (wo_raw[:], io.wo),
        ] + [(onorm[DH * h:DH * h + DH, :], io.onorm.rearrange("(d a) -> d a", a=1)) for h in range(H)]

        @block.sync
        def _(sp):
            for dst, src in loads:
                sp.dma_start(dst, src).then_inc(loaded, 16)
            sp.wait_ge(wiped, 1)
            for h in range(H):
                sp.dma_start(mixT[DH * h:DH * h + DH, 3 * DH * h:3 * DH * h + 3 * DH], io.mixT).then_inc(mixed, 16)
            sp.wait_ge(wiped, 2)
            for c in range(TOPK):
                queue = io.queue[c].rearrange("(p r) d -> p (r d)", p=P)
                for n in range(SLOTS // P // 20):
                    sp.dma_start(queue[:, n * 20 * D:(n + 1) * 20 * D], zero[:]).then_inc(cleared, 16)
                sp.dma_start(io.rows[c][SLOTS:SLOTS + 1, :], zero[0:1, 0:D]).then_inc(cleared, 16)
            sp.wait_ge(cleared, 16 * TOPK * (SLOTS // P // 20 + 1))

        @block.tensor
        def _(pe):
            pe.wait_ge(loaded, 16 * len(loads))
            pe.wait_ge(mixed, 16 * H)
            for s in range(3):
                mm = pe.matmul(pbase[:, s * D:s * D + D], mixT[:, s * D:s * D + D], chan[:], start=True, stop=True)
            mm.then_inc(based, 1)

        @block.vector
        def _(dve):
            dve.memset(mixT[:], 0.0).then_inc(wiped, 1)
            dve.memset(zero[:], 0.0).then_inc(wiped, 1)
            dve.memset(k.eps[:, 0:1], LN_EPS)
            dve.memset(k.eps[:, 1:2], L2_EPS)
            dve.memset(k.eps[:, 2:3], RMS_EPS)
            dve.memset(k.slot[:], 0)
            dve.wait_ge(loaded, 16 * len(loads))
            dve.tensor_copy(k.upper[:], k.const[:, C_UP:C_UP + P])
            dve.tensor_copy(k.ones[:], k.const[:, C_ONE:C_ONE + P])
            for j in range(TAPS):
                dve.tensor_tensor(k.wtap[:, j, :], taps[:, j, :], wqkv[:].rearrange("p a b -> p (a b)"), ALU.mult)
            dve.tensor_scalar(k.wout[:], wo_raw[:], onorm[:, 0:1], None, ALU.mult)
            dve.wait_ge(based, 1)
            dve.tensor_copy(base[:].rearrange("p a b -> p (a b)"), pbase[:, 0:3 * D]).then_inc(folded, 1)
            dve.wait_ge(folded, 1)
            for lag in range(LAGS):
                dve.tensor_scalar(k.lag[:, lag, :], base[:, 2, :], ms31[:, 30 - lag:31 - lag], None,
                                  ALU.mult).then_inc(folded, 1)
            dve.wait_ge(folded, 1 + LAGS)
            for lag in range(15):
                dve.scalar_tensor_tensor(k.lag[:, lag, :], base[:, 1, :], ms15[:, 14 - lag:15 - lag],
                                         k.lag[:, lag, :], ALU.mult, ALU.add).then_inc(folded, 1)
            dve.wait_ge(folded, 1 + LAGS + 15)
            for lag in range(3):
                dve.scalar_tensor_tensor(k.lag[:, lag, :], base[:, 0, :], ms3[:, 2 - lag:3 - lag],
                                         k.lag[:, lag, :], ALU.mult, ALU.add).then_inc(folded, 1)
            dve.wait_ge(folded, 1 + LAGS + 18)



class Steps:

    def __init__(self, eng, sem, base=0):
        self.eng, self.sem, self.base, self.n = eng, sem, base, 0

    def done(self, ins):
        self.n += 1
        ins.then_inc(self.sem, 1)
        self.eng.wait_ge(self.sem, self.base + self.n)


def wait_apart(eng, sem, value, beat):
    eng.wait_ge(sem, value)
    eng.sem_inc(beat, 1)


def layernorm_stats(dve, link, stat, mv, tiles, varied, beat):
    for j, tile in enumerate(tiles):
        last = dve.bn_stats(stat[:, j, :], tile)
    link(last)
    dve.sem_inc(beat, 1)
    for j in range(len(tiles)):
        last = dve.bn_aggr(mv[:, j, :], stat[:, j, :])
    last.then_inc(varied, 1)


def scatter(pool, k, io, j, c, sent):
    pool.indirect_dma_start(io.queue[c], bass.IndirectOffsetOnAxis(ap=k.slot[:, j, c:c + 1], axis=0),
                            k.xn[:, j, :], None, bounds_check=SLOTS - 1, oob_is_err=False).then_inc(sent, 16)


def gather(pool, io, c, slot, dst, got):
    pool.indirect_dma_start(dst, None, io.rows[c], bass.IndirectOffsetOnAxis(ap=slot, axis=0)).then_inc(got, 16)


def route(nc, io, keep, name):
    k = keep
    with ExitStack() as ctx:
        m = Memory(nc, ctx)
        sem = lambda s: m.sem(f"{name}_{s}")
        sb = lambda s, shape, dt=F32: m.sb(f"{name}_{s}", shape, dt)
        stat, mv = sb("stat", [P, GRP, 6]), sb("mv", [P, GRP, 2])
        std, rstd = sb("std", [P, GRP]), sb("rstd", [P, GRP])
        xn = k.xn
        xnT = sb("xnT", [P, GRP * P])
        logit = sb("logit", [P, GRP, E])
        top, index = sb("top", [P, GRP, 8]), sb("index", [P, GRP, 8], U32)
        idx = sb("idx", [P, GRP, TOPK])
        hot = sb("hot", [P, GRP, TOPK, E], BF16)
        seen = [sb(f"seen{i}", [P, 1, TOPK * E], BF16) for i in range(2)]
        more = sb("more", [P, TOPK * E])
        prod, pos = sb("prod", [P, GRP * TOPK, E]), sb("pos", [P, GRP, TOPK])
        place, valid = sb("place", [P, GRP, TOPK]), sb("valid", [P, GRP, TOPK])
        gap, ratio, share = sb("gap", [P, GRP]), sb("ratio", [P, GRP]), sb("share", [P, GRP, TOPK])
        ptr = m.ps(f"{name}_ptr", [P, 2, 512])
        plog, ppos = m.ps(f"{name}_plog", [P, 512]), m.ps(f"{name}_ppos", [P, 512])
        chain, beat = sem("chain"), sem("beat")
        varied, rooted, normed, turned = sem("varied"), sem("rooted"), sem("normed"), sem("turned")
        evac, scored, gapped, powered = sem("evac"), sem("scored"), sem("gapped"), sem("powered")
        counted, placed, slotted, sent = sem("counted"), sem("placed"), sem("slotted"), sem("sent")
        wgot = sem("wgot")
        block = ctx.enter_context(nc.Block())

        @block.sync
        def _(sp):
            for e in range(2):
                load_expert(sp, io, k.w[e], e, wgot)
            sp.wait_ge(wgot, 2 * 16)

        @block.vector
        def _(dve):
            steps = Steps(dve, chain)
            link = steps.done
            dve.memset(seen[0][:], 0.0)
            link(dve.memset(k.count[:], 0.0))

            def statistics(g):
                layernorm_stats(dve, link, stat, mv, [k.x[:, g * GRP + j, :] for j in range(GRP)], varied, beat)

            def normalise(g):
                dve.wait_ge(rooted, g + 1)
                link(dve.reciprocal(rstd[:], std[:]))
                for j in range(GRP):
                    last = dve.tensor_scalar(xn[:, g * GRP + j, :], k.x[:, g * GRP + j, :],
                                             mv[:, j, 0:1], rstd[:, j:j + 1], ALU.subtract, ALU.mult)
                last.then_inc(normed, 1)

            statistics(0)
            normalise(0)
            for g in range(NGRP):
                if g + 1 < NGRP:
                    statistics(g + 1)
                dve.wait_ge(scored, g + 1)
                link(dve.tensor_copy(logit[:].rearrange("p a b -> p (a b)"), plog[:, 0:GRP * E]))
                for j in range(GRP):
                    last = dve.max(top[:, j, :], logit[:, j, :])
                link(last)
                dve.tensor_tensor(gap[:], top[:, :, 1], top[:, :, 0], ALU.subtract).then_inc(gapped, 1)
                for j in range(GRP):
                    last = dve.max_index(index[:, j, :], top[:, j, :], logit[:, j, :])
                link(last)
                link(dve.tensor_copy(idx[:], index[:, :, 0:TOPK]))
                link(dve.tensor_tensor(
                    hot[:], bc(k.const[:, C_IOTA:C_IOTA + E].unsqueeze(1).unsqueeze(1), [P, GRP, TOPK, E]),
                    bc(idx[:].unsqueeze(3), [P, GRP, TOPK, E]), ALU.is_equal))
                dve.sem_inc(counted, 1)
                if g + 1 < NGRP:
                    normalise(g + 1)
                    link(dve.tensor_reduce(more[:], hot[:].rearrange("p a b c -> p (b c) a"), AX.X, ALU.add))
                    link(dve.tensor_tensor(k.count[:], k.count[:], more[:], ALU.add))
                    link(dve.tensor_copy(seen[(g + 1) % 2][:, 0, :], k.count[:]))
                dve.wait_ge(placed, g + 1)
                link(dve.tensor_tensor(prod[:], ppos[:, 0:GRP * TOPK * E].rearrange("p (a b) -> p a b", b=E),
                                       hot[:].rearrange("p a b c -> p (a b) c"), ALU.mult))
                link(dve.tensor_reduce(pos[:].rearrange("p a b -> p (a b)"), prod[:], AX.X, ALU.add))
                dve.tensor_scalar(valid[:], pos[:], float(CAP), None, ALU.is_lt)
                link(dve.scalar_tensor_tensor(place[:], idx[:], float(CAP), pos[:], ALU.mult, ALU.add))
                link(dve.scalar_tensor_tensor(place[:], place[:], -float(SLOTS), valid[:], ALU.add, ALU.mult))
                dve.tensor_scalar(k.slot[:, g * GRP:(g + 1) * GRP, :], place[:], float(SLOTS), None,
                                  ALU.add).then_inc(slotted, 1)
                dve.wait_ge(powered, g + 1)
                link(dve.tensor_scalar(gap[:], ratio[:], 1.0, None, ALU.add))
                link(dve.reciprocal(share[:, :, 0], gap[:]))
                link(dve.tensor_tensor(share[:, :, 1], share[:, :, 0], ratio[:], ALU.mult))
                link(dve.scalar_tensor_tensor(k.share[:, g * GRP:(g + 1) * GRP, :], share[:], 0.5, valid[:],
                                              ALU.mult, ALU.mult))

        @block.scalar
        def _(act):
            def root(g):
                act.wait_ge(varied, g + 1)
                act.activation(std[:], mv[:, :, 1], ACT.Sqrt, bias=k.eps[:, 0:1]).then_inc(rooted, 1)

            root(0)
            for g in range(NGRP):
                for n in range(2):
                    act.wait_ge(turned, g * 2 + n + 1)
                    act.activation(xnT[:, n * 512:n * 512 + 512], ptr[:, n, :], ACT.Copy).then_inc(evac, 1)
                if g + 1 < NGRP:
                    root(g + 1)
                act.wait_ge(gapped, g + 1)
                act.activation(ratio[:], gap[:], ACT.Exp).then_inc(powered, 1)

        @block.tensor
        def _(pe):
            for g in range(NGRP):
                pe.wait_ge(normed, g + 1)
                for n in range(2):
                    for j in range(4):
                        mm = pe.transpose(ptr[:, n, j * P:j * P + P], xn[:, g * GRP + n * 4 + j, :],
                                          k.const[:, C_ID:C_ID + P])
                    mm.then_inc(turned, 1)
                pe.wait_ge(evac, 2 * g + 2)
                for j in range(GRP):
                    mm = pe.matmul(plog[:, j * E:j * E + E], xnT[:, j * P:j * P + P], k.gate[:], start=True, stop=True)
                mm.then_inc(scored, 1)
                pe.wait_ge(counted, g + 1)
                flat = hot[:].rearrange("p a b c -> p a (b c)")
                pe.matmul(ppos[:, 0:GRP * TOPK * E], k.upper[:], flat, start=True, stop=False)
                for j in range(GRP - 1):
                    pe.matmul(ppos[:, (j + 1) * TOPK * E:GRP * TOPK * E], k.ones[:],
                              bc(flat[:, j:j + 1, :], [P, GRP - 1 - j, TOPK * E]), start=False, stop=False)
                pe.matmul(ppos[:, 0:GRP * TOPK * E], k.ones[:], bc(seen[g % 2][:], [P, GRP, TOPK * E]),
                          start=False, stop=True).then_inc(placed, 1)

        @block.gpsimd
        def _(pool):
            for g in range(NGRP):
                pool.wait_ge(slotted, g + 1)
                for j in range(g * GRP, (g + 1) * GRP):
                    scatter(pool, k, io, j, 0, sent)
            pool.wait_ge(sent, 16 * NT)


def load_expert(sp, io, w, e, got):
    sp.dma_start(w[:].rearrange("p a b -> p (a b)"), io.wexp[bass.ds(e * P, P), :]).then_inc(got, 16)


def experts(nc, io, keep, name):
    k = keep
    with ExitStack() as ctx:
        m = Memory(nc, ctx)
        sem = lambda s: m.sem(f"{name}_{s}")
        sb = lambda s, shape, dt=F32: m.sb(f"{name}_{s}", shape, dt)
        w = k.w
        xs = [sb(f"xs{i}", [P, CT, D]) for i in range(2)]
        xhi, xlo = ([sb(f"x{n}{i}", [P, CAP], F32R) for i in range(2)] for n in ("hi", "lo"))
        whi, wlo = ([sb(f"w{n}{i}", [P, 2, F], F32R) for i in range(2)] for n in ("hi", "lo"))
        sg = [sb(f"sg{i}", [P, HALF]) for i in range(2)]
        hid = [sb(f"hid{i}", [P, FT, CAP]) for i in range(2)]
        rows = [sb(f"rows{i}", [P, CT, D]) for i in range(2)]
        pt, po = m.ps(f"{name}_pt", [P, 2, 512]), m.ps(f"{name}_po", [P, 2, 512])
        pg = [m.ps(f"{name}_pg{i}", [P, 512]) for i in range(2)]
        pu = [m.ps(f"{name}_pu{i}", [P, 512]) for i in range(2)]
        wgot = [sem(f"wgot{i}") for i in range(2)]
        xgot = [sem(f"xgot{i}") for i in range(2)]
        beat = sem("beat")
        wfree, hfree = sem("wfree"), sem("hfree")
        turned, evac, gued, silued = sem("turned"), sem("evac"), sem("gued"), sem("silued")
        rounded, split = sem("rounded"), sem("split")
        downed, rready = sem("downed"), sem("rready")
        stored = [[sem(f"stored{c}{i}") for i in range(2)] for c in range(TOPK)]
        sent, fetched = sem("sent"), sem("fetched")
        block = ctx.enter_context(nc.Block())
        NQ = TOPK * E
        NB = 2 * FT
        SPLIT_AT = (4, 6)

        @block.sync
        def _(sp):
            for par in range(2):
                sp.sem_inc(wgot[par], 16)

            def load(c, e, par, weights=True):
                q = c * E + e
                wait_apart(sp, turned, q + 1, beat)
                sp.dma_start(xs[par][:], io.queue[c][bass.ds(e * CAP, CAP), :].rearrange(
                    "(s p) d -> p s d", p=P)).then_inc(xgot[par], 16)
                if weights:
                    wait_apart(sp, wfree, q - 1, beat)
                    load_expert(sp, io, w[par], e, wgot[par])

            def store(c, e, par):
                q = c * E + e
                wait_apart(sp, rready, 2 * q + 4, beat)
                sp.dma_start(io.rows[c][bass.ds(e * CAP, CAP), :].rearrange("(s p) d -> p s d", p=P),
                             rows[par][:]).then_inc(stored[c][par], 16)

            for c in range(TOPK):
                if c:
                    sp.wait_ge(sent, 16 * NT)
                for e in range(2):
                    load(c, e, e, weights=(c > 0))
                    if c:
                        store(c - 1, E - 2 + e, e)
                with sp.Fori(1, E // 2) as ee:
                    for par in range(2):
                        load(c, ee * 2 + par, par)
                        store(c, ee * 2 + par - 2, par)
            for e in range(2):
                store(TOPK - 1, E - 2 + e, e)
            for par in range(2):
                sp.wait_ge(stored[TOPK - 1][par], 16 * E // 2)

        @block.tensor
        def _(pe):
            pe.sem_inc(turned, 2)

            def turn(q, par, half):
                pe.wait_ge(xgot[par], 16 * half)
                for s in range(CT):
                    mm = pe.transpose(pt[:, s // 4, (s % 4) * P:(s % 4) * P + P], xs[par][:, s, :],
                                      k.const[:, C_ID:C_ID + P])
                mm.then_inc(turned, 1)

            def down(par, s):
                for f in range(FT):
                    mm = pe.matmul(po[:, s // 4, (s % 4) * P:(s % 4) * P + P], hid[par][:, f, s * P:s * P + P],
                                   w[par][:, 2, f * P:f * P + P], start=(f == 0), stop=(f == FT - 1))
                return mm

            def queue(q, par, half, follow):
                pe.wait_ge(evac, 2 * q + 2)
                pe.wait_ge(split, 4 * q + 4)
                for c in range(2):
                    for f in range(FT):
                        n = c * FT + f
                        pe.wait_ge(hfree, q * NB + n + 1)
                        cols = slice(c * HALF, c * HALF + HALF)
                        fs = slice(f * P, f * P + P)
                        for i, bank in enumerate((pg, pu)):
                            out = bank[n % 2][:, 0:HALF]
                            pe.matmul(out, whi[par][:, i, fs], xlo[par][:, cols], start=True, stop=False)
                            pe.matmul(out, wlo[par][:, i, fs], xhi[par][:, cols], start=False, stop=False)
                            pe.matmul(out, whi[par][:, i, fs], xhi[par][:, cols], start=False,
                                      stop=True).then_inc(gued, 1)
                if follow is not None:
                    turn(q + 1, 1 - par, follow)
                pe.wait_ge(rready, 2 * q + 2)
                pe.wait_ge(hfree, q * NB + FT + 2)
                for s in range(HALF // P):
                    down(par, s)
                pe.wait_ge(hfree, q * NB + NB + 2)
                for s in range(HALF // P, CT):
                    mm = down(par, s)
                mm.then_inc(downed, 1)

            turn(0, 0, 1)
            with pe.Fori(0, NQ // 2 - 1) as r:
                queue(r * 2, 0, r + 1, r + 1)
                queue(r * 2 + 1, 1, r + 1, r + 2)
            queue(NQ - 2, 0, NQ // 2, NQ // 2)
            queue(NQ - 1, 1, NQ // 2, None)

        @block.scalar
        def _(act):
            def evacuate(q, par):
                act.wait_ge(turned, q + 3)
                act.activation(xhi[par][:, 0:512], pt[:, 0, :], ACT.Copy).then_inc(evac, 1)
                act.activation(xhi[par][:, 512:CAP], pt[:, 1, 0:CAP - 512], ACT.Copy).then_inc(evac, 1)

            def high(par, half, i):
                act.wait_ge(wgot[par], 16 * half)
                act.activation(whi[par][:, i, :], w[par][:, i, :], ACT.Copy).then_inc(rounded, 1)

            def queue(q, par, follow):
                for n in range(NB):
                    act.wait_ge(gued, 2 * (q * NB + n) + 1)
                    act.activation(sg[n % 2][:], pg[n % 2][:, 0:HALF], ACT.Silu).then_inc(silued, 1)
                    if follow is not None and n in SPLIT_AT:
                        high(1 - par, follow, SPLIT_AT.index(n))
                if follow is not None:
                    evacuate(q + 1, 1 - par)

            high(0, 1, 0)
            high(0, 1, 1)
            evacuate(0, 0)
            with act.Fori(0, NQ // 2 - 1) as r:
                queue(r * 2, 0, r + 1)
                queue(r * 2 + 1, 1, r + 2)
            queue(NQ - 2, 0, NQ // 2)
            queue(NQ - 1, 1, None)

        @block.vector
        def _(dve):
            dve.sem_inc(hfree, 2)
            dve.sem_inc(rready, 2)

            def low_weights(q, par, i):
                dve.wait_ge(rounded, 2 * q + i + 1)
                dve.tensor_tensor(wlo[par][:, i, :], w[par][:, i, :], whi[par][:, i, :], ALU.subtract).then_inc(split, 1)

            def low_rows(q, par):
                dve.wait_ge(evac, 2 * q + 1)
                dve.tensor_tensor(xlo[par][:, 0:512], pt[:, 0, :], xhi[par][:, 0:512], ALU.subtract).then_inc(split, 1)
                dve.wait_ge(evac, 2 * q + 2)
                dve.tensor_tensor(xlo[par][:, 512:CAP], pt[:, 1, 0:CAP - 512], xhi[par][:, 512:CAP],
                                  ALU.subtract).then_inc(split, 1)

            def queue(q, par, follow=True):
                for n in range(NB):
                    c, f = n // FT, n % FT
                    dve.wait_ge(silued, q * NB + n + 1)
                    dve.wait_ge(gued, 2 * (q * NB + n) + 2)
                    dve.tensor_tensor(hid[par][:, f, c * HALF:c * HALF + HALF], sg[n % 2][:],
                                      pu[n % 2][:, 0:HALF], ALU.mult).then_inc(hfree, 1)
                    if follow and n in SPLIT_AT:
                        low_weights(q + 1, 1 - par, SPLIT_AT.index(n))
                if follow:
                    low_rows(q + 1, 1 - par)
                dve.wait_ge(downed, q + 1)
                dve.sem_inc(wfree, 1)

            def evacuate(q, par):
                flat = rows[par][:].rearrange("p a b -> p (a b)")
                dve.tensor_copy(flat[:, 0:512], po[:, 0, :]).then_inc(rready, 1)
                dve.tensor_copy(flat[:, 512:CAP], po[:, 1, 0:CAP - 512]).then_inc(rready, 1)

            low_weights(0, 0, 0)
            low_weights(0, 0, 1)
            low_rows(0, 0)
            for c in range(TOPK):
                for e in range(2):
                    queue(c * E + e, e)
                    if c:
                        dve.wait_ge(stored[c - 1][e], 16 * E // 2)
                    evacuate(c * E + e, e)
                last = E // 2 - c
                with dve.Fori(1, last) as r:
                    for par in range(2):
                        q = c * E + r * 2 + par
                        queue(q, par)
                        dve.wait_ge(stored[c][par], r * 16)
                        evacuate(q, par)
            for par in range(2):
                queue(NQ - 2 + par, par, follow=(par == 0))
                dve.wait_ge(stored[TOPK - 1][par], (E // 2 - 1) * 16)
                evacuate(NQ - 2 + par, par)

        @block.gpsimd
        def _(pool):
            for j in range(NT):
                scatter(pool, k, io, j, 1, sent)
            for par in range(2):
                pool.wait_ge(stored[0][par], 16 * E // 2)
            for j in range(NT):
                gather(pool, io, 0, k.slot[:, j, 0:1], k.first[:, j, :], fetched)
            pool.wait_ge(fetched, 16 * NT)


def substitute(eng, link, nmat, inv, prod, first, last):
    for j in range(first, last):
        shape = [P, j + 1, CHUNK - 1 - j]
        part = prod[:, 0:shape[1] * shape[2]].rearrange("p (c i) -> p c i", c=shape[1])
        factor = nmat[:, j + 1:CHUNK, j:j + 1].rearrange("p i j -> p j i")
        link(eng.tensor_tensor(part, bc(inv[:, 0:j + 1, j:j + 1], shape), bc(factor, shape), ALU.mult))
        rest = inv[:, 0:j + 1, j + 1:CHUNK]
        link(eng.tensor_tensor(rest, rest, part, ALU.add))


def project(nc, io, keep):
    k = keep
    G = TPP * H
    with ExitStack() as ctx:
        m = Memory(nc, ctx)
        sem, sb = m.sem, m.sb
        slots = [sb(f"slots{i}", [P, TPP], U32) for i in range(2)]
        got = [sb(f"got{i}", [P, TPP, D]) for i in range(2)]
        stat, mv = sb("stat", [P, TPP, 6]), sb("mv", [P, TPP, 2])
        std, rstd = sb("std", [P, TPP]), sb("rstd", [P, TPP])
        xn = sb("pxn", [P, PT])
        xnT = sb("xnT", [P, 2, PAD + SEQ])
        qkv = sb("qkv", [P, TPP, 3 * D])
        tanhb, beta = sb("tanhb", [P, G]), sb("beta", [P, G])
        sq, ss = sb("sq", [P, TPP, 2 * D]), sb("ss", [P, 2 * G])
        rn = sb("rn", [P, 2 * G])
        qk = sb("qk", [P, TPP, 2 * D])
        kq = sb("kq", [P, 2, PT])
        vpad = [sb(f"vpad{i}", [P, 2, LAGS - 1 + SEQ]) for i in range(2)]
        kb, vb = sb("kb", [P, PT]), sb("vb", [P, PT])
        low, loc = sb("low", [P, G, CHUNK]), sb("loc", [P, G, CHUNK])
        nmat = sb("nmat", [P, CHUNK, CHUNK])
        inv = sb("inv", [P, CHUNK, CHUNK])
        prod = sb("prod", [P, CHUNK * CHUNK])
        px, pk, pv = (m.ps(f"pp{i}", [P, 512]) for i in range(3))
        pq = px
        pm = m.ps("pm", [P, 512])
        pa = m.ps("pa", [P, 4, 512])
        chain, beat = sem("chain"), sem("beat")
        gathered = [sem(f"gathered{i}") for i in range(2)]
        indexed, varied = sem("indexed"), sem("varied")
        rooted, normed, turned, evac = sem("rooted"), sem("normed"), sem("turned"), sem("evac")
        projected, silued, squared, summed = sem("projected"), sem("silued"), sem("squared"), sem("summed")
        lengths, scaled, turned3, moved = sem("lengths"), sem("scaled"), sem("turned3"), sem("moved")
        grammed, masked, weighted, saved = sem("grammed"), sem("masked"), sem("weighted"), sem("saved")
        padded, room, unmasked, factors = sem("padded"), sem("room"), sem("unmasked"), sem("factors")
        convolved, kept = sem("convolved"), sem("kept")
        ngot, inverted, istored, nsaved = sem("ngot"), sem("inverted"), sem("istored"), sem("nsaved")
        block = ctx.enter_context(nc.Block())
        NSAVE = 8
        NG = NPAIR // 2
        SPLIT = 15
        MS_AT = (0, 24, 29, 34, 50, MS)

        @block.gpsimd
        def _(pool):
            def collect_second(t, par):
                wait_apart(pool, indexed, t + 1, beat)
                for j in range(TPP):
                    gather(pool, io, 1, slots[par][:, j:j + 1], got[par][:, j, :], gathered[par])

            def weigh(t):
                pool.wait_ge(masked, t + 1)
                pool.tensor_tensor(low[:], low[:], bc(beta[:].unsqueeze(2), [P, G, CHUNK]),
                                   ALU.mult).then_inc(weighted, 1)

            collect_second(0, 0)
            with pool.Fori(0, NPAIR // 2 - 1) as r:
                for par in range(2):
                    collect_second(r * 2 + par + 1, 1 - par)
                    weigh(r * 2 + par)
            collect_second(NPAIR - 1, 1)
            weigh(NPAIR - 2)
            weigh(NPAIR - 1)

        @block.vector
        def _(dve):
            def index(t, par):
                return dve.tensor_copy(slots[par][:].rearrange("p (a b) -> p a b", b=1),
                                       k.slot[:, bass.ds(t * TPP, TPP), 1:2])

            def invert_part(link, r, par):
                if par == 0:
                    dve.wait_ge(ngot, r * 16)
                    dve.wait_ge(istored, r * 16)
                    link(dve.tensor_copy(inv[:].rearrange("p a b -> p (a b)"), k.const[:, C_EYE:C_END]))
                    substitute(dve, link, nmat, inv, prod, 0, SPLIT)
                else:
                    substitute(dve, link, nmat, inv, prod, SPLIT, CHUNK - 1)
                    dve.sem_inc(inverted, 1)

            def normalise(link, r, par):
                t = r * 2 + par
                dve.wait_ge(gathered[par], (r + 1) * 16 * TPP)
                tile = lambda j: k.x[:, bass.ds(t * TPP + j, 1), :].rearrange("p a d -> p (a d)")
                index(t + 2, par)
                for c in range(TOPK):
                    for j in range(TPP):
                        row = k.first[:, bass.ds(t * TPP + j, 1), :].rearrange("p a d -> p (a d)") if c == 0 \
                            else got[par][:, j, :]
                        last = dve.scalar_tensor_tensor(tile(j), row, k.share[:, bass.ds(t * TPP + j, 1), c], tile(j),
                                                        ALU.mult, ALU.add)
                    link(last)
                dve.sem_inc(indexed, 1)
                layernorm_stats(dve, link, stat, mv, [tile(j) for j in range(TPP)], varied, beat)
                dve.wait_ge(rooted, t + 1)
                link(dve.reciprocal(rstd[:], std[:]))
                for j in range(TPP):
                    last = dve.tensor_scalar(xn[:, j * D:j * D + D], tile(j), mv[:, j, 0:1], rstd[:, j:j + 1],
                                             ALU.subtract, ALU.mult)
                last.then_inc(normed, 1)

            def pair(link, r, par, invert, ahead=True):
                t = r * 2 + par
                if invert:
                    invert_part(link, r, par)
                dve.wait_ge(squared, t + 1)
                dve.tensor_reduce(ss[:], sq[:].rearrange("p a (b c) -> p (a b) c", c=DH), AX.X,
                                  ALU.add).then_inc(summed, 1)
                dve.wait_ge(room, t + 1)
                link(dve.tensor_scalar(beta[:], tanhb[:], 0.5, 0.5, ALU.mult, ALU.add))
                dve.wait_ge(lengths, t + 1)
                link(dve.reciprocal(rn[:], rn[:]))
                for half in (1, 0):
                    part = slice(half * D, half * D + D)
                    dve.tensor_tensor(qk[:, :, part].rearrange("p a (b c) -> p a b c", c=DH),
                                      qkv[:, :, part].rearrange("p a (b c) -> p a b c", c=DH),
                                      bc(rn[:].rearrange("p (a b) -> p a b", a=TPP)[:, :, half * H:half * H + H]
                                         .unsqueeze(3), [P, TPP, H, DH]), ALU.mult).then_inc(scaled, 1)
                dve.wait_ge(turned3, 3 * t + 1)
                dve.tensor_copy(vpad[par][:, :, LAGS - 1:], pv[:].rearrange("p (b c) -> p b c", b=2)).then_inc(moved, 1)
                dve.wait_ge(turned3, 3 * t + 2)
                dve.tensor_copy(kq[:, 0, :], pk[:]).then_inc(moved, 1)
                dve.wait_ge(scaled, 2 * t + 2)
                b3 = bc(beta[:].rearrange("p (a b) -> p a b", a=TPP).unsqueeze(3), [P, TPP, H, DH])
                heads = lambda ap: ap.rearrange("p a (b c) -> p a b c", c=DH)
                dve.tensor_tensor(kb[:].rearrange("p (a b c) -> p a b c", a=TPP, c=DH),
                                  heads(qk[:, :, D:2 * D]), b3, ALU.mult).then_inc(factors, 1)
                dve.tensor_tensor(vb[:].rearrange("p (a b c) -> p a b c", a=TPP, c=DH),
                                  heads(qkv[:, :, 2 * D:3 * D]), b3, ALU.mult).then_inc(factors, 1)
                if ahead:
                    normalise(link, r + par, 1 - par)
                dve.wait_ge(grammed, t + 1)
                gram = lambda i: pa[:, :, 0:TPP * 2 * CHUNK].rearrange(
                    "p h (a g c) -> p h a g c", a=TPP, g=2)[:, :, :, i, :]
                mask = lambda c: bc(k.const[:, c:c + CHUNK].unsqueeze(1).unsqueeze(1), [P, H, TPP, CHUNK])
                to = lambda ap: ap.rearrange("p (a h) c -> p h a c", h=H)
                dve.tensor_tensor(to(low[:]), gram(0), mask(C_NEG), ALU.mult).then_inc(masked, 1)
                link(dve.tensor_tensor(to(loc[:]), gram(1), mask(C_INC), ALU.mult))
                dve.sem_inc(factors, 1)
                dve.sem_inc(unmasked, 1)

            for par in range(2):
                index(par, par).then_inc(indexed, 1)
            dve.memset(xnT[:, :, 0:PAD], 0.0).then_inc(padded, 1)
            for par in range(2):
                dve.memset(vpad[par][:, :, 0:LAGS - 1], 0.0).then_inc(padded, 1)
            steps = Steps(dve, chain)
            normalise(steps.done, 0, 0)
            for par in range(2):
                pair(steps.done, 0, par, False)
            FIRST, LINKS = 18, 77
            assert steps.n == FIRST, steps.n
            with dve.Fori(1, NG - 1) as r:
                steps = Steps(dve, chain, FIRST + (r - 1) * LINKS)
                for par in range(2):
                    pair(steps.done, r, par, True)
                assert steps.n == LINKS, steps.n
            steps = Steps(dve, chain, FIRST + (NG - 2) * LINKS)
            for par in range(2):
                pair(steps.done, NG - 1, par, True, ahead=(par == 0))

        @block.scalar
        def _(act):
            def keep_ms(t):
                act.wait_ge(convolved, t + 1)
                act.activation(k.ms[:, bass.ds(t * TPP, TPP // 2), :].rearrange("p a b -> p (a b)"), pm[:, 0:SEQ],
                               ACT.Copy).then_inc(kept, 1)

            def root(t):
                act.wait_ge(varied, t + 1)
                act.activation(std[:], mv[:, :, 1], ACT.Sqrt, bias=k.eps[:, 0:1]).then_inc(rooted, 1)

            def pair(t):
                act.wait_ge(turned, t + 1)
                act.wait_ge(room, t + 1)
                act.activation(xnT[:, :, PAD:], px[:].rearrange("p (b c) -> p b c", b=2), ACT.Copy).then_inc(evac, 1)
                for j in range(TPP):
                    act.wait_ge(projected, t * TPP + j + 1)
                    act.activation(qkv[:, j, :], pa[:, j, 0:3 * D], ACT.Silu)
                    act.activation(tanhb[:, j * H:j * H + H], pa[:, j, 3 * D:3 * D + H], ACT.Tanh,
                                   scale=0.5).then_inc(silued, 1)
                act.wait_ge(silued, (t + 1) * TPP)
                act.activation(sq[:], qkv[:, :, 0:2 * D], ACT.Square).then_inc(squared, 1)
                act.wait_ge(summed, t + 1)
                act.activation(rn[:], ss[:], ACT.Sqrt, bias=k.eps[:, 1:2]).then_inc(lengths, 1)
                act.wait_ge(turned3, 3 * t + 3)
                act.activation(kq[:, 1, :], pq[:], ACT.Copy).then_inc(moved, 1)

            act.wait_ge(padded, 3)
            act.sem_inc(kept, 1)
            root(0)
            pair(0)
            root(1)
            with act.Fori(1, NPAIR - 1) as t:
                pair(t)
                root(t + 1)
                keep_ms(t - 1)
            pair(NPAIR - 1)
            for t in (NPAIR - 2, NPAIR - 1):
                keep_ms(t)

        @block.tensor
        def _(pe):
            ident = k.const[:, C_ID:C_ID + P]

            def convolve(t, par, part):
                if part == 0:
                    pe.wait_ge(kept, t + 1)
                for i in range(MS_AT[part], MS_AT[part + 1]):
                    j, lag = i // LAGS, i % LAGS
                    at = LAGS - 1 - lag + j * P
                    mm = pe.matmul(pm[:, j * P:j * P + P], vpad[par][:, 0, at:at + P], k.lag[:, lag, :],
                                   start=(lag == 0), stop=(lag == LAGS - 1))
                if part == len(MS_AT) - 2:
                    mm.then_inc(convolved, 1)

            def pair(t, par, before):
                fill = (lambda part: convolve(t - 1, 1 - par, part)) if before else (lambda part: None)
                fill(0)
                pe.wait_ge(normed, t + 1)
                for j in range(TPP):
                    mm = pe.transpose(px[:, j * P:j * P + P], xn[:, j * D:j * D + D], ident)
                mm.then_inc(turned, 1)
                fill(1)
                pe.wait_ge(evac, t + 1)
                pe.wait_ge(unmasked, t + 1)
                for j in range(TPP):
                    at = (j % 2) * P
                    for tap in range(TAPS):
                        pe.matmul(pa[:, j, 0:3 * D], xnT[:, j // 2, at + tap:at + tap + P], k.wtap[:, tap, :],
                                  start=(tap == 0), stop=(tap == TAPS - 1))
                    pe.matmul(pa[:, j, 3 * D:3 * D + H], xnT[:, j // 2, at + PAD:at + PAD + P], k.wb[:],
                              start=True, stop=True).then_inc(projected, 1)
                fill(2)
                pe.wait_ge(silued, (t + 1) * TPP)
                for j in range(TPP):
                    mm = pe.transpose(pv[:, j * P:j * P + P], qkv[:, j, 2 * D:3 * D], ident)
                mm.then_inc(turned3, 1)
                fill(3)
                for half, bank in ((1, pk), (0, pq)):
                    pe.wait_ge(scaled, 2 * t + 2 - half)
                    for j in range(TPP):
                        mm = pe.transpose(bank[:, j * P:j * P + P], qk[:, j, half * D:half * D + D], ident)
                    mm.then_inc(turned3, 1)
                fill(4)
                wait_apart(pe, moved, 3 * (t + 1), beat)
                for j in range(TPP):
                    for n in range(QC):
                        at = j * P + n * CHUNK
                        for h in range(H):
                            rows = slice(h * DH, h * DH + DH)
                            mm = pe.matmul(pa[n * CHUNK:n * CHUNK + CHUNK, h, j * 64:j * 64 + 64],
                                           kq[rows, 0, at:at + CHUNK], kq[rows, :, at:at + CHUNK],
                                           start=True, stop=True)
                mm.then_inc(grammed, 1)

            pe.sem_inc(unmasked, 1)
            pair(0, 0, False)
            pair(1, 1, True)
            with pe.Fori(1, NG) as r:
                pair(r * 2, 0, True)
                pair(r * 2 + 1, 1, True)
            for part in range(len(MS_AT) - 1):
                convolve(NPAIR - 1, 1, part)

        @block.sync
        def _(sp):
            def save(t, field, src):
                dst = io.pair[bass.ds(t * P, P), field * PT:field * PT + PT]
                if len(src.shape) == 3:
                    dst = dst.rearrange("p (a b) -> p a b", a=src.shape[1])
                sp.dma_start(dst, src).then_inc(saved, 16)

            def pair(t, par):
                wait_apart(sp, evac, t + 1, beat)
                save(t, 6, xnT[:, :, PAD:])
                wait_apart(sp, silued, (t + 1) * TPP, beat)
                save(t, 2, qkv[:, :, 2 * D:3 * D])
                wait_apart(sp, scaled, 2 * (t + 1), beat)
                save(t, 1, qk[:, :, D:2 * D])
                wait_apart(sp, moved, 3 * (t + 1), beat)
                save(t, 0, kq[:, 1, :])
                sp.dma_start(io.pair[bass.ds(t * P, P), 7 * PT:7 * PT + SEQ],
                             vpad[par][:, 1, LAGS - 1:]).then_inc(saved, 16)
                wait_apart(sp, factors, 3 * (t + 1), beat)
                save(t, 3, kb[:])
                save(t, 4, vb[:])
                save(t, 5, loc[:].rearrange("p a b -> p (a b)"))
                wait_apart(sp, weighted, t + 1, beat)
                for n in range(QC):
                    dst = io.low[bass.ds((t * QC + n) * G, G), :].rearrange("g (c e) -> c g e", e=CHUNK)
                    sp.dma_start(dst, low[n * CHUNK:n * CHUNK + CHUNK, :, :]).then_inc(nsaved, 16)
                wait_apart(sp, nsaved, (t + 1) * 16 * QC, beat)
                wait_apart(sp, saved, (t + 1) * 16 * NSAVE, beat)
                sp.sem_inc(room, 1)

            def reload(r):
                sp.dma_start(nmat[:].rearrange("p a b -> p (a b)"), io.low[bass.ds(r * P, P), :]).then_inc(ngot, 16)

            def store(r):
                wait_apart(sp, inverted, r + 1, beat)
                sp.dma_start(io.inv[bass.ds(r * P, P), :], inv[:].rearrange("p a b -> p (a b)")).then_inc(istored, 16)

            sp.sem_inc(room, 1)
            sp.sem_inc(istored, 16)
            for par in range(2):
                pair(par, par)
            with sp.Fori(1, NG) as r:
                reload(r - 1)
                for par in range(2):
                    pair(r * 2 + par, par)
                store(r - 1)
            sp.wait_ge(istored, 16 * NG)


class Fill:

    def __init__(self, solve, scan, start, logits, read, update):
        self.solve, self.scan, self.start, self.logits, self.read, self.update = solve, scan, start, logits, read, update


def attend(nc, io, keep):
    k = keep
    G = TPP * H
    with ExitStack() as ctx:
        m = Memory(nc, ctx)
        sem, sb = m.sem, m.sb
        nmat, tinv = sb("a_nmat", [P, CHUNK, CHUNK]), sb("a_tinv", [P, CHUNK, CHUNK])
        prod = sb("a_prod", [P, CHUNK * CHUNK])
        qT, kn, kb, vb = (sb(f"a_{n}", [P, PT]) for n in ("qT", "kn", "kb", "vb"))
        loc, inv = sb("a_loc", [P, G, CHUNK]), sb("a_inv", [P, G, CHUNK])
        v, xnT = sb("a_v", [P, TPP, D]), sb("a_xnT", [P, PT])
        vpad = sb("a_vpad", [P, LAGS - 1 + SEQ])
        u, wT = sb("u", [P, TPP, D]), sb("wT", [P, PT])
        state = [[sb(f"state{b}{i}", [P, D]) for i in range(3)] for b in range(2)]
        delta = sb("delta", [P, TPP, D])
        mean = sb("mean", [P, TPP, NOUT])
        meanT = sb("meanT", [NOUT, PT])
        hdn = sb("hdn", [P, 2, PT])
        lg, top = sb("lg", [P, G, 3]), sb("ltop", [P, G])
        mix, part = sb("mix", [P, TPP, D]), sb("part", [P, TPP, D])
        sq, ss, rs = sb("osq", [P, TPP, D]), sb("oss", [P, G]), sb("ors", [P, G])
        oT = sb("oT", [P, PT])
        pm = m.ps("a_pm", [P, 512])
        pw = m.ps("a_pw", [P, 4, 512])
        po = m.ps("a_po", [P, 512])
        pf, pg = m.ps("a_pf", [P, 512]), m.ps("a_pg", [P, 512])
        pread, pstate = [pw[:, i, :] for i in range(2)], [pw[:, 2 + i, :] for i in range(2)]
        chain, rowchain, beat = sem("achain"), sem("rowchain"), sem("abeat")
        solvegot, scangot, gategot = sem("solvegot"), sem("scangot"), sem("gategot")
        solved, taken = sem("solved"), sem("taken")
        ngot, istored = sem("angot"), sem("aistored")
        padded, convolved = sem("apadded"), sem("aconvolved")
        reads, subbed, updated, stated = ([sem(f"{n}{i}") for i in range(2)]
                                          for n in ("reads", "subbed", "updated", "stated"))
        out, outed = sem("out"), sem("outed")
        meaned, meanturned, meankept = sem("meaned"), sem("meanturned"), sem("meankept")
        hidden, gelued, gated, lowered, powered = (sem("hidden"), sem("gelued"), sem("gated"), sem("lowered"),
                                                   sem("lpowered"))
        mixed, squared, summed, rooted = sem("omixed"), sem("osquared"), sem("osummed"), sem("orooted")
        scaled, oturned, okept, done, added = sem("oscaled"), sem("oturned"), sem("okept"), sem("done"), sem("added")
        block = ctx.enter_context(nc.Block())
        SOLVELOADS, SCANLOADS, GATELOADS = 2 + QC, 4, 2
        LINKS = 10
        LAST = NPAIR // 2 - 1
        FILL = Fill(solve=(14, 3, 3), scan=3, start=3, logits=2, read=2, update=2)

        @block.sync
        def _(sp):
            def load(t, dst, field, got):
                sp.dma_start(dst, io.pair[bass.ds(t * P, P), field * PT:field * PT + PT]).then_inc(got, 16)

            def load_solve(t):
                load(t, kb[:], 3, solvegot)
                load(t, vb[:], 4, solvegot)
                for n in range(QC):
                    src = io.inv[bass.ds((t * QC + n) * G, G), :].rearrange("g (e c) -> e g c", c=CHUNK)
                    sp.dma_start(inv[n * CHUNK:n * CHUNK + CHUNK, :, :], src).then_inc(solvegot, 16)

            def load_scan(t):
                load(t, qT[:], 0, scangot)
                load(t, kn[:], 1, scangot)
                load(t, loc[:].rearrange("p a b -> p (a b)"), 5, scangot)
                sp.dma_start(vpad[:, LAGS - 1:], io.pair[bass.ds(t * P, P), 7 * PT:7 * PT + SEQ]).then_inc(scangot, 16)

            def load_gate(t):
                wait_apart(sp, mixed, t + 1, beat)
                load(t, v[:].rearrange("p a b -> p (a b)"), 2, gategot)
                load(t, xnT[:], 6, gategot)

            sp.sem_inc(mixed, 1)
            sp.dma_start(nmat[:].rearrange("p a b -> p (a b)"), io.low[LAST * P:LAST * P + P, :]).then_inc(ngot, 16)
            load_solve(0)
            load_scan(0)
            for first, last in ((1, 2 * LAST), (2 * LAST, NPAIR)):
                with sp.Fori(first, last) as t:
                    wait_apart(sp, solved, t, beat)
                    load_solve(t)
                    load_gate(t - 1)
                    wait_apart(sp, out, t, beat)
                    load_scan(t)
                if first == 1:
                    sp.wait_ge(istored, 16)
            load_gate(NPAIR - 1)

        @block.gpsimd
        def _(pool):
            pool.wait_ge(ngot, 16)
            steps = Steps(pool, rowchain)
            steps.done(pool.tensor_copy(tinv[:].rearrange("p a b -> p (a b)"), k.const[:, C_EYE:C_END]))
            substitute(pool, steps.done, nmat, tinv, prod, 0, CHUNK - 1)
            pool.dma_start(io.inv[LAST * P:LAST * P + P, :], tinv[:].rearrange("p a b -> p (a b)")).then_inc(istored, 16)

        @block.tensor
        def _(pe):
            ident = k.const[:, C_ID:C_ID + P]

            def solve(j):
                for n in range(QC):
                    rows = slice(n * CHUNK, n * CHUNK + CHUNK)
                    for h in range(H):
                        g, at = j * H + h, j * D + h * DH
                        pe.matmul(po[rows, at:at + DH], inv[rows, g, :], vb[rows, at:at + DH], start=True, stop=True)
                        mm = pe.matmul(pw[h * DH:h * DH + DH, n, j * CHUNK:j * CHUNK + CHUNK],
                                       kb[rows, at:at + DH], inv[rows, g, :], start=True, stop=True)
                return mm

            def outputs(n, b):
                j, rows = 2 * b + n // QC, slice(n % QC * CHUNK, n % QC * CHUNK + CHUNK)
                if n:
                    at = j * P + n % QC * CHUNK
                    pe.matmul(po[rows, j * D:j * D + D], qT[:, at:at + CHUNK], state[b][n % 3][:],
                              start=True, stop=False, skip_group_check=True)
                for h in range(H):
                    col = j * D + h * DH
                    mm = pe.matmul(po[rows, col:col + DH], loc[rows, j * H + h, :],
                                   u[rows, j, h * DH:h * DH + DH], start=(n == 0), stop=True,
                                   skip_group_check=True)
                return mm

            def convolve(first, count):
                for i in range(first, min(first + count, MS)):
                    j, lag = i // LAGS, i % LAGS
                    at = LAGS - 1 - lag + j * P
                    mm = pe.matmul(pm[:, j * P:j * P + P], vpad[:, at:at + P], k.lag[:, lag, :],
                                   start=(lag == 0), stop=(lag == LAGS - 1))
                    if i == MS - 1:
                        mm.then_inc(convolved, 1)
                return min(first + count, MS)

            def step(t, n, at):
                j0, rows = n // QC, slice(n % QC * CHUNK, n % QC * CHUNK + CHUNK)
                for b in range(2):
                    j = 2 * b + j0
                    col = j * P + n % QC * CHUNK
                    if n:
                        pe.wait_ge(stated[b], t * (NCH - 1) + n)
                        pe.matmul(pread[b][rows, 0:D], wT[:, col:col + CHUNK], state[b][n % 3][:],
                                  start=True, stop=True).then_inc(reads[b], 1)
                if n:
                    outputs(n - 1, 0)
                    at = convolve(at, FILL.read)
                for b in range(2):
                    j = 2 * b + j0
                    if n:
                        wait_apart(pe, subbed[b], t * (NCH - 1) + n, beat)
                    if n < NCH - 1:
                        pe.matmul(pstate[b][:, 0:D], kn[rows, j * D:j * D + D], u[rows, j, :],
                                  start=(n == 0), stop=True, skip_group_check=True).then_inc(updated[b], 1)
                if n:
                    outputs(n - 1, 1)
                at = convolve(at, FILL.start if n == 0 else FILL.update if n < NCH - 1 else MS)
                if n == NCH - 1:
                    outputs(n, 0)
                    outputs(n, 1).then_inc(out, 1)
                return at

            def turn_means(q):
                pe.wait_ge(meaned, q + 1)
                for j in range(TPP):
                    mm = pe.transpose(pf[0:NOUT, j * P:j * P + P], mean[:, j, :], ident)
                mm.then_inc(meanturned, 1)

            def hide(q):
                pe.wait_ge(meankept, q + 1)
                pe.wait_ge(gategot, (q + 1) * 16 * GATELOADS)
                for f, bank in enumerate((pf, pg)):
                    if f:
                        pe.wait_ge(added, q + 1)
                    pe.matmul(bank[:], k.w1[:, f * P:f * P + P], xnT[:], start=True, stop=False)
                    pe.matmul(bank[:], k.w1s[:, f * P:f * P + P], meanT[:], start=False,
                              stop=True).then_inc(hidden, 1)

            def logits(q, at):
                pe.wait_ge(gelued, 2 * (q + 1))
                for j in range(TPP):
                    at = convolve(at, FILL.logits)
                    for f in range(2):
                        mm = pe.matmul(pf[:, j * NOUT:j * NOUT + NOUT], hdn[:, f, j * P:j * P + P], k.w2[:, f, :],
                                       start=(f == 0), stop=(f == 1))
                mm.then_inc(gated, 1)
                return at

            def turn_mixture(q):
                pe.wait_ge(scaled, q + 1)
                for j in range(TPP):
                    mm = pe.transpose(pg[:, j * P:j * P + P], mix[:, j, :], ident)
                mm.then_inc(oturned, 1)

            def output(q):
                pe.wait_ge(okept, q + 1)
                for j in range(TPP):
                    mm = pe.matmul(pg[:, j * P:j * P + P], oT[:, j * P:j * P + P], k.wout[:], start=True, stop=True)
                mm.then_inc(done, 1)

            def stage(t, gate, finish):
                pe.wait_ge(solvegot, (t + 1) * 16 * SOLVELOADS)
                wait_apart(pe, outed, 2 * t + 1, beat)
                solve(0)
                if finish:
                    output(t - 2)
                if gate:
                    turn_means(t - 1)
                pe.wait_ge(scangot, (t + 1) * 16 * SCANLOADS)
                wait_apart(pe, outed, 2 * t + 2, beat)
                solve(1)
                at = convolve(0, FILL.solve[0])
                solve(2)
                at = convolve(at, FILL.solve[1])
                solve(3).then_inc(solved, 1)
                at = convolve(at, FILL.solve[2])
                if gate:
                    hide(t - 1)
                at = convolve(at, FILL.scan)
                pe.wait_ge(taken, 2 * (t + 1))
                at = step(t, 1, step(t, 0, at))
                if gate:
                    at = logits(t - 1, at)
                for n in range(2, NCH):
                    at = step(t, n, at)
                assert at == MS
                if gate:
                    turn_mixture(t - 1)

            pe.sem_inc(added, 1)
            pe.sem_inc(outed, 2)
            pe.wait_ge(padded, 1)
            stage(0, False, False)
            stage(1, True, False)
            with pe.Fori(2, NPAIR) as t:
                stage(t, True, True)
            output(NPAIR - 2)
            turn_means(NPAIR - 1)
            hide(NPAIR - 1)
            logits(NPAIR - 1, MS)
            turn_mixture(NPAIR - 1)
            output(NPAIR - 1)

        @block.vector
        def _(dve):
            heads = lambda ap: ap.rearrange("p a (b c) -> p (a b) c", c=DH)
            weight = lambda i: bc(lg[:, :, i:i + 1], [P, G, DH])
            ms = lambda q: k.ms[:, bass.ds(q * TPP, TPP), :]

            def means(q):
                dve.wait_ge(outed, 2 * q + 4)
                dve.wait_ge(gategot, (q + 1) * 16 * GATELOADS)
                for i, src in enumerate((ms(q), delta[:], v[:])):
                    last = dve.tensor_reduce(mean[:, :, i * H:i * H + H],
                                             src.rearrange("p a (b c) -> p a b c", c=DH), AX.X, ALU.add,
                                             apply_absolute_value=True)
                last.then_inc(meaned, 1)

            def add_output(q):
                dve.wait_ge(done, q + 1)
                x = k.x[:, bass.ds(q * TPP, TPP), :].rearrange("p a b -> p (a b)")
                dve.tensor_tensor(x, x, pg[:], ALU.add).then_inc(added, 1)

            def lower(q, link):
                dve.wait_ge(gated, q + 1)
                link(dve.tensor_tensor(lg[:].rearrange("p (a h) b -> p a (h b)", a=TPP),
                                       pf[:, 0:TPP * NOUT].rearrange("p (a b) -> p a b", a=TPP),
                                       bc(k.b2[:].unsqueeze(1), [P, TPP, NOUT]), ALU.add))
                link(dve.tensor_reduce(top[:], lg[:], AX.X, ALU.max))
                dve.tensor_tensor(lg[:], lg[:], bc(top[:].unsqueeze(2), [P, G, 3]), ALU.subtract).then_inc(lowered, 1)

            def weights(q, link):
                dve.wait_ge(powered, q + 1)
                link(dve.tensor_reduce(top[:], lg[:], AX.X, ALU.add))
                link(dve.reciprocal(top[:], top[:]))
                link(dve.tensor_tensor(lg[:], lg[:], bc(top[:].unsqueeze(2), [P, G, 3]), ALU.mult))

            def mix_first(q, link):
                dve.tensor_tensor(heads(mix[:]), heads(ms(q)), weight(0), ALU.mult)
                link(dve.tensor_tensor(heads(part[:]), heads(delta[:]), weight(1), ALU.mult))

            def mix_second(q, link):
                link(dve.tensor_tensor(mix[:], mix[:], part[:], ALU.add))
                link(dve.tensor_tensor(heads(part[:]), heads(v[:]), weight(2), ALU.mult))

            def mix_third(q, link):
                link(dve.tensor_tensor(mix[:], mix[:], part[:], ALU.add))
                dve.sem_inc(mixed, 1)

            def squares(q, link):
                dve.wait_ge(squared, q + 1)
                dve.tensor_reduce(ss[:], heads(sq[:]), AX.X, ALU.add).then_inc(summed, 1)

            def scale(q, link):
                dve.wait_ge(rooted, q + 1)
                link(dve.reciprocal(rs[:], rs[:]))
                dve.tensor_tensor(heads(mix[:]), heads(mix[:]), bc(rs[:].unsqueeze(2), [P, G, DH]),
                                  ALU.mult).then_inc(scaled, 1)

            gate_parts = ((1, lower), (2, weights), (3, mix_first), (4, mix_second), (5, mix_third), (6, squares),
                          (7, scale))

            def step(t, n):
                j0, rows = n // QC, slice(n % QC * CHUNK, n % QC * CHUNK + CHUNK)
                for b in range(2):
                    if n:
                        dve.wait_ge(reads[b], t * (NCH - 1) + n)
                        dve.tensor_tensor(u[rows, 2 * b + j0, :], u[rows, 2 * b + j0, :], pread[b][rows, 0:D],
                                          ALU.subtract).then_inc(subbed[b], 1)
                for b in range(2):
                    if n < NCH - 1:
                        dve.wait_ge(updated[b], t * (NCH - 1) + n + 1)
                        dve.tensor_tensor(state[b][(n + 1) % 3][:], pstate[b][:, 0:D], k.const[:, C_HEAD:C_HEAD + P],
                                          ALU.mult).then_inc(stated[b], 1)

            def stage(t, gate, finish):
                if gate:
                    means(t - 1)
                if finish:
                    add_output(t - 2)
                dve.wait_ge(solved, t + 1)
                dve.tensor_copy(wT[:].rearrange("p (a n c) -> p n a c", a=TPP, n=QC),
                                pw[:, :, 0:TPP * CHUNK].rearrange("p n (a c) -> p n a c", a=TPP)).then_inc(taken, 1)
                dve.wait_ge(taken, 2 * (t + 1))
                steps = Steps(dve, chain, (t - 1) * LINKS)
                for n in range(NCH):
                    step(t, n)
                    for after, part_of in gate_parts:
                        if gate and after == n:
                            part_of(t - 1, steps.done)
                assert steps.n == (LINKS if gate else 0), steps.n

            dve.memset(vpad[:, 0:LAGS - 1], 0.0).then_inc(padded, 1)
            stage(0, False, False)
            stage(1, True, False)
            with dve.Fori(2, NPAIR) as t:
                stage(t, True, True)
            means(NPAIR - 1)
            add_output(NPAIR - 2)
            steps = Steps(dve, chain, (NPAIR - 1) * LINKS)
            for _, part_of in gate_parts:
                part_of(NPAIR - 1, steps.done)
            add_output(NPAIR - 1)

        @block.scalar
        def _(act):
            def keep_means(q):
                act.wait_ge(meanturned, q + 1)
                act.activation(meanT[:], pf[0:NOUT, :], ACT.Copy, scale=1.0 / DH).then_inc(meankept, 1)

            def gate(q):
                for f, bank in enumerate((pf, pg)):
                    act.wait_ge(hidden, q * 2 + f + 1)
                    act.activation(hdn[:, f, :], bank[:], ACT.Gelu, bias=k.b1[:, f:f + 1]).then_inc(gelued, 1)
                act.wait_ge(lowered, q + 1)
                act.activation(lg[:], lg[:], ACT.Exp).then_inc(powered, 1)
                act.wait_ge(mixed, q + 2)
                act.activation(sq[:], mix[:], ACT.Square).then_inc(squared, 1)
                act.wait_ge(summed, q + 1)
                act.activation(rs[:], ss[:], ACT.Sqrt, bias=k.eps[:, 2:3], scale=1.0 / DH).then_inc(rooted, 1)
                act.wait_ge(oturned, q + 1)
                act.activation(oT[:], pg[:], ACT.Copy).then_inc(okept, 1)

            def stage(t, with_gate):
                if with_gate:
                    keep_means(t - 1)
                act.wait_ge(solved, t + 1)
                act.activation(u[:].rearrange("p a b -> p (a b)"), po[:], ACT.Copy).then_inc(taken, 1)
                if with_gate:
                    gate(t - 1)
                act.wait_ge(out, t + 1)
                act.activation(delta[:].rearrange("p a b -> p (a b)"), po[:], ACT.Copy).then_inc(outed, 1)
                act.wait_ge(convolved, t + 1)
                act.activation(k.ms[:, bass.ds(t * TPP + 2, 2), :].rearrange("p a b -> p (a b)"), pm[:, 0:SEQ],
                               ACT.Copy).then_inc(outed, 1)

            stage(0, False)
            with act.Fori(1, NPAIR) as t:
                stage(t, True)
            keep_means(NPAIR - 1)
            gate(NPAIR - 1)


def collect(nc, io, keep):
    k = keep
    with ExitStack() as ctx:
        m = Memory(nc, ctx)
        second = m.sb("second", [P, NT, D])
        gathered = [m.sem(f"cgathered{i}") for i in range(NGRP)]
        added, stored = m.sem("cadded"), m.sem("cstored")
        block = ctx.enter_context(nc.Block())

        @block.gpsimd
        def _(pool):
            for j in range(NT):
                gather(pool, io, 1, k.slot[:, j, 1:2], second[:, j, :], gathered[j // GRP])

        @block.vector
        def _(dve):
            for c in range(TOPK):
                for g in range(NGRP):
                    if c:
                        dve.wait_ge(gathered[g], GRP * 16)
                        dve.wait_ge(added, (g + 1) * GRP)
                    for j in range(g * GRP, (g + 1) * GRP):
                        row = second[:, j, :] if c else k.first[:, j, :]
                        dve.scalar_tensor_tensor(k.x[:, j, :], row, k.share[:, j, c:c + 1], k.x[:, j, :],
                                                 ALU.mult, ALU.add).then_inc(added, 1)

        @block.sync
        def _(sp):
            dst = io.out.rearrange("(n p) d -> p n d", p=P)
            for t in range(NPAIR):
                sp.wait_ge(added, NT + (t + 1) * TPP)
                sp.dma_start(dst[:, t * TPP:(t + 1) * TPP, :], k.x[:, t * TPP:(t + 1) * TPP, :]).then_inc(stored, 16)
            sp.wait_ge(stored, 16 * NPAIR)


class Kept:

    def __init__(self, m):
        self.x = m.sb("x", [P, NT, D])
        self.const = m.sb("const", [P, C_END])
        self.gate = m.sb("gate", [P, E])
        self.wb = m.sb("wb", [P, H])
        self.wtap = m.sb("wtap", [P, TAPS, 3 * D])
        self.w1, self.w1s = m.sb("w1", [P, 2 * D]), m.sb("w1s", [NOUT, 2 * D])
        self.b1 = m.sb("b1", [P, 2])
        self.w2, self.b2 = m.sb("w2", [P, 2, NOUT]), m.sb("b2", [P, NOUT])
        self.wout = m.sb("wout", [P, D])
        self.lag = m.sb("lag", [P, LAGS, D])
        self.eps = m.sb("eps", [P, 3])
        self.count = m.sb("count", [P, TOPK * E])
        self.slot = m.sb("slot", [P, YB, TOPK], U32)
        self.share = m.sb("share", [P, NT, TOPK])
        self.upper, self.ones = m.sb("upper", [P, P], BF16), m.sb("ones", [P, P], BF16)
        self.xn = m.sb("xn", [P, NT, D])
        self.first = m.sb("first", [P, NT, D])
        self.w = [m.sb(f"expert{i}", [P, 3, F]) for i in range(2)]
        self.ms = m.sb("ms", [P, NT, D])


class Dram:

    def __init__(self, nc, arrays):
        def given(n):
            v = arrays[n]
            return nc.dram_tensor(n + "_in", v.shape, mybir.dt.from_np(v.dtype), kind="ExternalInput").ap()

        def scratch(n, *shape):
            return nc.dram_tensor(n, shape, F32, kind="Internal").ap()

        self.x, self.const, self.gate, self.wexp = given("x"), given("const"), given("gate"), given("wexp")
        self.wqkv, self.taps, self.wb = given("wqkv"), given("taps"), given("wb")
        self.ms3, self.ms15, self.ms31 = given("ms3"), given("ms15"), given("ms31")
        self.mixT, self.chan = given("mixT"), given("chan")
        self.w1, self.b1, self.w2, self.b2 = given("w1"), given("b1"), given("w2"), given("b2")
        self.onorm, self.wo = given("onorm"), given("wo")
        self.out = nc.dram_tensor("out", (BATCH * SEQ, D), F32, kind="ExternalOutput").ap()
        self.queue = [scratch(f"queue{c}", SLOTS, D) for c in range(TOPK)]
        self.rows = [scratch(f"rows{c}", SLOTS + 1, D) for c in range(TOPK)]
        self.pair = scratch("pair", NPAIR * P, 7 * PT + SEQ)
        self.low = scratch("low_dram", BATCH * H * NCH, CHUNK * CHUNK)
        self.inv = scratch("inv_dram", BATCH * H * NCH, CHUNK * CHUNK)


def program(nc, io):
    with ExitStack() as ctx:
        keep = Kept(Memory(nc, ctx))
        prepare(nc, io, keep)
        route(nc, io, keep, "r1")
        experts(nc, io, keep, "e1")
        project(nc, io, keep)
        attend(nc, io, keep)
        route(nc, io, keep, "r2")
        experts(nc, io, keep, "e2")
        collect(nc, io, keep)


def layouts(inputs):
    a = {n: np.asarray(v) for n, v in inputs.items()}
    at = lambda n: a["L0_attn_" + n]
    ff = lambda n: a["L0_ffn_" + n]
    wo = ff("wo").transpose(0, 2, 1).reshape(E, FT, P, D).transpose(0, 2, 1, 3).reshape(E, P, F)
    out = {
        "x": at("hidden_states").reshape(BATCH * SEQ, D),
        "const": shape_constants(),
        "gate": ff("gate_w").T,
        "wexp": np.concatenate([ff("wi_gate").transpose(0, 2, 1), ff("wi_up").transpose(0, 2, 1), wo],
                               axis=2).reshape(E * P, 3 * F),
        "wqkv": np.stack([at("Wq"), at("Wk"), at("Wv")], axis=1),
        "taps": np.stack([at("conv_q_w").T, at("conv_k_w").T, at("conv_v_w").T], axis=1).reshape(-1),
        "wb": at("Wb"), "ms3": at("ms_w3"), "ms15": at("ms_w15"), "ms31": at("ms_w31"),
        "mixT": at("kernel_mix_w").T, "chan": at("channel_mixer_w"),
        "w1": at("fusion_w1"), "b1": at("fusion_b1").reshape(2, P).T, "w2": at("fusion_w2"), "b2": at("fusion_b2"),
        "onorm": at("o_norm_w"), "wo": at("Wo"),
    }
    return {n: np.ascontiguousarray(v) for n, v in out.items()}


def build(nc, arrays):
    program(nc, Dram(nc, arrays))


def kernel(**inputs):
    import concourse.bacc as bacc
    from concourse.bass_utils import run_bass_kernel_spmd

    arrays = layouts(inputs)
    nc = bacc.Bacc("TRN2", target_bir_lowering=False, num_devices=1)
    build(nc, arrays)
    r = run_bass_kernel_spmd(nc, [{n + "_in": v for n, v in arrays.items()}], core_ids=[0])
    return r.results[0]["out"].reshape(BATCH, SEQ, D)
```

```python
from contextlib import ExitStack

import numpy as np

import concourse.bass as bass
from concourse import mybir

F32 = mybir.dt.float32
F32R = mybir.dt.float32r
BF16 = mybir.dt.bfloat16
U32 = mybir.dt.uint32
ALU = mybir.AluOpType
ACT = mybir.ActivationFunctionType
AX = mybir.AxisListType

P = 128
BATCH, SEQ, D = 16, 256, 128
H, DH = 4, 32
CHUNK = 32
NT = BATCH * SEQ // P
TPP = 4
NPAIR = NT // TPP
PT = TPP * P
NCH = SEQ // CHUNK
QC = P // CHUNK
E, TOPK, F = 8, 2, 512
CAP = int(BATCH * SEQ / E * 1.25)
SLOTS = E * CAP
CT = CAP // P
HALF = CAP // 2
FT = F // P
TAPS = 4
PAD = TAPS - 1
QKVB = 3 * D + H
LAGS = 31
MS = SEQ // P * LAGS
GRP = 8
YB = NT + 2 * TPP
NGRP = NT // GRP
NOUT = 3 * H
LN_EPS, L2_EPS, RMS_EPS = 1e-5, 1e-6, 1e-5

C_ID, C_HEAD, C_UP, C_ONE = 0, 128, 256, 384
C_NEG, C_INC, C_IOTA = 512, 544, 576
C_END = C_IOTA + E


def shape_constants():
    c = np.zeros((P, C_END), np.float32)
    p = np.arange(P)
    c[:, C_ID:C_ID + P] = np.eye(P)
    c[:, C_HEAD:C_HEAD + P] = p[:, None] // DH == p[None, :] // DH
    c[:, C_UP:C_UP + P] = p[:, None] < p[None, :]
    c[:, C_ONE:C_ONE + P] = 1.0
    e = np.arange(CHUNK)
    c[:, C_NEG:C_NEG + CHUNK] = -1.0 * (e[None, :] < p[:, None] % CHUNK)
    c[:, C_INC:C_INC + CHUNK] = p[:, None] % CHUNK <= e[None, :]
    c[:, C_IOTA:C_IOTA + E] = np.arange(E)
    return c


def bc(ap, shape):
    return ap.to_broadcast(list(shape))


class Memory:

    def __init__(self, nc, ctx):
        self.nc, self.ctx = nc, ctx

    def sb(self, name, shape, dt=F32):
        return self.ctx.enter_context(self.nc.sbuf_tensor(name, list(shape), dt))

    def ps(self, name, shape, dt=F32):
        return self.ctx.enter_context(self.nc.psum_tensor(name, list(shape), dt))

    def sem(self, name):
        return self.ctx.enter_context(self.nc.semaphore(name))


class Raw:

    def __init__(self, m):
        self.wqkv = m.sb("wqkv", [P, 3, D])
        self.taps = m.sb("taps", [P, TAPS, 3 * D])
        self.ms3, self.ms15, self.ms31 = m.sb("ms3", [P, 3]), m.sb("ms15", [P, 15]), m.sb("ms31", [P, 31])
        self.mixT = m.sb("mixT", [P, 3 * D])
        self.chan = m.sb("chan", [P, D])
        self.wtap = m.sb("wtap", [P, TAPS, QKVB])
        self.base = m.sb("base", [P, 3, D])
        self.wo, self.onorm = m.sb("wo_raw", [P, D]), m.sb("onorm", [P, 1])

    def loads(self, io, k):
        return [
            (self.wqkv[:], io.wqkv), (self.taps[:].rearrange("p a b -> p (a b)"), io.taps.partition_broadcast(P)),
            (self.ms3[:], io.ms3), (self.ms15[:], io.ms15), (self.ms31[:], io.ms31), (self.chan[:], io.chan),
            (self.wo[:], io.wo), (self.wtap[:, PAD, 3 * D:], io.wb), (k.w1[:], io.w1[0:D, :]), (k.w1s[:], io.w1[D:D + NOUT, :]),
            (k.b1[:], io.b1), (k.w2[:], io.w2.rearrange("(f p) n -> p f n", p=P)),
            (k.b2[:], io.b2.partition_broadcast(P)),
        ] + [(self.onorm[DH * h:DH * h + DH, :], io.onorm.rearrange("(d a) -> d a", a=1)) for h in range(H)] \
          + [(self.mixT[DH * h:DH * h + DH, 3 * DH * h:3 * DH * h + 3 * DH], io.mixT) for h in range(H)]

    def mix(self, pe, bank):
        for i in range(3):
            mm = pe.matmul(bank[:, i * D:i * D + D], self.mixT[:, i * D:i * D + D], self.chan[:], start=True, stop=True)
        return mm

    def fold(self, pool, k, folded):
        lag = lambda n: k.lag[:, n, :]
        pool.wait_ge(folded, 1)
        for tap in range(TAPS):
            pool.tensor_tensor(self.wtap[:, tap, 0:3 * D], self.taps[:, tap, :],
                               self.wqkv[:].rearrange("p a b -> p (a b)"), ALU.mult)
        pool.memset(self.wtap[:, 0:PAD, 3 * D:], 0.0).then_inc(folded, 1)
        pool.wait_ge(folded, 2)
        pool.tensor_copy(k.tap_hi[:], self.wtap[:]).then_inc(folded, 1)
        pool.wait_ge(folded, 3)
        pool.tensor_tensor(k.tap_lo[:], self.wtap[:], k.tap_hi[:], ALU.subtract)
        pool.tensor_scalar(k.wout[:], self.wo[:], self.onorm[:, 0:1], None, ALU.mult)
        sets = ((2, self.ms31, LAGS), (1, self.ms15, 15), (0, self.ms3, 3))
        count = 3
        for i, taps, size in sets:
            for n in range(size):
                dst = lag(n) if size == LAGS else k.ms[:, n, :]
                pool.tensor_scalar(dst, self.base[:, i, :], taps[:, size - 1 - n:size - n], None,
                                   ALU.mult).then_inc(folded, 1)
            count += size
            pool.wait_ge(folded, count)
            if size < LAGS:
                for n in range(size):
                    pool.tensor_tensor(lag(n), lag(n), k.ms[:, n, :], ALU.add).then_inc(folded, 1)
                count += size
                pool.wait_ge(folded, count)


class Steps:

    def __init__(self, eng, sem, base=0):
        self.eng, self.sem, self.base, self.n = eng, sem, base, 0

    def done(self, ins):
        self.n += 1
        ins.then_inc(self.sem, 1)
        self.eng.wait_ge(self.sem, self.base + self.n)


def wait_apart(eng, sem, value, beat):
    eng.wait_ge(sem, value)
    eng.sem_inc(beat, 1)


def layernorm_stats(dve, link, stat, mv, tiles, varied, beat):
    for j, tile in enumerate(tiles):
        last = dve.bn_stats(stat[:, j, :], tile)
    link(last)
    dve.sem_inc(beat, 1)
    for j in range(len(tiles)):
        last = dve.bn_aggr(mv[:, j, :], stat[:, j, :])
    last.then_inc(varied, 1)


def scatter(pool, k, io, j, c, sent):
    pool.indirect_dma_start(io.queue[c], bass.IndirectOffsetOnAxis(ap=k.slot[:, j, c:c + 1], axis=0),
                            k.xn[:, j, :], None, bounds_check=SLOTS - 1, oob_is_err=False).then_inc(sent, 16)


def gather(pool, io, c, slot, dst, got):
    pool.indirect_dma_start(dst, None, io.rows[c], bass.IndirectOffsetOnAxis(ap=slot, axis=0)).then_inc(got, 16)


def route(nc, io, keep, name, raw=None):
    k = keep
    with ExitStack() as ctx:
        m = Memory(nc, ctx)
        sem = lambda s: m.sem(f"{name}_{s}")
        sb = lambda s, shape, dt=F32: m.sb(f"{name}_{s}", shape, dt)
        stat, mv = sb("stat", [P, GRP, 6]), sb("mv", [P, GRP, 2])
        std, rstd = sb("std", [P, GRP]), sb("rstd", [P, GRP])
        xn = k.xn
        xnT = sb("xnT", [P, GRP * P])
        logit = sb("logit", [P, GRP, E])
        top, index = sb("top", [P, GRP, 8]), sb("index", [P, GRP, 8], U32)
        idx = sb("idx", [P, GRP, TOPK])
        hot = sb("hot", [P, GRP, TOPK, E], BF16)
        seen = [sb(f"seen{i}", [P, 1, TOPK * E], BF16) for i in range(2)]
        more = sb("more", [P, TOPK * E])
        prod, pos = sb("prod", [P, GRP * TOPK, E]), sb("pos", [P, GRP, TOPK])
        place, valid = sb("place", [P, GRP, TOPK]), sb("valid", [P, GRP, TOPK])
        gap, ratio, share = sb("gap", [P, GRP]), sb("ratio", [P, GRP]), sb("share", [P, GRP, TOPK])
        ptr = m.ps(f"{name}_ptr", [P, 2, 512])
        plog, ppos = m.ps(f"{name}_plog", [P, 512]), m.ps(f"{name}_ppos", [P, 512])
        chain, beat = sem("chain"), sem("beat")
        varied, rooted, normed, turned = sem("varied"), sem("rooted"), sem("normed"), sem("turned")
        evac, scored, gapped, powered = sem("evac"), sem("scored"), sem("gapped"), sem("powered")
        counted, placed, slotted, sent = sem("counted"), sem("placed"), sem("slotted"), sem("sent")
        later = sem("later")
        CLEARS = 3
        if raw:
            zero = sb("zero", [P, SLOTS // P // 2 * D])
            xgot, cleared = [sem(f"xgot{i}") for i in range(2)], sem("cleared")
            cgot, wiped = sem("cgot"), sem("wiped")

        def clear(sp, c, done):
            queue = io.queue[c].rearrange("(p r) d -> p (r d)", p=P)
            half = SLOTS // P // 2 * D
            for n in range(2):
                sp.dma_start(queue[:, n * half:(n + 1) * half], zero[:]).then_inc(done, 16)
            sp.dma_start(io.rows[c][SLOTS:SLOTS + 1, :], zero[0:1, 0:D]).then_inc(done, 16)

        block = ctx.enter_context(nc.Block())

        @block.sync
        def _(sp):
            if raw:
                x = io.x.rearrange("(n p) d -> p n d", p=P)
                sp.dma_start(k.x[:, 0:GRP, :], x[:, 0:GRP, :]).then_inc(xgot[0], 16)
                sp.dma_start(k.const[:], io.const).then_inc(cgot, 16)
                sp.dma_start(k.gate[:], io.gate).then_inc(cgot, 16)
                sp.dma_start(k.x[:, GRP:NT, :], x[:, GRP:NT, :]).then_inc(xgot[1], 16)
                sp.wait_ge(wiped, 2)
                clear(sp, 0, cleared)
            for e in range(2):
                load_expert(sp, io, k.w[e], e, later)
            if raw:
                loads = raw.loads(io, k)
                for dst, src in loads:
                    sp.dma_start(dst, src).then_inc(later, 16)
                clear(sp, 1, later)
            sp.wait_ge(later, 16 * (2 + (len(loads) + CLEARS if raw else 0)))

        @block.vector
        def _(dve):
            steps = Steps(dve, chain)
            link = steps.done
            dve.memset(seen[0][:], 0.0)
            link(dve.memset(k.count[:], 0.0))

            def statistics(g):
                if raw and g < 2:
                    dve.wait_ge(xgot[g], 16)
                layernorm_stats(dve, link, stat, mv, [k.x[:, g * GRP + j, :] for j in range(GRP)], varied, beat)

            def normalise(g):
                dve.wait_ge(rooted, g + 1)
                link(dve.reciprocal(rstd[:], std[:]))
                for j in range(GRP):
                    last = dve.tensor_scalar(xn[:, g * GRP + j, :], k.x[:, g * GRP + j, :],
                                             mv[:, j, 0:1], rstd[:, j:j + 1], ALU.subtract, ALU.mult)
                last.then_inc(normed, 1)

            if raw:
                for i, eps in enumerate((LN_EPS, L2_EPS, RMS_EPS)):
                    dve.memset(k.eps[:, i:i + 1], eps)
                dve.memset(k.slot[:], 0)
            statistics(0)
            normalise(0)
            if raw:
                dve.wait_ge(cgot, 32)
                dve.tensor_copy(k.upper[:], k.const[:, C_UP:C_UP + P])
                dve.tensor_copy(k.ones[:], k.const[:, C_ONE:C_ONE + P])
            for g in range(NGRP):
                if g + 1 < NGRP:
                    statistics(g + 1)
                dve.wait_ge(scored, g + 1)
                link(dve.tensor_copy(logit[:].rearrange("p a b -> p (a b)"), plog[:, 0:GRP * E]))
                for j in range(GRP):
                    last = dve.max(top[:, j, :], logit[:, j, :])
                link(last)
                dve.tensor_tensor(gap[:], top[:, :, 1], top[:, :, 0], ALU.subtract).then_inc(gapped, 1)
                for j in range(GRP):
                    last = dve.max_index(index[:, j, :], top[:, j, :], logit[:, j, :])
                link(last)
                link(dve.tensor_copy(idx[:], index[:, :, 0:TOPK]))
                link(dve.tensor_tensor(
                    hot[:], bc(k.const[:, C_IOTA:C_IOTA + E].unsqueeze(1).unsqueeze(1), [P, GRP, TOPK, E]),
                    bc(idx[:].unsqueeze(3), [P, GRP, TOPK, E]), ALU.is_equal))
                dve.sem_inc(counted, 1)
                if g + 1 < NGRP:
                    normalise(g + 1)
                    link(dve.tensor_reduce(more[:], hot[:].rearrange("p a b c -> p (b c) a"), AX.X, ALU.add))
                    link(dve.tensor_tensor(k.count[:], k.count[:], more[:], ALU.add))
                    link(dve.tensor_copy(seen[(g + 1) % 2][:, 0, :], k.count[:]))
                dve.wait_ge(placed, g + 1)
                link(dve.tensor_tensor(prod[:], ppos[:, 0:GRP * TOPK * E].rearrange("p (a b) -> p a b", b=E),
                                       hot[:].rearrange("p a b c -> p (a b) c"), ALU.mult))
                link(dve.tensor_reduce(pos[:].rearrange("p a b -> p (a b)"), prod[:], AX.X, ALU.add))
                dve.tensor_scalar(valid[:], pos[:], float(CAP), None, ALU.is_lt)
                link(dve.scalar_tensor_tensor(place[:], idx[:], float(CAP), pos[:], ALU.mult, ALU.add))
                link(dve.scalar_tensor_tensor(place[:], place[:], -float(SLOTS), valid[:], ALU.add, ALU.mult))
                dve.tensor_scalar(k.slot[:, g * GRP:(g + 1) * GRP, :], place[:], float(SLOTS), None,
                                  ALU.add).then_inc(slotted, 1)
                dve.wait_ge(powered, g + 1)
                link(dve.tensor_scalar(gap[:], ratio[:], 1.0, None, ALU.add))
                link(dve.reciprocal(share[:, :, 0], gap[:]))
                link(dve.tensor_tensor(share[:, :, 1], share[:, :, 0], ratio[:], ALU.mult))
                link(dve.scalar_tensor_tensor(k.share[:, g * GRP:(g + 1) * GRP, :], share[:], 0.5, valid[:],
                                              ALU.mult, ALU.mult))

        @block.scalar
        def _(act):
            def root(g):
                act.wait_ge(varied, g + 1)
                act.activation(std[:], mv[:, :, 1], ACT.Sqrt, bias=k.eps[:, 0:1]).then_inc(rooted, 1)

            root(0)
            for g in range(NGRP):
                for n in range(2):
                    act.wait_ge(turned, g * 2 + n + 1)
                    act.activation(xnT[:, n * 512:n * 512 + 512], ptr[:, n, :], ACT.Copy).then_inc(evac, 1)
                if g + 1 < NGRP:
                    root(g + 1)
                act.wait_ge(gapped, g + 1)
                act.activation(ratio[:], gap[:], ACT.Exp).then_inc(powered, 1)

        @block.tensor
        def _(pe):
            if raw:
                pe.wait_ge(cgot, 32)
            for g in range(NGRP):
                pe.wait_ge(normed, g + 1)
                for n in range(2):
                    for j in range(4):
                        mm = pe.transpose(ptr[:, n, j * P:j * P + P], xn[:, g * GRP + n * 4 + j, :],
                                          k.const[:, C_ID:C_ID + P])
                    mm.then_inc(turned, 1)
                pe.wait_ge(evac, 2 * g + 2)
                for j in range(GRP):
                    mm = pe.matmul(plog[:, j * E:j * E + E], xnT[:, j * P:j * P + P], k.gate[:], start=True, stop=True)
                mm.then_inc(scored, 1)
                pe.wait_ge(counted, g + 1)
                flat = hot[:].rearrange("p a b c -> p a (b c)")
                pe.matmul(ppos[:, 0:GRP * TOPK * E], k.upper[:], flat, start=True, stop=False)
                for j in range(GRP - 1):
                    pe.matmul(ppos[:, (j + 1) * TOPK * E:GRP * TOPK * E], k.ones[:],
                              bc(flat[:, j:j + 1, :], [P, GRP - 1 - j, TOPK * E]), start=False, stop=False)
                pe.matmul(ppos[:, 0:GRP * TOPK * E], k.ones[:], bc(seen[g % 2][:], [P, GRP, TOPK * E]),
                          start=False, stop=True).then_inc(placed, 1)

        @block.gpsimd
        def _(pool):
            if raw:
                pool.memset(zero[:], 0.0).then_inc(wiped, 1)
                pool.memset(raw.mixT[:], 0.0).then_inc(wiped, 1)
                pool.wait_ge(cleared, 16 * CLEARS)
            for g in range(NGRP):
                pool.wait_ge(slotted, g + 1)
                for j in range(g * GRP, (g + 1) * GRP):
                    scatter(pool, k, io, j, 0, sent)
            pool.wait_ge(sent, 16 * NT)


def load_expert(sp, io, w, e, got):
    sp.dma_start(w[:].rearrange("p a b -> p (a b)"), io.wexp[bass.ds(e * P, P), :]).then_inc(got, 16)


def experts(nc, io, keep, name, raw=None):
    k = keep
    with ExitStack() as ctx:
        m = Memory(nc, ctx)
        sem = lambda s: m.sem(f"{name}_{s}")
        sb = lambda s, shape, dt=F32: m.sb(f"{name}_{s}", shape, dt)
        w = k.w
        xs = [sb(f"xs{i}", [P, CT, D]) for i in range(2)]
        xhi, xlo = ([sb(f"x{n}{i}", [P, CAP], F32R) for i in range(2)] for n in ("hi", "lo"))
        whi, wlo = ([sb(f"w{n}{i}", [P, 2, F], F32R) for i in range(2)] for n in ("hi", "lo"))
        sg = [sb(f"sg{i}", [P, HALF]) for i in range(2)]
        hid = [sb(f"hid{i}", [P, FT, CAP]) for i in range(2)]
        rows = [sb(f"rows{i}", [P, CT, D]) for i in range(2)]
        pt, po = m.ps(f"{name}_pt", [P, 2, 512]), m.ps(f"{name}_po", [P, 2, 512])
        pg = [m.ps(f"{name}_pg{i}", [P, 512]) for i in range(2)]
        pu = [m.ps(f"{name}_pu{i}", [P, 512]) for i in range(2)]
        wgot = [sem(f"wgot{i}") for i in range(2)]
        xgot = [sem(f"xgot{i}") for i in range(2)]
        beat = sem("beat")
        wfree, hfree = sem("wfree"), sem("hfree")
        turned, evac, gued, silued = sem("turned"), sem("evac"), sem("gued"), sem("silued")
        rounded, split = sem("rounded"), sem("split")
        if raw:
            based, folded = sem("based"), sem("folded")
        downed, rready = sem("downed"), sem("rready")
        stored = [[sem(f"stored{c}{i}") for i in range(2)] for c in range(TOPK)]
        sent, fetched = sem("sent"), sem("fetched")
        block = ctx.enter_context(nc.Block())
        NQ = TOPK * E
        NB = 2 * FT
        SPLIT_AT = (4, 6)

        @block.sync
        def _(sp):
            for par in range(2):
                sp.sem_inc(wgot[par], 16)

            def load(c, e, par, weights=True):
                q = c * E + e
                wait_apart(sp, turned, q + 1, beat)
                sp.dma_start(xs[par][:], io.queue[c][bass.ds(e * CAP, CAP), :].rearrange(
                    "(s p) d -> p s d", p=P)).then_inc(xgot[par], 16)
                if weights:
                    wait_apart(sp, wfree, q - 1, beat)
                    load_expert(sp, io, w[par], e, wgot[par])

            def store(c, e, par):
                q = c * E + e
                wait_apart(sp, rready, 2 * q + 4, beat)
                sp.dma_start(io.rows[c][bass.ds(e * CAP, CAP), :].rearrange("(s p) d -> p s d", p=P),
                             rows[par][:]).then_inc(stored[c][par], 16)

            for c in range(TOPK):
                if c:
                    sp.wait_ge(sent, 16 * NT)
                for e in range(2):
                    load(c, e, e, weights=(c > 0))
                    if c:
                        store(c - 1, E - 2 + e, e)
                with sp.Fori(1, E // 2) as ee:
                    for par in range(2):
                        load(c, ee * 2 + par, par)
                        store(c, ee * 2 + par - 2, par)
            for e in range(2):
                store(TOPK - 1, E - 2 + e, e)
            for par in range(2):
                sp.wait_ge(stored[TOPK - 1][par], 16 * E // 2)

        @block.tensor
        def _(pe):
            pe.sem_inc(turned, 2)

            def turn(q, par, half):
                pe.wait_ge(xgot[par], 16 * half)
                for s in range(CT):
                    mm = pe.transpose(pt[:, s // 4, (s % 4) * P:(s % 4) * P + P], xs[par][:, s, :],
                                      k.const[:, C_ID:C_ID + P])
                mm.then_inc(turned, 1)

            def down(par, s):
                for f in range(FT):
                    mm = pe.matmul(po[:, s // 4, (s % 4) * P:(s % 4) * P + P], hid[par][:, f, s * P:s * P + P],
                                   w[par][:, 2, f * P:f * P + P], start=(f == 0), stop=(f == FT - 1))
                return mm

            def queue(q, par, half, follow):
                pe.wait_ge(evac, 2 * q + 2)
                pe.wait_ge(split, 4 * q + 4)
                for c in range(2):
                    for f in range(FT):
                        n = c * FT + f
                        pe.wait_ge(hfree, q * NB + n + 1)
                        cols = slice(c * HALF, c * HALF + HALF)
                        fs = slice(f * P, f * P + P)
                        for i, bank in enumerate((pg, pu)):
                            out = bank[n % 2][:, 0:HALF]
                            pe.matmul(out, whi[par][:, i, fs], xlo[par][:, cols], start=True, stop=False)
                            pe.matmul(out, wlo[par][:, i, fs], xhi[par][:, cols], start=False, stop=False)
                            pe.matmul(out, whi[par][:, i, fs], xhi[par][:, cols], start=False,
                                      stop=True).then_inc(gued, 1)
                if follow is not None:
                    turn(q + 1, 1 - par, follow)
                pe.wait_ge(rready, 2 * q + 2)
                pe.wait_ge(hfree, q * NB + FT + 2)
                for s in range(HALF // P):
                    down(par, s)
                pe.wait_ge(hfree, q * NB + NB + 2)
                for s in range(HALF // P, CT):
                    mm = down(par, s)
                mm.then_inc(downed, 1)

            turn(0, 0, 1)
            if raw:
                raw.mix(pe, pg[0]).then_inc(based, 1)
                pe.wait_ge(folded, 1)
            with pe.Fori(0, NQ // 2 - 1) as r:
                queue(r * 2, 0, r + 1, r + 1)
                queue(r * 2 + 1, 1, r + 1, r + 2)
            queue(NQ - 2, 0, NQ // 2, NQ // 2)
            queue(NQ - 1, 1, NQ // 2, None)

        @block.scalar
        def _(act):
            def evacuate(q, par):
                act.wait_ge(turned, q + 3)
                act.activation(xhi[par][:, 0:512], pt[:, 0, :], ACT.Copy).then_inc(evac, 1)
                act.activation(xhi[par][:, 512:CAP], pt[:, 1, 0:CAP - 512], ACT.Copy).then_inc(evac, 1)

            def high(par, half, i):
                act.wait_ge(wgot[par], 16 * half)
                act.activation(whi[par][:, i, :], w[par][:, i, :], ACT.Copy).then_inc(rounded, 1)

            def queue(q, par, follow):
                for n in range(NB):
                    act.wait_ge(gued, 2 * (q * NB + n) + 1)
                    act.activation(sg[n % 2][:], pg[n % 2][:, 0:HALF], ACT.Silu).then_inc(silued, 1)
                    if follow is not None and n in SPLIT_AT:
                        high(1 - par, follow, SPLIT_AT.index(n))
                if follow is not None:
                    evacuate(q + 1, 1 - par)

            high(0, 1, 0)
            high(0, 1, 1)
            evacuate(0, 0)
            with act.Fori(0, NQ // 2 - 1) as r:
                queue(r * 2, 0, r + 1)
                queue(r * 2 + 1, 1, r + 2)
            queue(NQ - 2, 0, NQ // 2)
            queue(NQ - 1, 1, None)

        @block.vector
        def _(dve):
            dve.sem_inc(hfree, 2)
            dve.sem_inc(rready, 2)

            def low_weights(q, par, i):
                dve.wait_ge(rounded, 2 * q + i + 1)
                dve.tensor_tensor(wlo[par][:, i, :], w[par][:, i, :], whi[par][:, i, :], ALU.subtract).then_inc(split, 1)

            def low_rows(q, par):
                dve.wait_ge(evac, 2 * q + 1)
                dve.tensor_tensor(xlo[par][:, 0:512], pt[:, 0, :], xhi[par][:, 0:512], ALU.subtract).then_inc(split, 1)
                dve.wait_ge(evac, 2 * q + 2)
                dve.tensor_tensor(xlo[par][:, 512:CAP], pt[:, 1, 0:CAP - 512], xhi[par][:, 512:CAP],
                                  ALU.subtract).then_inc(split, 1)

            def queue(q, par, follow=True):
                for n in range(NB):
                    c, f = n // FT, n % FT
                    dve.wait_ge(silued, q * NB + n + 1)
                    dve.wait_ge(gued, 2 * (q * NB + n) + 2)
                    dve.tensor_tensor(hid[par][:, f, c * HALF:c * HALF + HALF], sg[n % 2][:],
                                      pu[n % 2][:, 0:HALF], ALU.mult).then_inc(hfree, 1)
                    if follow and n in SPLIT_AT:
                        low_weights(q + 1, 1 - par, SPLIT_AT.index(n))
                if follow:
                    low_rows(q + 1, 1 - par)
                dve.wait_ge(downed, q + 1)
                dve.sem_inc(wfree, 1)

            def evacuate(q, par):
                flat = rows[par][:].rearrange("p a b -> p (a b)")
                dve.tensor_copy(flat[:, 0:512], po[:, 0, :]).then_inc(rready, 1)
                dve.tensor_copy(flat[:, 512:CAP], po[:, 1, 0:CAP - 512]).then_inc(rready, 1)

            if raw:
                dve.wait_ge(based, 1)
                dve.tensor_copy(raw.base[:].rearrange("p a b -> p (a b)"), pg[0][:, 0:3 * D]).then_inc(folded, 1)
            low_weights(0, 0, 0)
            low_weights(0, 0, 1)
            low_rows(0, 0)
            for c in range(TOPK):
                for e in range(2):
                    queue(c * E + e, e)
                    if c:
                        dve.wait_ge(stored[c - 1][e], 16 * E // 2)
                    evacuate(c * E + e, e)
                last = E // 2 - c
                with dve.Fori(1, last) as r:
                    for par in range(2):
                        q = c * E + r * 2 + par
                        queue(q, par)
                        dve.wait_ge(stored[c][par], r * 16)
                        evacuate(q, par)
            for par in range(2):
                queue(NQ - 2 + par, par, follow=(par == 0))
                dve.wait_ge(stored[TOPK - 1][par], (E // 2 - 1) * 16)
                evacuate(NQ - 2 + par, par)

        @block.gpsimd
        def _(pool):
            for j in range(NT):
                scatter(pool, k, io, j, 1, sent)
            if raw:
                raw.fold(pool, k, folded)
            for par in range(2):
                pool.wait_ge(stored[0][par], 16 * E // 2)
            for j in range(NT):
                gather(pool, io, 0, k.slot[:, j, 0:1], k.first[:, j, :], fetched)
            pool.wait_ge(fetched, 16 * NT)


def identities(eng, link, inv):
    link(eng.memset(inv[:], 0.0))
    link(eng.memset(inv[:].rearrange("p a b -> p (a b)")[:, 0:CHUNK * CHUNK:CHUNK + 1], 1.0))


def substitute(eng, link, nmat, inv, prod, first, last):
    for j in range(first, last):
        shape = [P, j + 1, CHUNK - 1 - j]
        part = prod[:, 0:shape[1] * shape[2]].rearrange("p (c i) -> p c i", c=shape[1])
        factor = nmat[:, j + 1:CHUNK, j:j + 1].rearrange("p i j -> p j i")
        link(eng.tensor_tensor(part, bc(inv[:, 0:j + 1, j:j + 1], shape), bc(factor, shape), ALU.mult))
        rest = inv[:, 0:j + 1, j + 1:CHUNK]
        link(eng.tensor_tensor(rest, rest, part, ALU.add))


class Inputs:

    SOLVE, SCAN = 2 + QC, 4

    def __init__(self, m):
        self.qT, self.kn, self.kb, self.vb = (m.sb(f"a_{n}", [P, PT]) for n in ("qT", "kn", "kb", "vb"))
        self.loc, self.inv = (m.sb(f"a_{n}", [P, TPP * H, CHUNK]) for n in ("loc", "inv"))
        self.vpad = m.sb("a_vpad", [P, LAGS - 1 + SEQ])

    def field(self, sp, io, t, dst, field, got, width=PT):
        sp.dma_start(dst, io.pair[bass.ds(t * P, P), field * PT:field * PT + width]).then_inc(got, 16)

    def load_solve(self, sp, io, t, got):
        self.field(sp, io, t, self.kb[:], 3, got)
        self.field(sp, io, t, self.vb[:], 4, got)
        for n in range(QC):
            src = io.inv[bass.ds((t * QC + n) * TPP * H, TPP * H), :].rearrange("g (e c) -> e g c", c=CHUNK)
            sp.dma_start(self.inv[n * CHUNK:n * CHUNK + CHUNK, :, :], src).then_inc(got, 16)

    def load_scan(self, sp, io, t, got):
        self.field(sp, io, t, self.qT[:], 0, got)
        self.field(sp, io, t, self.kn[:], 1, got)
        self.field(sp, io, t, self.loc[:].rearrange("p a b -> p (a b)"), 5, got)
        self.field(sp, io, t, self.vpad[:, LAGS - 1:], 7, got, width=SEQ)


def project(nc, io, keep, inputs):
    k = keep
    G = TPP * H
    with ExitStack() as ctx:
        m = Memory(nc, ctx)
        sem, sb = m.sem, m.sb
        slots = [sb(f"slots{i}", [P, TPP], U32) for i in range(2)]
        got = [sb(f"got{i}", [P, TPP, D]) for i in range(2)]
        stat, mv = sb("stat", [P, TPP, 6]), sb("mv", [P, TPP, 2])
        std, rstd = sb("std", [P, TPP]), sb("rstd", [P, TPP])
        xn = sb("pxn", [P, PT])
        xnT = sb("xnT", [P, 2, SEQ])
        xhi, xlo = (sb(f"px{n}", [P, 2, PAD + SEQ], F32R) for n in ("hi", "lo"))
        qkv = sb("qkv", [P, TPP, 3 * D])
        tanhb, beta = sb("tanhb", [P, G]), sb("beta", [P, G])
        sq, ss = sb("sq", [P, TPP, 2 * D]), sb("ss", [P, 2 * G])
        rn = sb("rn", [P, 2 * G])
        qk = sb("qk", [P, TPP, 2 * D])
        kq = sb("kq", [P, 2, PT])
        vpad = [sb(f"vpad{i}", [P, 2, LAGS - 1 + SEQ]) for i in range(2)]
        kb, vb = sb("kb", [P, PT]), sb("vb", [P, PT])
        low, loc = sb("low", [P, G, CHUNK]), sb("loc", [P, G, CHUNK])
        nmat = sb("nmat", [P, CHUNK, CHUNK])
        inv = sb("inv", [P, CHUNK, CHUNK])
        prod = sb("prod", [P, CHUNK * CHUNK])
        px, pk, pv = (m.ps(f"pp{i}", [P, 512]) for i in range(3))
        pq = px
        pm = m.ps("pm", [P, 512])
        pa = m.ps("pa", [P, 4, 512])
        chain, beat = sem("chain"), sem("beat")
        gathered = [sem(f"gathered{i}") for i in range(2)]
        indexed, varied = sem("indexed"), sem("varied")
        remained = sem("remained")
        rooted, normed, turned, evac = sem("rooted"), sem("normed"), sem("turned"), sem("evac")
        projected, silued, squared, summed = sem("projected"), sem("silued"), sem("squared"), sem("summed")
        lengths, scaled, turned3, moved = sem("lengths"), sem("scaled"), sem("turned3"), sem("moved")
        grammed, masked, weighted, saved = sem("grammed"), sem("masked"), sem("weighted"), sem("saved")
        padded, room, unmasked, factors = sem("padded"), sem("room"), sem("unmasked"), sem("factors")
        convolved, kept = sem("convolved"), sem("kept")
        ngot, inverted, istored, xsaved = sem("ngot"), sem("inverted"), sem("istored"), sem("xsaved")
        block = ctx.enter_context(nc.Block())
        NSAVE = 6 + QC
        NG = NPAIR // 2
        SPLIT = 14
        MS_AT = (0, 6, 24, 34, 52, MS)

        @block.gpsimd
        def _(pool):
            def collect_second(t, par):
                wait_apart(pool, indexed, t + 1, beat)
                for j in range(TPP):
                    gather(pool, io, 1, slots[par][:, j:j + 1], got[par][:, j, :], gathered[par])

            def weigh(t):
                pool.wait_ge(masked, t + 1)
                pool.tensor_tensor(low[:], low[:], bc(beta[:].unsqueeze(2), [P, G, CHUNK]),
                                   ALU.mult).then_inc(weighted, 1)

            collect_second(0, 0)
            with pool.Fori(0, NPAIR // 2 - 1) as r:
                for par in range(2):
                    collect_second(r * 2 + par + 1, 1 - par)
                    weigh(r * 2 + par)
            collect_second(NPAIR - 1, 1)
            weigh(NPAIR - 2)
            weigh(NPAIR - 1)

        @block.vector
        def _(dve):
            def index(t, par):
                return dve.tensor_copy(slots[par][:].rearrange("p (a b) -> p a b", b=1),
                                       k.slot[:, bass.ds(t * TPP, TPP), 1:2])

            def invert_first(link, r):
                dve.wait_ge(ngot, r * 16)
                dve.wait_ge(istored, r * 16)
                identities(dve, link, inv)
                substitute(dve, link, nmat, inv, prod, 0, SPLIT)

            def invert_rest(link):
                substitute(dve, link, nmat, inv, prod, SPLIT, CHUNK - 1)
                dve.sem_inc(inverted, 1)

            def normalise(link, r, par):
                t = r * 2 + par
                dve.wait_ge(gathered[par], (r + 1) * 16 * TPP)
                tile = lambda j: k.x[:, bass.ds(t * TPP + j, 1), :].rearrange("p a d -> p (a d)")
                index(t + 2, par)
                for c in range(TOPK):
                    for j in range(TPP):
                        row = k.first[:, bass.ds(t * TPP + j, 1), :].rearrange("p a d -> p (a d)") if c == 0 \
                            else got[par][:, j, :]
                        last = dve.scalar_tensor_tensor(tile(j), row, k.share[:, bass.ds(t * TPP + j, 1), c], tile(j),
                                                        ALU.mult, ALU.add)
                    link(last)
                dve.sem_inc(indexed, 1)
                layernorm_stats(dve, link, stat, mv, [tile(j) for j in range(TPP)], varied, beat)
                dve.wait_ge(rooted, t + 1)
                link(dve.reciprocal(rstd[:], std[:]))
                for j in range(TPP):
                    last = dve.tensor_scalar(xn[:, j * D:j * D + D], tile(j), mv[:, j, 0:1], rstd[:, j:j + 1],
                                             ALU.subtract, ALU.mult)
                last.then_inc(normed, 1)

            def pair(link, r, par, invert=None, ahead=True):
                t = r * 2 + par
                dve.wait_ge(evac, 2 * t + 2)
                dve.tensor_tensor(xlo[:, :, PAD:], xnT[:], xhi[:, :, PAD:], ALU.subtract).then_inc(remained, 1)
                if invert == "first":
                    invert_first(link, r)
                elif invert == "rest":
                    invert_rest(link)
                dve.wait_ge(squared, t + 1)
                dve.tensor_reduce(ss[:], sq[:].rearrange("p a (b c) -> p (a b) c", c=DH), AX.X,
                                  ALU.add).then_inc(summed, 1)
                dve.wait_ge(room, t + 1)
                link(dve.tensor_scalar(beta[:], tanhb[:], 0.5, 0.5, ALU.mult, ALU.add))
                dve.wait_ge(lengths, t + 1)
                link(dve.reciprocal(rn[:], rn[:]))
                for half in (1, 0):
                    part = slice(half * D, half * D + D)
                    dve.tensor_tensor(qk[:, :, part].rearrange("p a (b c) -> p a b c", c=DH),
                                      qkv[:, :, part].rearrange("p a (b c) -> p a b c", c=DH),
                                      bc(rn[:].rearrange("p (a b) -> p a b", a=TPP)[:, :, half * H:half * H + H]
                                         .unsqueeze(3), [P, TPP, H, DH]), ALU.mult).then_inc(scaled, 1)
                dve.wait_ge(turned3, 3 * t + 1)
                dve.tensor_copy(vpad[par][:, :, LAGS - 1:], pv[:].rearrange("p (b c) -> p b c", b=2)).then_inc(moved, 1)
                dve.wait_ge(turned3, 3 * t + 2)
                dve.tensor_copy(kq[:, 0, :], pk[:]).then_inc(moved, 1)
                dve.wait_ge(scaled, 2 * t + 2)
                b3 = bc(beta[:].rearrange("p (a b) -> p a b", a=TPP).unsqueeze(3), [P, TPP, H, DH])
                heads = lambda ap: ap.rearrange("p a (b c) -> p a b c", c=DH)
                dve.tensor_tensor(kb[:].rearrange("p (a b c) -> p a b c", a=TPP, c=DH),
                                  heads(qk[:, :, D:2 * D]), b3, ALU.mult).then_inc(factors, 1)
                dve.tensor_tensor(vb[:].rearrange("p (a b c) -> p a b c", a=TPP, c=DH),
                                  heads(qkv[:, :, 2 * D:3 * D]), b3, ALU.mult).then_inc(factors, 1)
                if ahead:
                    normalise(link, r + par, 1 - par)
                dve.wait_ge(grammed, t + 1)
                gram = lambda i: pa[:, :, 0:TPP * 2 * CHUNK].rearrange(
                    "p h (a g c) -> p h a g c", a=TPP, g=2)[:, :, :, i, :]
                mask = lambda c: bc(k.const[:, c:c + CHUNK].unsqueeze(1).unsqueeze(1), [P, H, TPP, CHUNK])
                to = lambda ap: ap.rearrange("p (a h) c -> p h a c", h=H)
                dve.tensor_tensor(to(low[:]), gram(0), mask(C_NEG), ALU.mult).then_inc(masked, 1)
                link(dve.tensor_tensor(to(loc[:]), gram(1), mask(C_INC), ALU.mult))
                dve.sem_inc(factors, 1)
                dve.sem_inc(unmasked, 1)

            for par in range(2):
                index(par, par).then_inc(indexed, 1)
            for part in (xhi, xlo):
                dve.memset(part[:, :, 0:PAD].bitcast(F32), 0.0).then_inc(padded, 1)
            for par in range(2):
                dve.memset(vpad[par][:, :, 0:LAGS - 1], 0.0).then_inc(padded, 1)
            steps = Steps(dve, chain)
            normalise(steps.done, 0, 0)
            for par in range(2):
                pair(steps.done, 0, par)
            pair(steps.done, 1, 0)
            pair(steps.done, 1, 1, "first")
            FIRST, LINKS = 62, 78
            assert steps.n == FIRST, steps.n
            with dve.Fori(2, NG - 1) as r:
                steps = Steps(dve, chain, FIRST + (r - 2) * LINKS)
                pair(steps.done, r, 0, "rest")
                pair(steps.done, r, 1, "first")
                assert steps.n == LINKS, steps.n
            steps = Steps(dve, chain, FIRST + (NG - 3) * LINKS)
            pair(steps.done, NG - 1, 0, "rest")
            pair(steps.done, NG - 1, 1, "first", ahead=False)
            invert_rest(steps.done)

        @block.scalar
        def _(act):
            def keep_ms(t):
                act.wait_ge(convolved, t + 1)
                act.activation(k.ms[:, bass.ds(t * TPP, TPP // 2), :].rearrange("p a b -> p (a b)"), pm[:, 0:SEQ],
                               ACT.Copy).then_inc(kept, 1)

            def root(t):
                act.wait_ge(varied, t + 1)
                act.activation(std[:], mv[:, :, 1], ACT.Sqrt, bias=k.eps[:, 0:1]).then_inc(rooted, 1)

            def pair(t):
                act.wait_ge(turned, t + 1)
                act.wait_ge(xsaved, 32 * (t + 1))
                rows = px[:].rearrange("p (b c) -> p b c", b=2)
                act.activation(xhi[:, :, PAD:], rows, ACT.Copy).then_inc(evac, 1)
                act.activation(xnT[:], rows, ACT.Copy).then_inc(evac, 1)
                for j in range(TPP):
                    act.wait_ge(projected, t * TPP + j + 1)
                    act.activation(qkv[:, j, :], pa[:, j, 0:3 * D], ACT.Silu)
                    act.activation(tanhb[:, j * H:j * H + H], pa[:, j, 3 * D:3 * D + H], ACT.Tanh,
                                   scale=0.5).then_inc(silued, 1)
                act.wait_ge(silued, (t + 1) * TPP)
                act.activation(sq[:], qkv[:, :, 0:2 * D], ACT.Square).then_inc(squared, 1)
                act.wait_ge(summed, t + 1)
                act.activation(rn[:], ss[:], ACT.Sqrt, bias=k.eps[:, 1:2]).then_inc(lengths, 1)
                act.wait_ge(turned3, 3 * t + 3)
                act.activation(kq[:, 1, :], pq[:], ACT.Copy).then_inc(moved, 1)

            act.wait_ge(padded, 4)
            act.sem_inc(kept, 1)
            root(0)
            pair(0)
            root(1)
            with act.Fori(1, NPAIR - 1) as t:
                pair(t)
                root(t + 1)
                keep_ms(t - 1)
            pair(NPAIR - 1)
            for t in (NPAIR - 2, NPAIR - 1):
                keep_ms(t)

        @block.tensor
        def _(pe):
            ident = k.const[:, C_ID:C_ID + P]

            def convolve(t, par, part):
                if part == 0:
                    pe.wait_ge(kept, t + 1)
                for i in range(MS_AT[part], MS_AT[part + 1]):
                    j, lag = i // LAGS, i % LAGS
                    at = LAGS - 1 - lag + j * P
                    mm = pe.matmul(pm[:, j * P:j * P + P], vpad[par][:, 0, at:at + P], k.lag[:, lag, :],
                                   start=(lag == 0), stop=(lag == LAGS - 1))
                if part == len(MS_AT) - 2:
                    mm.then_inc(convolved, 1)

            def pair(t, par, before):
                fill = (lambda part: convolve(t - 1, 1 - par, part)) if before else (lambda part: None)
                fill(0)
                pe.wait_ge(normed, t + 1)
                for j in range(TPP):
                    mm = pe.transpose(px[:, j * P:j * P + P], xn[:, j * D:j * D + D], ident)
                mm.then_inc(turned, 1)
                fill(1)
                pe.wait_ge(remained, t + 1)
                pe.wait_ge(unmasked, t + 1)
                for j in range(TPP):
                    at = (j % 2) * P
                    for tap in range(TAPS):
                        cols = slice(at + tap, at + tap + P)
                        for i, (x, w) in enumerate(((xhi, k.tap_hi), (xhi, k.tap_lo), (xlo, k.tap_hi))):
                            mm = pe.matmul(pa[:, j, 0:QKVB], x[:, j // 2, cols], w[:, tap, :],
                                           start=(tap == 0 and i == 0), stop=(tap == TAPS - 1 and i == 2))
                    mm.then_inc(projected, 1)
                fill(2)
                pe.wait_ge(silued, (t + 1) * TPP)
                for j in range(TPP):
                    mm = pe.transpose(pv[:, j * P:j * P + P], qkv[:, j, 2 * D:3 * D], ident)
                mm.then_inc(turned3, 1)
                fill(3)
                for half, bank in ((1, pk), (0, pq)):
                    pe.wait_ge(scaled, 2 * t + 2 - half)
                    for j in range(TPP):
                        mm = pe.transpose(bank[:, j * P:j * P + P], qk[:, j, half * D:half * D + D], ident)
                    mm.then_inc(turned3, 1)
                fill(4)
                wait_apart(pe, moved, 3 * (t + 1), beat)
                for j in range(TPP):
                    for n in range(QC):
                        at = j * P + n * CHUNK
                        for h in range(H):
                            rows = slice(h * DH, h * DH + DH)
                            mm = pe.matmul(pa[n * CHUNK:n * CHUNK + CHUNK, h, j * 64:j * 64 + 64],
                                           kq[rows, 0, at:at + CHUNK], kq[rows, :, at:at + CHUNK],
                                           start=True, stop=True)
                mm.then_inc(grammed, 1)

            pe.sem_inc(unmasked, 1)
            pair(0, 0, False)
            pair(1, 1, True)
            with pe.Fori(1, NG) as r:
                pair(r * 2, 0, True)
                pair(r * 2 + 1, 1, True)
            for part in range(len(MS_AT) - 1):
                convolve(NPAIR - 1, 1, part)

        @block.sync
        def _(sp):
            def save(t, field, src, done=saved):
                dst = io.pair[bass.ds(t * P, P), field * PT:field * PT + PT]
                if len(src.shape) == 3:
                    dst = dst.rearrange("p (a b) -> p a b", a=src.shape[1])
                sp.dma_start(dst, src).then_inc(done, 16)

            def pair(t, par, between=None):
                wait_apart(sp, evac, 2 * t + 2, beat)
                save(t, 6, xnT[:], xsaved)
                wait_apart(sp, silued, (t + 1) * TPP, beat)
                save(t, 2, qkv[:, :, 2 * D:3 * D], xsaved)
                wait_apart(sp, scaled, 2 * (t + 1), beat)
                save(t, 1, qk[:, :, D:2 * D])
                wait_apart(sp, moved, 3 * (t + 1), beat)
                save(t, 0, kq[:, 1, :])
                sp.dma_start(io.pair[bass.ds(t * P, P), 7 * PT:7 * PT + SEQ],
                             vpad[par][:, 1, LAGS - 1:]).then_inc(saved, 16)
                wait_apart(sp, factors, 3 * t + 2, beat)
                save(t, 3, kb[:])
                save(t, 4, vb[:])
                if between:
                    between()
                wait_apart(sp, factors, 3 * t + 3, beat)
                save(t, 5, loc[:].rearrange("p a b -> p (a b)"))
                wait_apart(sp, weighted, t + 1, beat)
                for n in range(QC):
                    dst = io.low[bass.ds((t * QC + n) * G, G), :].rearrange("g (c e) -> c g e", e=CHUNK)
                    sp.dma_start(dst, low[n * CHUNK:n * CHUNK + CHUNK, :, :]).then_inc(saved, 16)
                wait_apart(sp, saved, (t + 1) * 16 * NSAVE, beat)
                sp.sem_inc(room, 1)

            def reload(r):
                sp.dma_start(nmat[:].rearrange("p a b -> p (a b)"), io.low[bass.ds(r * P, P), :]).then_inc(ngot, 16)

            def store(r):
                wait_apart(sp, inverted, r + 1, beat)
                sp.dma_start(io.inv[bass.ds(r * P, P), :], inv[:].rearrange("p a b -> p (a b)")).then_inc(istored, 16)

            sp.sem_inc(room, 1)
            sp.sem_inc(istored, 16)
            sp.sem_inc(xsaved, 32)
            for par in range(2):
                pair(par, par)
            pair(2, 0, lambda: reload(0))
            pair(3, 1)
            def exchange(r):
                store(r - 2)
                reload(r - 1)

            with sp.Fori(2, NG - 1) as r:
                pair(r * 2, 0, lambda: exchange(r))
                pair(r * 2 + 1, 1)
            pair(NPAIR - 2, 0, lambda: exchange(NG - 1))
            sp.wait_ge(istored, 16 * (NG - 1))
            inputs.load_solve(sp, io, 0, istored)
            inputs.load_scan(sp, io, 0, istored)
            pair(NPAIR - 1, 1)
            store(NG - 2)
            sp.wait_ge(istored, 16 * (NG + inputs.SOLVE + inputs.SCAN))


class Fill:

    def __init__(self, solve, scan, start, logits, read, update, last):
        self.solve, self.scan, self.start, self.logits = solve, scan, start, logits
        self.read, self.update, self.last = read, update, last


def attend(nc, io, keep, inputs):
    k = keep
    G = TPP * H
    with ExitStack() as ctx:
        m = Memory(nc, ctx)
        sem, sb = m.sem, m.sb
        nmat, tinv = sb("a_nmat", [P, CHUNK, CHUNK]), sb("a_tinv", [P, CHUNK, CHUNK])
        prod = sb("a_prod", [P, CHUNK * CHUNK])
        qT, kn, kb, vb, loc, inv, vpad = (inputs.qT, inputs.kn, inputs.kb, inputs.vb, inputs.loc, inputs.inv,
                                          inputs.vpad)
        v, xnT = sb("a_v", [P, TPP, D]), sb("a_xnT", [P, PT])
        u, wT = sb("u", [P, TPP, D]), sb("wT", [P, PT])
        state = [[sb(f"state{b}{i}", [P, D]) for i in range(3)] for b in range(2)]
        delta = sb("delta", [P, TPP, D])
        mean = sb("mean", [P, TPP, NOUT])
        meanT = sb("meanT", [NOUT, PT])
        hdn = sb("hdn", [P, 2, PT])
        lg, top = sb("lg", [P, G, 3]), sb("ltop", [P, G])
        mix, part, direct = (sb(n, [P, TPP, D]) for n in ("mix", "part", "direct"))
        sq, ss, rs = sb("osq", [P, TPP, D]), sb("oss", [P, G]), sb("ors", [P, G])
        oT = sb("oT", [P, PT])
        pm = m.ps("a_pm", [P, 512])
        pw = m.ps("a_pw", [P, 4, 512])
        po = m.ps("a_po", [P, 512])
        pf, pg = m.ps("a_pf", [P, 512]), m.ps("a_pg", [P, 512])
        pread, pstate = [pw[:, i, :] for i in range(2)], [pw[:, 2 + i, :] for i in range(2)]
        chain, rowchain, beat = sem("achain"), sem("rowchain"), sem("abeat")
        solvegot, scangot, gategot = sem("solvegot"), sem("scangot"), sem("gategot")
        solved, taken = sem("solved"), sem("taken")
        ngot, istored = sem("angot"), sem("aistored")
        weighed, shared = sem("weighed"), sem("shared")
        padded, convolved = sem("apadded"), sem("aconvolved")
        reads, subbed, updated, stated = ([sem(f"{n}{i}") for i in range(2)]
                                          for n in ("reads", "subbed", "updated", "stated"))
        out, outed = sem("out"), sem("outed")
        meaned, meanturned, meankept = sem("meaned"), sem("meanturned"), sem("meankept")
        hidden, gelued, gated, lowered, powered = (sem("hidden"), sem("gelued"), sem("gated"), sem("lowered"),
                                                   sem("lpowered"))
        mixed, squared, summed, rooted = sem("omixed"), sem("osquared"), sem("osummed"), sem("orooted")
        scaled, oturned, okept, done, added = sem("oscaled"), sem("oturned"), sem("okept"), sem("done"), sem("added")
        block = ctx.enter_context(nc.Block())
        SOLVELOADS, SCANLOADS, GATELOADS = inputs.SOLVE, inputs.SCAN, 2
        LINKS = 9
        heads = lambda ap: ap.rearrange("p a (b c) -> p (a b) c", c=DH)
        weight = lambda i: bc(lg[:, :, i:i + 1], [P, G, DH])
        ms = lambda q: k.ms[:, bass.ds(q * TPP, TPP), :]
        LAST = NPAIR // 2 - 1
        FILL = Fill(solve=(15, 4), scan=3, start=3, logits=2, read=2, update=2, last=1)

        @block.sync
        def _(sp):
            def load_gate(t):
                wait_apart(sp, mixed, t + 1, beat)
                inputs.field(sp, io, t, v[:].rearrange("p a b -> p (a b)"), 2, gategot)
                inputs.field(sp, io, t, xnT[:], 6, gategot)

            sp.sem_inc(mixed, 1)
            sp.dma_start(nmat[:].rearrange("p a b -> p (a b)"), io.low[LAST * P:LAST * P + P, :]).then_inc(ngot, 16)
            sp.sem_inc(solvegot, 16 * SOLVELOADS)
            sp.sem_inc(scangot, 16 * SCANLOADS)
            for first, last in ((1, 2 * LAST), (2 * LAST, NPAIR)):
                with sp.Fori(first, last) as t:
                    wait_apart(sp, solved, t, beat)
                    inputs.load_solve(sp, io, t, solvegot)
                    load_gate(t - 1)
                    wait_apart(sp, out, t, beat)
                    wait_apart(sp, convolved, t, beat)
                    inputs.load_scan(sp, io, t, scangot)
                if first == 1:
                    sp.wait_ge(istored, 16)
            load_gate(NPAIR - 1)

        @block.gpsimd
        def _(pool):
            def weigh(q):
                pool.wait_ge(weighed, q + 1)
                pool.tensor_tensor(heads(mix[:]), heads(ms(q)), weight(0), ALU.mult).then_inc(shared, 1)
                pool.tensor_tensor(heads(direct[:]), heads(v[:]), weight(2), ALU.mult).then_inc(shared, 1)

            pool.wait_ge(ngot, 16)
            steps = Steps(pool, rowchain)
            identities(pool, steps.done, tinv)
            for first, last in ((0, 16), (16, CHUNK - 1)):
                substitute(pool, steps.done, nmat, tinv, prod, first, last)
                weigh(first // 16)
            pool.dma_start(io.inv[LAST * P:LAST * P + P, :], tinv[:].rearrange("p a b -> p (a b)")).then_inc(istored, 16)
            with pool.Fori(2, NPAIR) as q:
                weigh(q)

        @block.tensor
        def _(pe):
            ident = k.const[:, C_ID:C_ID + P]

            def solve(j):
                for n in range(QC):
                    rows = slice(n * CHUNK, n * CHUNK + CHUNK)
                    for h in range(H):
                        g, at = j * H + h, j * D + h * DH
                        pe.matmul(po[rows, at:at + DH], inv[rows, g, :], vb[rows, at:at + DH], start=True, stop=True)
                        mm = pe.matmul(pw[h * DH:h * DH + DH, n, j * CHUNK:j * CHUNK + CHUNK],
                                       kb[rows, at:at + DH], inv[rows, g, :], start=True, stop=True)
                return mm

            def outputs(n, b):
                j, rows = 2 * b + n // QC, slice(n % QC * CHUNK, n % QC * CHUNK + CHUNK)
                if n:
                    at = j * P + n % QC * CHUNK
                    pe.matmul(po[rows, j * D:j * D + D], qT[:, at:at + CHUNK], state[b][n % 3][:],
                              start=True, stop=False, skip_group_check=True)
                for h in range(H):
                    col = j * D + h * DH
                    mm = pe.matmul(po[rows, col:col + DH], loc[rows, j * H + h, :],
                                   u[rows, j, h * DH:h * DH + DH], start=(n == 0), stop=True,
                                   skip_group_check=True)
                return mm

            def convolve(first, count):
                for i in range(first, min(first + count, MS)):
                    j, lag = i // LAGS, i % LAGS
                    at = LAGS - 1 - lag + j * P
                    mm = pe.matmul(pm[:, j * P:j * P + P], vpad[:, at:at + P], k.lag[:, lag, :],
                                   start=(lag == 0), stop=(lag == LAGS - 1))
                    if i == MS - 1:
                        mm.then_inc(convolved, 1)
                return min(first + count, MS)

            def step(t, n, at):
                j0, rows = n // QC, slice(n % QC * CHUNK, n % QC * CHUNK + CHUNK)
                for b in range(2):
                    j = 2 * b + j0
                    col = j * P + n % QC * CHUNK
                    if n:
                        pe.wait_ge(stated[b], t * (NCH - 1) + n)
                        pe.matmul(pread[b][rows, 0:D], wT[:, col:col + CHUNK], state[b][n % 3][:],
                                  start=True, stop=True).then_inc(reads[b], 1)
                if n:
                    outputs(n - 1, 0)
                    at = convolve(at, FILL.read)
                for b in range(2):
                    j = 2 * b + j0
                    if n:
                        wait_apart(pe, subbed[b], t * (NCH - 1) + n, beat)
                    if n < NCH - 1:
                        pe.matmul(pstate[b][:, 0:D], kn[rows, j * D:j * D + D], u[rows, j, :],
                                  start=(n == 0), stop=True, skip_group_check=True).then_inc(updated[b], 1)
                if n:
                    outputs(n - 1, 1)
                at = convolve(at, FILL.start if n == 0 else FILL.update if n < NCH - 1 else FILL.last)
                if n == NCH - 1:
                    outputs(n, 0)
                    outputs(n, 1).then_inc(out, 1)
                return at

            def turn_means(q):
                pe.wait_ge(meaned, q + 1)
                for j in range(TPP):
                    mm = pe.transpose(pf[0:NOUT, j * P:j * P + P], mean[:, j, :], ident)
                mm.then_inc(meanturned, 1)

            def hide(q):
                pe.wait_ge(meankept, q + 1)
                pe.wait_ge(gategot, (q + 1) * 16 * GATELOADS)
                for f, bank in enumerate((pf, pg)):
                    if f:
                        pe.wait_ge(added, q + 1)
                    pe.matmul(bank[:], k.w1[:, f * P:f * P + P], xnT[:], start=True, stop=False)
                    pe.matmul(bank[:], k.w1s[:, f * P:f * P + P], meanT[:], start=False,
                              stop=True).then_inc(hidden, 1)

            def logits(q, at):
                pe.wait_ge(gelued, 2 * (q + 1))
                for j in range(TPP):
                    at = convolve(at, FILL.logits)
                    for f in range(2):
                        mm = pe.matmul(pf[:, j * NOUT:j * NOUT + NOUT], hdn[:, f, j * P:j * P + P], k.w2[:, f, :],
                                       start=(f == 0), stop=(f == 1))
                mm.then_inc(gated, 1)
                return at

            def turn_mixture(q):
                pe.wait_ge(scaled, q + 1)
                for j in range(TPP):
                    mm = pe.transpose(pg[:, j * P:j * P + P], mix[:, j, :], ident)
                mm.then_inc(oturned, 1)

            def output(q):
                pe.wait_ge(okept, q + 1)
                for j in range(TPP):
                    mm = pe.matmul(pg[:, j * P:j * P + P], oT[:, j * P:j * P + P], k.wout[:], start=True, stop=True)
                mm.then_inc(done, 1)

            def stage(t, gate, finish):
                pe.wait_ge(solvegot, (t + 1) * 16 * SOLVELOADS)
                wait_apart(pe, outed, 2 * t + 1, beat)
                solve(0)
                if finish:
                    output(t - 2)
                solve(1)
                if gate:
                    turn_means(t - 1)
                solve(2)
                wait_apart(pe, outed, 2 * t + 2, beat)
                pe.wait_ge(scangot, (t + 1) * 16 * SCANLOADS)
                at = convolve(0, FILL.solve[0])
                solve(3).then_inc(solved, 1)
                at = convolve(at, FILL.solve[1])
                if gate:
                    hide(t - 1)
                at = convolve(at, FILL.scan)
                pe.wait_ge(taken, 2 * (t + 1))
                at = step(t, 1, step(t, 0, at))
                if gate:
                    at = logits(t - 1, at)
                for n in range(2, NCH):
                    at = step(t, n, at)
                if gate:
                    turn_mixture(t - 1)
                convolve(at, MS)

            pe.sem_inc(added, 1)
            pe.sem_inc(outed, 2)
            pe.wait_ge(padded, 1)
            stage(0, False, False)
            stage(1, True, False)
            with pe.Fori(2, NPAIR) as t:
                stage(t, True, True)
            output(NPAIR - 2)
            turn_means(NPAIR - 1)
            hide(NPAIR - 1)
            logits(NPAIR - 1, MS)
            turn_mixture(NPAIR - 1)
            output(NPAIR - 1)

        @block.vector
        def _(dve):

            def means(q):
                dve.wait_ge(outed, 2 * q + 4)
                dve.wait_ge(gategot, (q + 1) * 16 * GATELOADS)
                for i, src in enumerate((ms(q), delta[:], v[:])):
                    last = dve.tensor_reduce(mean[:, :, i * H:i * H + H],
                                             src.rearrange("p a (b c) -> p a b c", c=DH), AX.X, ALU.add,
                                             apply_absolute_value=True)
                last.then_inc(meaned, 1)

            def add_output(q):
                dve.wait_ge(done, q + 1)
                x = k.x[:, bass.ds(q * TPP, TPP), :].rearrange("p a b -> p (a b)")
                dve.tensor_tensor(x, x, pg[:], ALU.add).then_inc(added, 1)

            def lower(q, link):
                dve.wait_ge(gated, q + 1)
                link(dve.tensor_tensor(lg[:].rearrange("p (a h) b -> p a (h b)", a=TPP),
                                       pf[:, 0:TPP * NOUT].rearrange("p (a b) -> p a b", a=TPP),
                                       bc(k.b2[:].unsqueeze(1), [P, TPP, NOUT]), ALU.add))
                link(dve.tensor_reduce(top[:], lg[:], AX.X, ALU.max))
                dve.tensor_tensor(lg[:], lg[:], bc(top[:].unsqueeze(2), [P, G, 3]), ALU.subtract).then_inc(lowered, 1)

            def weights(q, link):
                dve.wait_ge(powered, q + 1)
                link(dve.tensor_reduce(top[:], lg[:], AX.X, ALU.add))
                link(dve.reciprocal(top[:], top[:]))
                link(dve.tensor_tensor(lg[:], lg[:], bc(top[:].unsqueeze(2), [P, G, 3]), ALU.mult))
                dve.sem_inc(weighed, 1)

            def mix_first(q, link):
                link(dve.tensor_tensor(heads(part[:]), heads(delta[:]), weight(1), ALU.mult))

            def mix_second(q, link):
                dve.wait_ge(shared, 2 * q + 1)
                link(dve.tensor_tensor(mix[:], mix[:], part[:], ALU.add))

            def mix_third(q, link):
                dve.wait_ge(shared, 2 * q + 2)
                link(dve.tensor_tensor(mix[:], mix[:], direct[:], ALU.add))
                dve.sem_inc(mixed, 1)

            def squares(q, link):
                dve.wait_ge(squared, q + 1)
                dve.tensor_reduce(ss[:], heads(sq[:]), AX.X, ALU.add).then_inc(summed, 1)

            def scale(q, link):
                dve.wait_ge(rooted, q + 1)
                link(dve.reciprocal(rs[:], rs[:]))
                dve.tensor_tensor(heads(mix[:]), heads(mix[:]), bc(rs[:].unsqueeze(2), [P, G, DH]),
                                  ALU.mult).then_inc(scaled, 1)

            gate_parts = ((1, lower), (2, weights), (3, mix_first), (4, mix_second), (5, mix_third), (6, squares),
                          (7, scale))

            def step(t, n):
                j0, rows = n // QC, slice(n % QC * CHUNK, n % QC * CHUNK + CHUNK)
                for b in range(2):
                    if n:
                        dve.wait_ge(reads[b], t * (NCH - 1) + n)
                        dve.tensor_tensor(u[rows, 2 * b + j0, :], u[rows, 2 * b + j0, :], pread[b][rows, 0:D],
                                          ALU.subtract).then_inc(subbed[b], 1)
                for b in range(2):
                    if n < NCH - 1:
                        dve.wait_ge(updated[b], t * (NCH - 1) + n + 1)
                        dve.tensor_tensor(state[b][(n + 1) % 3][:], pstate[b][:, 0:D], k.const[:, C_HEAD:C_HEAD + P],
                                          ALU.mult).then_inc(stated[b], 1)

            def stage(t, gate, finish):
                if gate:
                    means(t - 1)
                if finish:
                    add_output(t - 2)
                dve.wait_ge(solved, t + 1)
                dve.tensor_copy(wT[:].rearrange("p (a n c) -> p n a c", a=TPP, n=QC),
                                pw[:, :, 0:TPP * CHUNK].rearrange("p n (a c) -> p n a c", a=TPP)).then_inc(taken, 1)
                dve.wait_ge(taken, 2 * (t + 1))
                steps = Steps(dve, chain, (t - 1) * LINKS)
                for n in range(NCH):
                    step(t, n)
                    for after, part_of in gate_parts:
                        if gate and after == n:
                            part_of(t - 1, steps.done)
                assert steps.n == (LINKS if gate else 0), steps.n

            dve.memset(vpad[:, 0:LAGS - 1], 0.0).then_inc(padded, 1)
            stage(0, False, False)
            stage(1, True, False)
            with dve.Fori(2, NPAIR) as t:
                stage(t, True, True)
            means(NPAIR - 1)
            add_output(NPAIR - 2)
            steps = Steps(dve, chain, (NPAIR - 1) * LINKS)
            for _, part_of in gate_parts:
                part_of(NPAIR - 1, steps.done)
            add_output(NPAIR - 1)

        @block.scalar
        def _(act):
            def keep_means(q):
                act.wait_ge(meanturned, q + 1)
                act.activation(meanT[:], pf[0:NOUT, :], ACT.Copy, scale=1.0 / DH).then_inc(meankept, 1)

            def gate(q):
                for f, bank in enumerate((pf, pg)):
                    act.wait_ge(hidden, q * 2 + f + 1)
                    act.activation(hdn[:, f, :], bank[:], ACT.Gelu, bias=k.b1[:, f:f + 1]).then_inc(gelued, 1)
                act.wait_ge(lowered, q + 1)
                act.activation(lg[:], lg[:], ACT.Exp).then_inc(powered, 1)
                act.wait_ge(mixed, q + 2)
                act.activation(sq[:], mix[:], ACT.Square).then_inc(squared, 1)
                act.wait_ge(summed, q + 1)
                act.activation(rs[:], ss[:], ACT.Sqrt, bias=k.eps[:, 2:3], scale=1.0 / DH).then_inc(rooted, 1)

            def keep_mixture(q):
                act.wait_ge(oturned, q + 1)
                act.activation(oT[:], pg[:], ACT.Copy).then_inc(okept, 1)

            def stage(t, with_gate):
                if with_gate:
                    keep_means(t - 1)
                act.wait_ge(solved, t + 1)
                act.activation(u[:].rearrange("p a b -> p (a b)"), po[:], ACT.Copy).then_inc(taken, 1)
                if with_gate:
                    gate(t - 1)
                act.wait_ge(out, t + 1)
                act.activation(delta[:].rearrange("p a b -> p (a b)"), po[:], ACT.Copy).then_inc(outed, 1)
                if with_gate:
                    keep_mixture(t - 1)
                act.wait_ge(convolved, t + 1)
                act.activation(k.ms[:, bass.ds(t * TPP + 2, 2), :].rearrange("p a b -> p (a b)"), pm[:, 0:SEQ],
                               ACT.Copy).then_inc(outed, 1)

            stage(0, False)
            with act.Fori(1, NPAIR) as t:
                stage(t, True)
            keep_means(NPAIR - 1)
            gate(NPAIR - 1)
            keep_mixture(NPAIR - 1)


def collect(nc, io, keep):
    k = keep
    with ExitStack() as ctx:
        m = Memory(nc, ctx)
        second = m.sb("second", [P, NT, D])
        GROUPS = ((0, NT - GRP), (NT - GRP, NT))
        gathered = [m.sem(f"cgathered{i}") for i in range(2)]
        added, stored = m.sem("cadded"), m.sem("cstored")
        block = ctx.enter_context(nc.Block())

        @block.gpsimd
        def _(pool):
            for (first, last), got in zip(GROUPS, gathered):
                for j in range(first, last):
                    gather(pool, io, 1, k.slot[:, j, 1:2], second[:, j, :], got)

        @block.vector
        def _(dve):
            for c in range(TOPK):
                for (first, last), got in zip(GROUPS, gathered):
                    if c:
                        dve.wait_ge(got, (last - first) * 16)
                        dve.wait_ge(added, last)
                    for j in range(first, last):
                        row = second[:, j, :] if c else k.first[:, j, :]
                        dve.scalar_tensor_tensor(k.x[:, j, :], row, k.share[:, j, c:c + 1], k.x[:, j, :],
                                                 ALU.mult, ALU.add).then_inc(added, 1)

        @block.sync
        def _(sp):
            dst = io.out.rearrange("(n p) d -> p n d", p=P)
            for t in range(NPAIR):
                sp.wait_ge(added, NT + (t + 1) * TPP)
                sp.dma_start(dst[:, t * TPP:(t + 1) * TPP, :], k.x[:, t * TPP:(t + 1) * TPP, :]).then_inc(stored, 16)
            sp.wait_ge(stored, 16 * NPAIR)


class Kept:

    def __init__(self, m):
        self.x = m.sb("x", [P, NT, D])
        self.const = m.sb("const", [P, C_END])
        self.gate = m.sb("gate", [P, E])
        self.tap_hi, self.tap_lo = (m.sb(f"tap_{n}", [P, TAPS, QKVB], F32R) for n in ("hi", "lo"))
        self.w1, self.w1s = m.sb("w1", [P, 2 * D]), m.sb("w1s", [NOUT, 2 * D])
        self.b1 = m.sb("b1", [P, 2])
        self.w2, self.b2 = m.sb("w2", [P, 2, NOUT]), m.sb("b2", [P, NOUT])
        self.wout = m.sb("wout", [P, D])
        self.lag = m.sb("lag", [P, LAGS, D])
        self.eps = m.sb("eps", [P, 3])
        self.count = m.sb("count", [P, TOPK * E])
        self.slot = m.sb("slot", [P, YB, TOPK], U32)
        self.share = m.sb("share", [P, NT, TOPK])
        self.upper, self.ones = m.sb("upper", [P, P], BF16), m.sb("ones", [P, P], BF16)
        self.xn = m.sb("xn", [P, NT, D])
        self.first = m.sb("first", [P, NT, D])
        self.w = [m.sb(f"expert{i}", [P, 3, F]) for i in range(2)]
        self.ms = m.sb("ms", [P, NT, D])


class Dram:

    def __init__(self, nc, arrays):
        def given(n):
            v = arrays[n]
            return nc.dram_tensor(n + "_in", v.shape, mybir.dt.from_np(v.dtype), kind="ExternalInput").ap()

        def scratch(n, *shape):
            return nc.dram_tensor(n, shape, F32, kind="Internal").ap()

        self.x, self.const, self.gate, self.wexp = given("x"), given("const"), given("gate"), given("wexp")
        self.wqkv, self.taps, self.wb = given("wqkv"), given("taps"), given("wb")
        self.ms3, self.ms15, self.ms31 = given("ms3"), given("ms15"), given("ms31")
        self.mixT, self.chan = given("mixT"), given("chan")
        self.w1, self.b1, self.w2, self.b2 = given("w1"), given("b1"), given("w2"), given("b2")
        self.onorm, self.wo = given("onorm"), given("wo")
        self.out = nc.dram_tensor("out", (BATCH * SEQ, D), F32, kind="ExternalOutput").ap()
        self.queue = [scratch(f"queue{c}", SLOTS, D) for c in range(TOPK)]
        self.rows = [scratch(f"rows{c}", SLOTS + 1, D) for c in range(TOPK)]
        self.pair = scratch("pair", NPAIR * P, 7 * PT + SEQ)
        self.low = scratch("low_dram", BATCH * H * NCH, CHUNK * CHUNK)
        self.inv = scratch("inv_dram", BATCH * H * NCH, CHUNK * CHUNK)


def program(nc, io):
    with ExitStack() as ctx:
        keep = Kept(Memory(nc, ctx))
        with ExitStack() as first:
            raw = Raw(Memory(nc, first))
            route(nc, io, keep, "r1", raw)
            experts(nc, io, keep, "e1", raw)
        with ExitStack() as second:
            inputs = Inputs(Memory(nc, second))
            project(nc, io, keep, inputs)
            attend(nc, io, keep, inputs)
        route(nc, io, keep, "r2")
        experts(nc, io, keep, "e2")
        collect(nc, io, keep)


def layouts(inputs):
    a = {n: np.asarray(v) for n, v in inputs.items()}
    at = lambda n: a["L0_attn_" + n]
    ff = lambda n: a["L0_ffn_" + n]
    wo = ff("wo").transpose(0, 2, 1).reshape(E, FT, P, D).transpose(0, 2, 1, 3).reshape(E, P, F)
    out = {
        "x": at("hidden_states").reshape(BATCH * SEQ, D),
        "const": shape_constants(),
        "gate": ff("gate_w").T,
        "wexp": np.concatenate([ff("wi_gate").transpose(0, 2, 1), ff("wi_up").transpose(0, 2, 1), wo],
                               axis=2).reshape(E * P, 3 * F),
        "wqkv": np.stack([at("Wq"), at("Wk"), at("Wv")], axis=1),
        "taps": np.stack([at("conv_q_w").T, at("conv_k_w").T, at("conv_v_w").T], axis=1).reshape(-1),
        "wb": at("Wb"), "ms3": at("ms_w3"), "ms15": at("ms_w15"), "ms31": at("ms_w31"),
        "mixT": at("kernel_mix_w").T, "chan": at("channel_mixer_w"),
        "w1": at("fusion_w1"), "b1": at("fusion_b1").reshape(2, P).T, "w2": at("fusion_w2"), "b2": at("fusion_b2"),
        "onorm": at("o_norm_w"), "wo": at("Wo"),
    }
    return {n: np.ascontiguousarray(v) for n, v in out.items()}


def build(nc, arrays):
    program(nc, Dram(nc, arrays))


def kernel(**inputs):
    import concourse.bacc as bacc
    from concourse.bass_utils import run_bass_kernel_spmd

    arrays = layouts(inputs)
    nc = bacc.Bacc("TRN2", target_bir_lowering=False, num_devices=1)
    build(nc, arrays)
    r = run_bass_kernel_spmd(nc, [{n + "_in": v for n, v in arrays.items()}], core_ids=[0])
    return r.results[0]["out"].reshape(BATCH, SEQ, D)
```
